# Optimizing a Trainium2 kernel written in Bass

```python
import numpy as np
import jax
import jax.numpy as jnp

def _softmax(x, axis=-1):
    return jax.nn.softmax(x, axis=axis)

def _gelu(x):
    return jax.nn.gelu(x, approximate=True)

def _silu(x):
    return jax.nn.silu(x)

def _sigmoid(x):
    return jax.nn.sigmoid(x)

def _layernorm(x, axis=-1, eps=1e-05):
    m = jnp.mean(x, axis=axis, keepdims=True)
    v = jnp.var(x, axis=axis, keepdims=True)
    return (x - m) / jnp.sqrt(v + eps)

def _scatter_add(tgt, idx, src, axis=0):
    return tgt.at[idx].add(src)

def _segment_sum(src, seg, n):
    return jax.ops.segment_sum(src, seg, n)
kernel_name = 'mk_vit_tower_d1_tok_img1024_r4_087300'

def setup_inputs(seed: int=0):
    np.random.seed(seed)
    _w = jnp.asarray

    def _rec_inputs():
        import jax
        import jax.numpy as jnp
        _rk = jax.random.key(seed)
        x = 7.22013e-05 + 1.00017 * jax.random.normal(jax.random.fold_in(_rk, 1), (4, 64, 64, 64), jnp.float32)
        return x
    x = _rec_inputs()

    def _L0_tok_setup():
        import jax, jax.numpy as jnp
        import numpy as np
        from jax import lax
        H = 64
        V = 256
        EPS = 0.0001
        key = jax.random.key(seed)
        ks = jax.random.split(key, 6)
        x = jax.random.normal(ks[0], (8, 64, 64, H), dtype=jnp.float32)
        conv_w = jax.random.normal(ks[1], (H, 1, 3, 3), dtype=jnp.float32) * (1.0 / 3.0)
        conv_b = jax.random.normal(ks[2], (H,), dtype=jnp.float32) * 0.01
        proj_w = jax.random.normal(ks[3], (V, H), dtype=jnp.float32) * (1.0 / np.sqrt(H))
        proj_b = jax.random.normal(ks[4], (V,), dtype=jnp.float32) * 0.01
        norm_w = jnp.ones((V,), dtype=jnp.float32)
        return {'x': x, 'conv_w': conv_w, 'conv_b': conv_b, 'proj_w': proj_w, 'proj_b': proj_b, 'norm_w': norm_w}
    _L0_tok_all = _L0_tok_setup()
    _L0_tok_in = {k: v for k, v in _L0_tok_all.items() if k in ('conv_w', 'conv_b', 'proj_w', 'proj_b', 'norm_w')}
    del _L0_tok_all

    def _L0_attn_setup():
        import jax, jax.numpy as jnp
        import numpy as np
        D_MODEL = 256
        NUM_HEADS = 16
        HEAD_DIM = D_MODEL // NUM_HEADS
        key = jax.random.key(seed)
        ks = jax.random.split(key, 9)
        s = 1.0 / np.sqrt(D_MODEL)
        x = jax.random.normal(ks[0], (4, 2048, D_MODEL), dtype=jnp.float32)
        Wq = jax.random.uniform(ks[1], (D_MODEL, D_MODEL), jnp.float32, -s, s)
        bq = jax.random.uniform(ks[2], (D_MODEL,), jnp.float32, -s, s)
        Wk = jax.random.uniform(ks[3], (D_MODEL, D_MODEL), jnp.float32, -s, s)
        bk = jax.random.uniform(ks[4], (D_MODEL,), jnp.float32, -s, s)
        Wv = jax.random.uniform(ks[5], (D_MODEL, D_MODEL), jnp.float32, -s, s)
        bv = jax.random.uniform(ks[6], (D_MODEL,), jnp.float32, -s, s)
        Wo = jax.random.uniform(ks[7], (D_MODEL, D_MODEL), jnp.float32, -s, s)
        bo = jax.random.uniform(ks[8], (D_MODEL,), jnp.float32, -s, s)
        return {'x': x, 'Wq': Wq, 'bq': bq, 'Wk': Wk, 'bk': bk, 'Wv': Wv, 'bv': bv, 'Wo': Wo, 'bo': bo}
    _L0_attn_all = _L0_attn_setup()
    _L0_attn_in = {k: v for k, v in _L0_attn_all.items() if k in ('Wq', 'bq', 'Wk', 'bk', 'Wv', 'bv', 'Wo', 'bo')}
    del _L0_attn_all

    def _L0_ffn_setup():
        import jax, jax.numpy as jnp
        import numpy as np
        LN_EPS = 1e-05

        def layer_norm(x, g, b):
            mu = jnp.mean(x, axis=-1, keepdims=True)
            var = jnp.mean(jnp.square(x - mu), axis=-1, keepdims=True)
            return (x - mu) * jax.lax.rsqrt(var + LN_EPS) * g + b

        def ternary_quant(w):
            scale = 1.0 / jnp.clip(jnp.mean(jnp.abs(w)), 1e-05)
            wq = jnp.clip(jnp.round(w * scale), -1.0, 1.0) / scale
            return w + jax.lax.stop_gradient(wq - w)
        key = jax.random.key(seed)
        ks = jax.random.split(key, 3)
        dim, hidden = (256, 1024)
        B, S = (8, 256)
        x = jax.random.normal(ks[0], (B, S, dim), dtype=jnp.float32)
        w1 = jax.random.normal(ks[1], (hidden, dim), dtype=jnp.float32) * 0.02
        w2 = jax.random.normal(ks[2], (dim, hidden), dtype=jnp.float32) * 0.02
        return {'x': x, 'ln1_g': jnp.ones((dim,), jnp.float32), 'ln1_b': jnp.zeros((dim,), jnp.float32), 'w1': w1, 'b1': jnp.zeros((hidden,), jnp.float32), 'ln2_g': jnp.ones((hidden,), jnp.float32), 'ln2_b': jnp.zeros((hidden,), jnp.float32), 'w2': w2, 'b2': jnp.zeros((dim,), jnp.float32)}
    _L0_ffn_all = _L0_ffn_setup()
    _L0_ffn_in = {k: v for k, v in _L0_ffn_all.items() if k in ('ln1_g', 'ln1_b', 'w1', 'b1', 'ln2_g', 'ln2_b', 'w2', 'b2')}
    del _L0_ffn_all
    return {'x': x, 'L0_tok_conv_w': _L0_tok_in['conv_w'], 'L0_tok_conv_b': _L0_tok_in['conv_b'], 'L0_tok_proj_w': _L0_tok_in['proj_w'], 'L0_tok_proj_b': _L0_tok_in['proj_b'], 'L0_tok_norm_w': _L0_tok_in['norm_w'], 'L0_attn_Wq': _L0_attn_in['Wq'], 'L0_attn_bq': _L0_attn_in['bq'], 'L0_attn_Wk': _L0_attn_in['Wk'], 'L0_attn_bk': _L0_attn_in['bk'], 'L0_attn_Wv': _L0_attn_in['Wv'], 'L0_attn_bv': _L0_attn_in['bv'], 'L0_attn_Wo': _L0_attn_in['Wo'], 'L0_attn_bo': _L0_attn_in['bo'], 'L0_ffn_ln1_g': _L0_ffn_in['ln1_g'], 'L0_ffn_ln1_b': _L0_ffn_in['ln1_b'], 'L0_ffn_w1': _L0_ffn_in['w1'], 'L0_ffn_b1': _L0_ffn_in['b1'], 'L0_ffn_ln2_g': _L0_ffn_in['ln2_g'], 'L0_ffn_ln2_b': _L0_ffn_in['ln2_b'], 'L0_ffn_w2': _L0_ffn_in['w2'], 'L0_ffn_b2': _L0_ffn_in['b2']}

def reference(x, L0_tok_conv_w, L0_tok_conv_b, L0_tok_proj_w, L0_tok_proj_b, L0_tok_norm_w, L0_attn_Wq, L0_attn_bq, L0_attn_Wk, L0_attn_bk, L0_attn_Wv, L0_attn_bv, L0_attn_Wo, L0_attn_bo, L0_ffn_ln1_g, L0_ffn_ln1_b, L0_ffn_w1, L0_ffn_b1, L0_ffn_ln2_g, L0_ffn_ln2_b, L0_ffn_w2, L0_ffn_b2):
    import jax
    import jax.numpy as jnp

    def _L0_tok_ref(x, conv_w, conv_b, proj_w, proj_b, norm_w):
        import jax, jax.numpy as jnp
        import numpy as np
        from jax import lax
        H = 64
        V = 256
        EPS = 0.0001
        B, h, w, C = x.shape
        x_nchw = jnp.transpose(x, (0, 3, 1, 2))
        y = lax.conv_general_dilated(x_nchw, conv_w, window_strides=(1, 1), padding='SAME', feature_group_count=C, dimension_numbers=('NCHW', 'OIHW', 'NCHW'))
        y = y + conv_b[None, :, None, None]
        y = jnp.transpose(y, (0, 2, 3, 1))
        y = jnp.einsum('bhwc,vc->bhwv', y, proj_w) + proj_b
        y = y.reshape(B, h * w, V)
        y = jax.nn.gelu(y, approximate=False)
        rms = jax.lax.rsqrt(jnp.mean(y * y, axis=-1, keepdims=True) + EPS)
        return y * rms * norm_w

    def _L0_attn_ref(x, Wq, bq, Wk, bk, Wv, bv, Wo, bo):
        import jax, jax.numpy as jnp
        import numpy as np
        D_MODEL = 256
        NUM_HEADS = 16
        HEAD_DIM = D_MODEL // NUM_HEADS
        b, n, d_model = x.shape
        h, dh = (NUM_HEADS, HEAD_DIM)

        def heads(t):
            return t.reshape(b, n, h, dh).transpose(0, 2, 1, 3)
        q = heads(x @ Wq + bq)
        k = heads(x @ Wk + bk)
        v = heads(x @ Wv + bv)
        q = jax.nn.softmax(q, axis=-1)
        k = jax.nn.softmax(k, axis=-1)
        k_sum = k.sum(axis=-2, keepdims=True)
        d_inv = 1.0 / (q * k_sum).sum(axis=-1, keepdims=True)
        context = jnp.einsum('bhnd,bhne->bhde', k, v)
        y = jnp.einsum('bhnd,bhde->bhne', q, context) * d_inv + q
        y = y.transpose(0, 2, 1, 3).reshape(b, n, d_model)
        return y @ Wo + bo

    def _L0_ffn_ref(x, ln1_g, ln1_b, w1, b1, ln2_g, ln2_b, w2, b2):
        import jax, jax.numpy as jnp
        import numpy as np
        LN_EPS = 1e-05

        def layer_norm(x, g, b):
            mu = jnp.mean(x, axis=-1, keepdims=True)
            var = jnp.mean(jnp.square(x - mu), axis=-1, keepdims=True)
            return (x - mu) * jax.lax.rsqrt(var + LN_EPS) * g + b

        def ternary_quant(w):
            scale = 1.0 / jnp.clip(jnp.mean(jnp.abs(w)), 1e-05)
            wq = jnp.clip(jnp.round(w * scale), -1.0, 1.0) / scale
            return w + jax.lax.stop_gradient(wq - w)
        h = layer_norm(x, ln1_g, ln1_b)
        h = jnp.einsum('bsd,hd->bsh', h, ternary_quant(w1)) + b1
        h = jax.nn.gelu(h, approximate=False)
        h = layer_norm(h, ln2_g, ln2_b)
        out = jnp.einsum('bsh,dh->bsd', h, ternary_quant(w2)) + b2
        return out
    h = _L0_tok_ref(x, L0_tok_conv_w, L0_tok_conv_b, L0_tok_proj_w, L0_tok_proj_b, L0_tok_norm_w)
    h = h + _L0_attn_ref(_layernorm(h, axis=-1), L0_attn_Wq, L0_attn_bq, L0_attn_Wk, L0_attn_bk, L0_attn_Wv, L0_attn_bv, L0_attn_Wo, L0_attn_bo)
    h = h + _L0_ffn_ref(_layernorm(h, axis=-1), L0_ffn_ln1_g, L0_ffn_ln1_b, L0_ffn_w1, L0_ffn_b1, L0_ffn_ln2_g, L0_ffn_ln2_b, L0_ffn_w2, L0_ffn_b2)
    return h

_drawn_inputs = setup_inputs


def setup_inputs(seed=0):
    import zlib

    import numpy as np

    out = dict(_drawn_inputs(seed))
    spreads = {'L0_tok_norm_w': (1.0, 0.2),
     'L0_ffn_ln1_g': (1.0, 0.2),
     'L0_ffn_ln1_b': (0.0, 0.1),
     'L0_ffn_b1': (0.0, 0.1),
     'L0_ffn_ln2_g': (1.0, 0.2),
     'L0_ffn_ln2_b': (0.0, 0.1),
     'L0_ffn_b2': (0.0, 0.1)}
    factors = {'L0_tok_conv_b': 5.683,
     'L0_tok_proj_b': 5.528,
     'L0_attn_Wq': 2.799,
     'L0_attn_bq': 29.367,
     'L0_attn_Wk': 8.0,
     'L0_attn_bk': 200.0,
     'L0_attn_bv': 2.836}
    for name, (base, spread) in spreads.items():
        noise = np.random.default_rng([zlib.crc32(name.encode()), seed]).standard_normal(out[name].shape)
        drawn = base * np.exp(spread * noise) if base else spread * noise
        out[name] = jnp.asarray(drawn.astype(out[name].dtype))
    for name, factor in factors.items():
        out[name] = (out[name] * factor).astype(out[name].dtype)
    return out
```

```python
from contextlib import ExitStack

import concourse.bass as bass
from concourse import mybir

F32 = mybir.dt.float32
F16 = mybir.dt.float16
ALU = mybir.AluOpType
ACT = mybir.ActivationFunctionType
AX = mybir.AxisListType

P = 128
XS = 16.0
WS = 64.0
QS = XS * WS
BROW = 32.0
START = 1
RING = 9
TOK_EPS, LN_EPS = 1e-4, 1e-5


def vit_block(nc, x, conv_w, conv_b, proj_w, proj_b, norm_w, Wq, bq, Wk, bk, Wv, bv, Wo, bo,
              ln1_g, ln1_b, w1, b1, ln2_g, ln2_b, w2, b2, out):
    NB, H, W, C = x.shape
    D = Wq.shape[0]
    HID = w1.shape[0]
    NH, HD = 16, D // 16
    KH = D // P
    NC = HID // P
    T = 4
    TOK = T * P
    GI = H * W // TOK
    NG = NB * GI
    HR = H // 2
    GR = HR // GI
    PR, PW = HR + 2, W + 2
    XP = PR * PW
    HH = NH // KH
    VC = P + 1
    CC = P + HH
    JT = H * W // 2 // P
    assert C == 64 and D == 256 and HD == 16 and GI == 8 and GR * W == 2 * P and P % HD == 0

    ctx = ExitStack()
    with ctx:
        def sb(name, shape, dt=F32):
            return ctx.enter_context(nc.sbuf_tensor(name, shape, dt))

        def sem(name):
            return ctx.enter_context(nc.semaphore(name))

        h_ring = sb("h_ring", [P, RING * T * D])
        q_ring = sb("q_ring", [P, RING * T * D])
        xpad = sb("xpad", [P, NB * XP])
        w1T = [sb(f"w1T{h}", [P, HID], F16) for h in range(KH)]
        w2T = sb("w2T", [P, NC, D], F16)
        wqkv_hi = sb("wqkv_hi", [P, KH, 3 * D], F16)
        wqkv_lo = sb("wqkv_lo", [P, KH, 3 * D], F16)
        wo = sb("wo", [P, KH, D])
        proj = sb("proj", [P, 2, D])
        ones_rows = sb("ones_rows", [P, P], F16)
        qk_bias = sb("qk_bias", [P, 2 * D], F16)
        proj_bias = sb("proj_bias", [P, D], F16)
        norm_bc = sb("norm_bc", [P, D])
        bo_bc = sb("bo_bc", [P, D])
        b2_bc = sb("b2_bc", [P, D])
        g2w_bc = sb("g2w_bc", [P, D])
        ident = sb("ident", [P, P])
        mask = sb("mask", [P, P])
        ones = sb("ones", [P, P])
        cols = sb("cols", [P, 32])
        conv_k = sb("conv_k", [P, 9])
        conv_c = sb("conv_c", [P, 1])
        tern = sb("tern", [P, 2, 4])
        absum = sb("absum", [P, 2])
        gelu_scale = sb("gelu_scale", [P, 1])
        b1c = sb("b1c", [P, NC])
        carrier = sb("carrier", [P, 1])
        g1c = sb("g1c", [P, KH])
        g2c = sb("g2c", [P, NC])
        a2c = sb("a2c", [P, 1])
        mhalf = sb("mhalf", [P, T])
        kv_acc = sb("kv_acc", [P, KH, VC])
        kv = sb("kv", [P, KH, CC])
        conv = sb("conv", [P, 2 * P])
        y = sb("y", [P, T, D])
        z = sb("z", [P, T, D])
        ssq = sb("ssq", [P, T])
        stA = sb("stA", [P, T, 6])
        mvA = sb("mvA", [P, T, 2])
        smA = sb("smA", [P, 6, T])
        xT_hi = sb("xT_hi", [P, KH, TOK], F16)
        xT_lo = sb("xT_lo", [P, KH, TOK], F16)
        qk = sb("qk", [P, T, 2 * D])
        mx = sb("mx", [P, T, 2 * NH])
        sm = sb("sm", [P, T, 2 * NH])
        rs = sb("rs", [P, T, 2 * NH])
        v = sb("v", [P, T, KH, VC])
        bwork = sb("bwork", [P, 3 * T * D])
        qT, y1, h2 = (bwork[:, j * T * D:(j + 1) * T * D] for j in range(3))
        qT = qT.rearrange("p (h t) -> p h t", h=KH)
        y1 = y1.rearrange("p (t d) -> p t d", t=T)
        h2 = h2.rearrange("p (t d) -> p t d", t=T)
        yT, x2 = qT, y1
        q_now = sb("q_now", [P, T, D])
        rden = sb("rden", [P, T, KH, HH])
        stB = sb("stB", [P, T, 6])
        mvB = sb("mvB", [P, T, 2])
        smB = sb("smB", [P, 6, T])
        x2T_hi = sb("x2T_hi", [P, KH, TOK], F16)
        x2T_lo = sb("x2T_lo", [P, KH, TOK], F16)
        GB, SB, HB = 3, 2, 3
        g = sb("g", [P, GB, TOK])
        sq = sb("sq", [P, SB, TOK])
        g_hi = sb("g_hi", [P, HB, TOK], F16)
        g_lo = sb("g_lo", [P, HB, TOK], F16)
        s12 = sb("s12", [P, 2, TOK])
        res = sb("res", [P, T, D])
        smF = sb("smF", [P, 8, T])

        psA = [ctx.enter_context(nc.psum_tensor(f"psA{i}", [P, 512], F32)) for i in range(2)]
        psB = [ctx.enter_context(nc.psum_tensor(f"psB{i}", [P, 512], F32)) for i in range(2)]
        psF = [ctx.enter_context(nc.psum_tensor(f"psF{i}", [P, 512], F32)) for i in range(2)]
        psO = [ctx.enter_context(nc.psum_tensor(f"psO{i}", [P, 512], F32)) for i in range(2)]

        stage_sems = []

        def stage_sem(name):
            stage_sems.append(sem(name))
            return stage_sems[-1]

        conv_step, proj_done, gelu_done, ssq_done = stage_sem("conv_step"), stage_sem("proj_done"), stage_sem("gelu_done"), stage_sem("ssq_done")
        z_done, normA_step, ms_done, rms_done = stage_sem("z_done"), stage_sem("normA_step"), stage_sem("ms_done"), stage_sem("rms_done")
        varA_done, rstdA_done, xn_done, xT_done = stage_sem("varA_done"), stage_sem("rstdA_done"), stage_sem("xn_done"), stage_sem("xT_done")
        xhi_done, xlo_done, qkp_done, vp_done = stage_sem("xhi_done"), stage_sem("xlo_done"), stage_sem("qkp_done"), stage_sem("vp_done")
        max_done, shift_done, exp_done, v_out = stage_sem("max_done"), stage_sem("shift_done"), stage_sem("exp_done"), stage_sem("v_out")
        hsum_done, rs_done, q_done, k_done = stage_sem("hsum_done"), stage_sem("rs_done"), stage_sem("q_done"), stage_sem("k_done")
        ctx_done, acc_done, kv_ready = stage_sem("ctx_done"), stage_sem("acc_done"), stage_sem("kv_ready")
        qT_done, qT_out, qc_done, rden_done = stage_sem("qT_done"), stage_sem("qT_out"), stage_sem("qc_done"), stage_sem("rden_done")
        num_done, y_done, yT_done, yT_out = stage_sem("num_done"), stage_sem("y_done"), stage_sem("yT_done"), stage_sem("yT_out")
        wo_done, h2_done, normB_step = stage_sem("wo_done"), stage_sem("h2_done"), stage_sem("normB_step")
        varB_done, rstdB_done, x2_done = stage_sem("varB_done"), stage_sem("rstdB_done"), stage_sem("x2_done")
        x2T_done, x2hi_done, x2lo_done, res_done = stage_sem("x2T_done"), stage_sem("x2hi_done"), stage_sem("x2lo_done"), stage_sem("res_done")
        f1_done, g_done, ghi_done, glo_done = stage_sem("f1_done"), stage_sem("g_done"), stage_sem("ghi_done"), stage_sem("glo_done")
        sq_done, s1_done, sum_done, f2_done = stage_sem("sq_done"), stage_sem("s1_done"), stage_sem("sum_done"), stage_sem("f2_done")
        st_done, ssum_done, normF_step, varF_done = stage_sem("st_done"), stage_sem("ssum_done"), stage_sem("normF_step"), stage_sem("varF_done")
        rstdF_done, coef_done, u_done, fin_done = stage_sem("rstdF_done"), stage_sem("coef_done"), stage_sem("u_done"), stage_sem("fin_done")

        XB = JT * 2 * C
        xin = h_ring[:, 0:NB * XB].rearrange("p (b j h c) -> p b j h c", b=NB, j=JT, h=2)
        WN = NC * D
        w1n, w2n, t1T, tmp = (q_ring[:, j * WN:(j + 1) * WN] for j in range(4))
        t1T = t1T.rearrange("p (h n) -> p h n", h=KH)
        t2T = qk[:].rearrange("p t n -> p (t n)").rearrange("p (c n) -> p c n", c=NC)
        wn = bwork[:, 0:KH * 3 * D].rearrange("p (h n) -> p h n", h=KH)
        bc = q_ring[:, 3 * WN:3 * WN + (2 * NC + KH) * P].rearrange("p (r n) -> p r n", n=P)
        pn = y[:].rearrange("p t n -> p (t n)")[:, 0:2 * P].rearrange("p (b n) -> p b n", b=2)
        pack = z[:].rearrange("p t n -> p (t n)")[:, 0:P]
        brow = z[:].rearrange("p t n -> p (t n)")[:, P:P + 3 * D]

        x_in = [sem(f"x_in{b}") for b in range(NB)]
        w12_in, wqkv_in, small_in, rows_in = sem("w12_in"), sem("wqkv_in"), sem("small_in"), sem("rows_in")
        cleared, const_step, consts, pad_clear = sem("cleared"), sem("const_step"), sem("consts"), sem("pad_clear")
        abs_done, tot_done, ternary, prep_step = sem("abs_done"), sem("tot_done"), sem("ternary"), sem("prep_step")
        tr_done, tr_out, x_tr, x_out, halo = sem("tr_done"), sem("tr_out"), sem("x_tr"), sem("x_out"), sem("halo")
        col_done, col_out, pj_done, pj_out = sem("col_done"), sem("col_out"), sem("pj_done"), sem("pj_out")
        bc_ready, sums_done, hi_done = sem("bc_ready"), sem("sums_done"), sem("hi_done")

        GCOL, BCOL, B1COL, G2COL, B2COL, BVCOL = 0, KH, 2 * KH, 2 * KH + NC, 2 * KH + 2 * NC, 2 * KH + 3 * NC
        with nc.Block() as block:

            @block.sync
            def _(sp):
                for s in stage_sems:
                    sp.sem_inc(s, START)
                sp.dma_start(w1n.rearrange("p (c d) -> p c d", c=NC), w1.rearrange("(c p) d -> p c d", p=P)).then_inc(w12_in, 16)
                sp.dma_start(w2n.rearrange("p (c d) -> p c d", c=KH), w2.rearrange("(c p) d -> p c d", p=P)).then_inc(w12_in, 16)
                for b in range(NB):
                    for half in range(2):
                        rows = x[b, half * HR:(half + 1) * HR, :, :].rearrange("r w c -> (r w) c")
                        sp.dma_start(xin[:, b, :, half, :], rows.rearrange("(p j) c -> p j c", j=JT)).then_inc(x_in[b], 16)

            @block.scalar
            def _(act):
                act.wait_ge(cleared, 1)
                for row, src in ((GCOL, ln1_g), (BCOL, ln1_b), (B1COL, b1), (G2COL, ln2_g), (B2COL, ln2_b), (BVCOL, bv)):
                    n = src.shape[0] // P
                    act.dma_start(pack[row:row + n, :], src.rearrange("(r n) -> r n", n=P)).then_inc(rows_in, 16)
                for part in (0, 32):
                    for col, src in ((0, bq), (D, bk), (2 * D, proj_b)):
                        act.dma_start(brow[part:part + 1, col:col + D], src.rearrange("(a n) -> a n", a=1)).then_inc(rows_in, 16)
                for i, src in enumerate((Wq, Wk, Wv)):
                    act.dma_start(wn[:, :, i * D:(i + 1) * D], src.rearrange("(h p) n -> p h n", p=P)).then_inc(wqkv_in, 16)
                act.dma_start(wo[:], Wo.rearrange("(h p) n -> p h n", p=P)).then_inc(wqkv_in, 16)
                for rep in range(2):
                    act.dma_start(pn[:, :, rep * C:(rep + 1) * C], proj_w.rearrange("(b p) c -> p b c", p=P)).then_inc(small_in, 16)
                    act.dma_start(conv_k[rep * C:(rep + 1) * C, :], conv_w.rearrange("c o a b -> c (o a b)")).then_inc(small_in, 16)
                    act.dma_start(conv_c[rep * C:(rep + 1) * C, :], conv_b.rearrange("(c o) -> c o", o=1)).then_inc(small_in, 16)
                for dst, src in ((norm_bc, norm_w), (bo_bc, bo), (b2_bc, b2)):
                    act.dma_start(dst[:], 
                                  src.rearrange("(a n) -> a n", a=1).to_broadcast([P, D])).then_inc(small_in, 16)
                act.wait_ge(pad_clear, 1)
                for b in range(NB):
                    for u in range(JT // 4):
                        n = b * (JT // 4) + u
                        act.wait_ge(x_tr, n + 1)
                        dst = xpad[:, b * XP:(b + 1) * XP].rearrange("p (r w) -> p r w", w=PW)[:, 1:HR + 1, 1:PW - 1]
                        dst = dst.rearrange("p r (q j) -> p r q j", j=JT)
                        src = psB[n % 2][:].rearrange("p (j r q) -> p j r q", j=4, q=P // HR)
                        for j in range(4):
                            ins = nc.scalar.activation(dst[:, :, :, 4 * u + j], src[:, j, :, :], ACT.Copy)
                        ins.then_inc(x_out, 1)

            @block.gpsimd
            def _(pool):
                nc.gpsimd.memset(z[:], 0.0).then_inc(cleared, 1)
                nc.gpsimd.memset(xpad[:], 0.0).then_inc(pad_clear, 1)
                nc.gpsimd.memset(ones[:], 1.0).then_inc(const_step, 1)
                nc.gpsimd.memset(ident[:], 0.0).then_inc(const_step, 1)
                nc.gpsimd.memset(mask[:], 1.0).then_inc(const_step, 1)
                nc.gpsimd.memset(mhalf[:], -0.5).then_inc(const_step, 1)
                nc.gpsimd.memset(kv_acc[:], 0.0).then_inc(const_step, 1)
                nc.gpsimd.memset(v[:], 1.0).then_inc(const_step, 1)
                nc.gpsimd.memset(ones_rows[:], 0.0).then_inc(const_step, 1)
                nc.gpsimd.memset(qk_bias[:], 0.0).then_inc(const_step, 1)
                nc.gpsimd.memset(proj_bias[:], 0.0).then_inc(const_step, 1)
                nc.gpsimd.memset(proj[:], 0.0).then_inc(const_step, 1)
                pool.wait_ge(const_step, 10)
                nc.gpsimd.affine_select(out=ident[:], in_=ident[:], compare_op=ALU.not_equal, fill=1.0, base=0,
                                        pattern=[[-1, P]], channel_multiplier=1).then_inc(const_step, 1)
                m = mask[:].rearrange("p (b i) -> p b i", i=16)
                nc.gpsimd.affine_select(out=m, in_=m, compare_op=ALU.is_ge, fill=0.0, base=0,
                                        pattern=[[-16, 8], [0, 16]], channel_multiplier=1).then_inc(const_step, 1)
                pool.wait_ge(const_step, 12)
                nc.gpsimd.affine_select(out=m, in_=m, compare_op=ALU.is_ge, fill=0.0, base=15,
                                        pattern=[[16, 8], [0, 16]], channel_multiplier=-1).then_inc(const_step, 1)
                pool.wait_ge(const_step, 13)
                nc.gpsimd.memset(smA[:], 0.0).then_inc(consts, 1)

            @block.vector
            def _(dve):
                steps = [0]

                def step(ins):
                    steps[0] += 1
                    ins.then_inc(prep_step, 1)
                    dve.wait_ge(prep_step, steps[0])

                dve.wait_ge(w12_in, 32)
                nc.vector.tensor_reduce(absum[:, 0:1], w1n, AX.X, ALU.add, apply_absolute_value=True)
                nc.vector.tensor_reduce(absum[:, 1:2], w2n, AX.X, ALU.add, apply_absolute_value=True).then_inc(abs_done, 1)
                dve.wait_ge(tot_done, 1)
                step(nc.vector.tensor_scalar(tern[:, :, 0], psA[0][:, 0:2], 1.0 / (D * HID), 1e-5, ALU.mult, ALU.max))
                step(nc.vector.reciprocal(tern[:, :, 1], tern[:, :, 0]))
                step(nc.vector.reciprocal(tern[:, :, 2], tern[:, :, 1]))
                step(nc.vector.tensor_scalar(gelu_scale[:], tern[:, 0, 2:3], 1.0 / XS, None, ALU.mult))
                step(nc.vector.tensor_scalar(a2c[:], tern[:, 1, 2:3], 1.0 / XS, None, ALU.mult))
                for i, w in enumerate((w1n, w2n)):
                    step(nc.vector.tensor_scalar(tmp, w, tern[:, i, 1:2], 0.5, ALU.mult, ALU.is_gt))
                    step(nc.vector.tensor_scalar(w, w, tern[:, i, 1:2], -0.5, ALU.mult, ALU.is_lt))
                    step(nc.vector.tensor_tensor(w, tmp, w, ALU.subtract))
                    nc.vector.memset(absum[:, i:i + 1], 0.0).then_inc(ternary, 1)
                dve.wait_ge(col_done, 1)
                step(nc.vector.tensor_copy(cols[:, 0:32], psA[1][:, 0:32]))
                nc.vector.tensor_copy(g1c[:], cols[:, GCOL:GCOL + KH])
                step(nc.vector.tensor_scalar(g2c[:], cols[:, G2COL:G2COL + NC], XS, None, ALU.mult))
                dve.wait_ge(consts, 1)
                for part in (0, 32):
                    nc.vector.memset(ones_rows[part:part + 1, :], BROW)
                for r in range(2 * NC + KH):
                    ins = nc.vector.tensor_scalar(bc[:, r, :], ones[:], cols[:, G2COL + r:G2COL + r + 1], None, ALU.mult)
                ins.then_inc(bc_ready, 1)
                for n in range(2 * NC * KH // 4):
                    dve.wait_ge(tr_done, n + 1)
                    if n < NC * KH // 4:
                        h, q = n // 2, n % 2
                        dst, dst32 = w1T[h][:, q * 512:(q + 1) * 512], t1T[:, h, q * 512:(q + 1) * 512]
                    else:
                        h, q = divmod(n - NC * KH // 4, 2)
                        dst, dst32 = w2T[:, 4 * q:4 * q + 4, h * P:(h + 1) * P], t2T[:, 4 * q:4 * q + 4, h * P:(h + 1) * P]
                    src = psF[n % 2][:] if n < NC * KH // 4 else psF[n % 2][:].rearrange("p (c n) -> p c n", c=4)
                    nc.vector.tensor_copy(dst, src)
                    nc.vector.tensor_copy(dst32, src).then_inc(tr_out, 1)
                dve.wait_ge(wqkv_in, 64)
                nc.vector.tensor_scalar(wqkv_hi[:], wn, WS, None, ALU.mult).then_inc(hi_done, 1)
                dve.wait_ge(hi_done, 1)
                nc.vector.scalar_tensor_tensor(wqkv_lo[:], wn, WS, wqkv_hi[:], ALU.mult, ALU.subtract)
                dve.wait_ge(rows_in, 16 * 12)
                for dst, src in ((qk_bias, brow[:, 0:2 * D]), (proj_bias, brow[:, 2 * D:3 * D])):
                    nc.vector.tensor_scalar(dst[0:1, :], src[0:1, :], BROW, None, ALU.mult)
                    step(nc.vector.tensor_scalar(dst[32:33, :], src[32:33, :], BROW, None, ALU.mult))
                    step(nc.vector.scalar_tensor_tensor(dst[32:33, :], src[32:33, :], BROW, dst[32:33, :], ALU.mult, ALU.subtract))
                dve.wait_ge(small_in, 16 * 9)
                dve.wait_ge(pj_done, 1)
                for half in range(2):
                    rows = slice(half * C, (half + 1) * C)
                    nc.vector.tensor_scalar(proj[rows, half, :], psO[0][rows, 0:D], QS, None, ALU.mult)
                dve.wait_ge(sums_done, 1)
                nc.vector.tensor_scalar(g2w_bc[:], psA[0][:, 0:D], tern[:, 1, 2:3], None, ALU.mult)
                nc.vector.scalar_tensor_tensor(b2_bc[:], psA[1][:, 0:D], tern[:, 1, 2:3], b2_bc[:], ALU.mult, ALU.add)
                nc.vector.scalar_tensor_tensor(b1c[:], psF[0][:, 0:NC], tern[:, 0, 2:3], cols[:, B1COL:B1COL + NC],
                                               ALU.mult, ALU.add)
                nc.vector.tensor_tensor(bo_bc[:], psO[1][:, 0:D], bo_bc[:], ALU.add)
                dve.wait_ge(x_out, NB * JT // 4)
                for b in range(NB):
                    img = xpad[:, b * XP:(b + 1) * XP].rearrange("p (r w) -> p r w", w=PW)
                    nc.vector.tensor_copy(img[0:C, HR + 1, :], img[C:2 * C, 1, :])
                    nc.vector.tensor_copy(img[C:2 * C, 0, :], img[0:C, HR, :])

            @block.tensor
            def _(pe):
                pe.wait_ge(consts, 1)
                pe.wait_ge(abs_done, 1)
                nc.tensor.matmul(psA[0][:, 0:2], ones[:], absum[:], start=True, stop=True).then_inc(tot_done, 1)
                pe.wait_ge(rows_in, 16 * 12)
                nc.tensor.transpose(psA[1][:, 0:P], pack, ident[:]).then_inc(col_done, 1)
                for b in range(NB):
                    pe.wait_ge(x_in[b], 32)
                    for u in range(JT // 4):
                        n = b * (JT // 4) + u
                        if n >= 2:
                            pe.wait_ge(x_out, n - 1)
                        for j in range(4):
                            ins = nc.tensor.transpose(psB[n % 2][:, j * P:(j + 1) * P], xin[:, b, 4 * u + j, :, :], ident[:])
                        ins.then_inc(x_tr, 1)
                for n in range(2 * NC * KH // 4):
                    if n >= 2:
                        pe.wait_ge(tr_out, n - 1)
                    if n < NC * KH // 4:
                        pe.wait_ge(ternary, 1)
                        h, q = n // 2, n % 2
                        blocks = [w1n[:, (4 * q + c) * D + h * P:(4 * q + c) * D + (h + 1) * P] for c in range(4)]
                    else:
                        pe.wait_ge(ternary, 2)
                        h, q = divmod(n - NC * KH // 4, 2)
                        blocks = [w2n[:, h * HID + (4 * q + c) * P:h * HID + (4 * q + c + 1) * P] for c in range(4)]
                    for c, block_ in enumerate(blocks):
                        ins = nc.tensor.transpose(psF[n % 2][:, c * P:(c + 1) * P], block_, ident[:])
                    ins.then_inc(tr_done, 1)
                pe.wait_ge(small_in, 16 * 9)
                for b in range(2):
                    ins = nc.tensor.transpose(psO[0][:, b * P:(b + 1) * P], pn[:, b, :], ident[:])
                ins.then_inc(pj_done, 1)
                pe.wait_ge(bc_ready, 1)
                pe.wait_ge(tr_out, 2 * NC * KH // 4)
                for i in range(2):
                    for c in range(NC):
                        nc.tensor.matmul(psA[i][:, 0:D], bc[:, i * NC + c, :], t2T[:, c, :], start=(c == 0), stop=(c == NC - 1))
                pe.wait_ge(wqkv_in, 64)
                for h in range(KH):
                    nc.tensor.matmul(psO[1][:, 0:D], bc[:, 2 * NC + h, :], wo[:, h, :], start=(h == 0), stop=(h == KH - 1))
                for c in range(NC):
                    for h in range(KH):
                        ins = nc.tensor.matmul(psF[0][:, c:c + 1], t1T[:, h, c * P:(c + 1) * P], cols[:, BCOL + h:BCOL + h + 1],
                                               start=(h == 0), stop=(h == KH - 1))
                ins.then_inc(sums_done, 1)

        q_in = sem("q_in")
        stored = sem("stored")

        LAG = GI + 1

        def slot(ring, n):
            return ring[:, bass.ds((n % RING) * (T * D), T * D)].rearrange("p (t d) -> p t d", t=T)

        def per_head(ap, j):
            return ap[:, 2 * j:2 * j + 2, :].unsqueeze(3).to_broadcast([P, 2, ap.shape[2], HD])

        def image_loops(eng, only_A, A_and_B, all_three, close_image, B_and_F, only_F):
            with eng.Fori(0, GI) as n:
                only_A(n)
            close_image(0)
            A_and_B(GI, 0)
            with eng.Fori(0, NB - 1) as k:
                with eng.Fori((k * (2 * GI - 1)) // 2, k * GI + GI - 1) as m:
                    all_three(m)
                close_image(k + 1)
            with eng.Fori(NG - LAG, NG - 1) as m:
                B_and_F(m)
            only_F(NG - 1)

        with nc.Block() as block:

            @block.sync
            def _(sp):
                rows = out.rearrange("b n d -> (b n) d")

                def stage_q(m):
                    if isinstance(m, int):
                        sp.wait_ge(q_done, START + 2)
                    else:
                        sp.wait_ge(qT_done, START + 2 * m)
                        sp.wait_ge(y_done, START + 2 * m)
                    sp.dma_start(q_now[:], slot(q_ring, m)).then_inc(q_in, 16)

                def store(m):
                    firsts = [(m // GI) * (H * W) + (m % GI) * (2 * P) + half * (H * W // 2) for half in range(2)]
                    if not isinstance(m, int):
                        firsts = [sp.snap(first) for first in firsts]
                    sp.wait_ge(fin_done, START + T * m + T)
                    for half, first in enumerate(firsts):
                        dst = rows[bass.ds(first, 2 * P), :].rearrange("(t p) d -> p t d", p=P)
                        sp.dma_start(dst, res[:, 2 * half:2 * half + 2, :]).then_inc(stored, 16)

                stage_q(0)
                with sp.Fori(0, NG - 1) as m:
                    stage_q(m + 1)
                    store(m)
                store(NG - 1)
                sp.wait_ge(stored, 32 * NG)

            @block.tensor
            def _(pe):
                mm, tr = nc.tensor.matmul, nc.tensor.transpose

                def project(n):
                    pe.wait_ge(conv_step, START + 9 * n + 9)
                    for j in range(2):
                        pe.wait_ge(*((acc_done, START + n) if j == 0 else (v_out, START + 2 * n)))
                        for u in range(2):
                            dst = psA[j][:, u * D:(u + 1) * D]
                            mm(dst, conv[:, u * P:(u + 1) * P], proj[:, j, :], start=(u == 0), stop=False, skip_group_check=True)
                            ins = mm(dst, ones_rows[:], proj_bias[:], start=False, stop=True, skip_group_check=True)
                        ins.then_inc(proj_done, 1)

                def transpose_x(n):
                    pe.wait_ge(xn_done, START + n + 1)
                    pe.wait_ge(ssq_done, START + n + 1)
                    for h in range(KH):
                        for t in range(T):
                            ins = tr(psA[h][:, t * P:(t + 1) * P], y[:, t, h * P:(h + 1) * P], ident[:])
                        ins.then_inc(xT_done, 1)

                def split_product(dst, t, cols_, first, last):
                    tok = slice(t * P, (t + 1) * P)
                    n_ = 0
                    for h in range(KH):
                        for xa, wa in ((xT_hi, wqkv_hi), (xT_hi, wqkv_lo), (xT_lo, wqkv_hi)):
                            ins = mm(dst, xa[:, h, tok], wa[:, h, cols_], start=(first and n_ == 0),
                                     stop=(last and n_ == 3 * KH - 1), skip_group_check=True)
                            n_ += 1
                    return ins

                def project_qk(n, t):
                    bank = (0, 1, 1, 0)[t]
                    if t == 0:
                        pe.wait_ge(xlo_done, START + 2 * n + 2)
                    elif t == 2:
                        pe.wait_ge(shift_done, START + 4 * n + 2)
                    elif t == 3:
                        pe.wait_ge(v_out, START + 2 * n + 1)
                    split_product(psA[bank][:], t, slice(0, 2 * D), True, False)
                    mm(psA[bank][:], ones_rows[:], qk_bias[:], start=False, stop=True, skip_group_check=True).then_inc(qkp_done, 1)

                def project_v(n, j):
                    pe.wait_ge(shift_done, START + 4 * n + (1, 3)[j])
                    for u in range(2):
                        ins = split_product(psA[j][:, u * D:(u + 1) * D], 2 * j + u, slice(2 * D, 3 * D), u == 0, True)
                    ins.then_inc(vp_done, 1)

                def keys_values(n):
                    pe.wait_ge(k_done, START + 2 * n + 2)
                    pe.wait_ge(v_out, START + 2 * n + 2)
                    pe.wait_ge(shift_done, START + 4 * n + 4)
                    for t in range(T):
                        for h in range(KH):
                            ins = mm(psA[0][:, h * VC:(h + 1) * VC], qk[:, t, D + h * P:D + (h + 1) * P], v[:, t, h, :],
                                     start=(t == 0 and h == 0), stop=(t == T - 1), skip_group_check=True)
                    ins.then_inc(ctx_done, 1)

                def transpose_q(m):
                    pe.wait_ge(q_in, 16 * m + 16)
                    pe.wait_ge(x2lo_done, START + 2 * m)
                    for h in range(KH):
                        for t in range(T):
                            ins = tr(psB[h][:, t * P:(t + 1) * P], q_now[:, t, h * P:(h + 1) * P], ident[:])
                        ins.then_inc(qT_done, 1)

                def attend(m, t):
                    if t == 0:
                        pe.wait_ge(qT_out, START + 2 * m + 2)
                        pe.wait_ge(kv_ready, START + m // GI + 1)
                    elif t >= 2:
                        pe.wait_ge(num_done, START + 4 * m + t - 1)
                    for h in range(KH):
                        ins = mm(psB[t % 2][:, h * CC:(h + 1) * CC], qT[:, h, t * P:(t + 1) * P], kv[:, h, :],
                                 start=(h == 0), stop=True, skip_group_check=True)
                    ins.then_inc(qc_done, 1)

                def transpose_y(m):
                    pe.wait_ge(y_done, START + 2 * m + 2)
                    for h in range(KH):
                        for t in range(T):
                            ins = tr(psB[h][:, t * P:(t + 1) * P], y1[:, t, h * P:(h + 1) * P], ident[:])
                        ins.then_inc(yT_done, 1)

                def output_product(m):
                    pe.wait_ge(yT_out, START + 2 * m + 2)
                    for j in range(2):
                        for u in range(2):
                            t = 2 * j + u
                            for h in range(KH):
                                ins = mm(psB[j][:, u * D:(u + 1) * D], yT[:, h, t * P:(t + 1) * P], wo[:, h, :],
                                         start=(u == 0 and h == 0), stop=(h == KH - 1), skip_group_check=True)
                        ins.then_inc(wo_done, 1)

                def transpose_x2(m):
                    pe.wait_ge(x2_done, START + m + 1)
                    for h in range(KH):
                        for t in range(T):
                            ins = tr(psB[h][:, t * P:(t + 1) * P], x2[:, t, h * P:(h + 1) * P], ident[:])
                        ins.then_inc(x2T_done, 1)

                def up(m, c):
                    if c == 0:
                        pe.wait_ge(x2lo_done, START + 2 * m + 2)
                    if c < 2:
                        pe.wait_ge(ssum_done, START + 2 * m)
                    else:
                        pe.wait_ge(g_done, START + NC * m + c - 1)
                    n_ = 0
                    for h in range(KH):
                        for xa in (x2T_hi, x2T_lo):
                            ins = mm(psF[c % 2][:], w1T[h][:, c * P:(c + 1) * P], xa[:, h, :], start=(n_ == 0), stop=(n_ == 3))
                            n_ += 1
                    ins.then_inc(f1_done, 1)

                def down(m, c):
                    if c == 0:
                        pe.wait_ge(u_done, START + T * m)
                    pe.wait_ge(glo_done, START + NC * m + c + 1)
                    for t in range(T):
                        for ga in (g_hi, g_lo):
                            ins = mm(psO[t // 2][:, (t % 2) * D:(t % 2 + 1) * D], ga[:, c % HB, t * P:(t + 1) * P], w2T[:, c, :],
                                     start=(c == 0 and t % 2 == 0 and ga is g_hi), stop=(c == NC - 1 and ga is g_lo),
                                     skip_group_check=True)
                    ins.then_inc(f2_done, 1)

                def transpose_sums(m):
                    pe.wait_ge(sum_done, START + 7 * m + 7)
                    pe.wait_ge(g_done, START + NC * m + NC)
                    for i in range(2):
                        for t in range(T):
                            ins = tr(psF[i][:, t * P:(t + 1) * P], s12[:, i, t * P:(t + 1) * P], ident[:])
                        ins.then_inc(st_done, 1)

                def only_A(n):
                    project(n)
                    transpose_x(n)
                    project_qk(n, 0)
                    project_qk(n, 1)
                    project_v(n, 0)
                    project_qk(n, 2)
                    project_qk(n, 3)
                    project_v(n, 1)
                    keys_values(n)

                def A_and_B(n, b):
                    transpose_q(b)
                    project(n)
                    for t in range(T):
                        attend(b, t)
                    transpose_y(b)
                    transpose_x(n)
                    output_product(b)
                    project_qk(n, 0)
                    project_qk(n, 1)
                    project_v(n, 0)
                    transpose_x2(b)
                    project_qk(n, 2)
                    project_qk(n, 3)
                    project_v(n, 1)
                    keys_values(n)

                def all_three(m):
                    n, b = m + LAG, m + 1
                    up(m, 0)
                    transpose_q(b)
                    up(m, 1)
                    down(m, 0)
                    project(n)
                    up(m, 2)
                    down(m, 1)
                    for t in range(T):
                        attend(b, t)
                    up(m, 3)
                    down(m, 2)
                    up(m, 4)
                    down(m, 3)
                    transpose_y(b)
                    up(m, 5)
                    down(m, 4)
                    output_product(b)
                    transpose_x(n)
                    up(m, 6)
                    down(m, 5)
                    project_qk(n, 0)
                    project_qk(n, 1)
                    project_v(n, 0)
                    up(m, 7)
                    down(m, 6)
                    project_qk(n, 2)
                    project_qk(n, 3)
                    project_v(n, 1)
                    transpose_x2(b)
                    down(m, 7)
                    transpose_sums(m)
                    keys_values(n)

                def B_and_F(m):
                    b = m + 1
                    up(m, 0)
                    transpose_q(b)
                    up(m, 1)
                    down(m, 0)
                    for t in range(T):
                        attend(b, t)
                    up(m, 2)
                    down(m, 1)
                    up(m, 3)
                    down(m, 2)
                    transpose_y(b)
                    up(m, 4)
                    down(m, 3)
                    output_product(b)
                    for c in (5, 6, 7):
                        up(m, c)
                        down(m, c - 1)
                    transpose_x2(b)
                    down(m, 7)
                    transpose_sums(m)

                def only_F(m):
                    up(m, 0)
                    for c in range(1, NC):
                        up(m, c)
                        down(m, c - 1)
                    down(m, NC - 1)
                    transpose_sums(m)

                image_loops(pe, only_A, A_and_B, all_three, lambda k: None, B_and_F, only_F)

            @block.scalar
            def _(act):
                fn = nc.scalar.activation

                def gelu_y(n):
                    act.wait_ge(xT_done, START + 2 * n)
                    for j in range(2):
                        act.wait_ge(proj_done, START + 2 * n + j + 1)
                        fn(y[:, 2 * j:2 * j + 2, :], psA[j][:].rearrange("p (t d) -> p t d", t=2), ACT.Gelu,
                           scale=1.0 / QS).then_inc(gelu_done, 1)
                    act.wait_ge(gelu_done, START + 2 * n + 2)
                    act.wait_ge(xn_done, START + n)
                    for t in range(T):
                        ins = fn(psA[t // 2][:, (t % 2) * D:(t % 2 + 1) * D], y[:, t, :], ACT.Square, accum_out=ssq[:, t:t + 1])
                    ins.then_inc(ssq_done, 1)

                def high_x(n):
                    act.wait_ge(vp_done, START + 2 * n)
                    for h in range(KH):
                        act.wait_ge(xT_done, START + 2 * n + h + 1)
                        fn(xT_hi[:, h, :], psA[h][:], ACT.Copy).then_inc(xhi_done, 1)

                def take_v(n, j):
                    if j == 0:
                        act.wait_ge(ctx_done, START + n)
                    act.wait_ge(vp_done, START + 2 * n + j + 1)
                    fn(v[:, 2 * j:2 * j + 2, :, 0:P], psA[j][:].rearrange("p (t h d) -> p t h d", t=2, h=KH), ACT.Copy,
                       scale=1.0 / QS).then_inc(v_out, 1)

                def exps(n, j):
                    act.wait_ge(shift_done, START + 4 * n + 2 * j + 2)
                    fn(qk[:, 2 * j:2 * j + 2, :], qk[:, 2 * j:2 * j + 2, :], ACT.Exp, scale=1.0 / QS).then_inc(exp_done, 1)

                def take_qT(m):
                    act.wait_ge(wo_done, START + 2 * m)
                    for h in range(KH):
                        act.wait_ge(qT_done, START + 2 * m + h + 1)
                        fn(qT[:, h, :], psB[h][:], ACT.Copy).then_inc(qT_out, 1)

                def take_yT(m):
                    act.wait_ge(qc_done, START + 4 * m + 4)
                    for h in range(KH):
                        act.wait_ge(yT_done, START + 2 * m + h + 1)
                        fn(yT[:, h, :], psB[h][:], ACT.Copy).then_inc(yT_out, 1)

                def high_x2(m):
                    act.wait_ge(f1_done, START + NC * m)
                    for h in range(KH):
                        act.wait_ge(x2T_done, START + 2 * m + h + 1)
                        fn(x2T_hi[:, h, :], psB[h][:], ACT.Copy, scale=g1c[:, h:h + 1]).then_inc(x2hi_done, 1)

                def gelu_g(m, c):
                    act.wait_ge(f1_done, START + NC * m + c + 1)
                    if c < GB:
                        act.wait_ge(glo_done, START + NC * m)
                        act.wait_ge(sum_done, START + 7 * m)
                    else:
                        act.wait_ge(glo_done, START + NC * m + c - GB + 1)
                        act.wait_ge(sum_done, START + 7 * m + max(c - GB, 1))
                    fn(g[:, c % GB, :], psF[c % 2][:], ACT.Gelu, scale=gelu_scale[:], bias=b1c[:, c:c + 1]).then_inc(g_done, 1)
                    act.wait_ge(g_done, START + NC * m + c + 1)
                    act.wait_ge(f2_done, START + NC * m + max(c - HB + 1, 0))
                    fn(g_hi[:, c % HB, :], g[:, c % GB, :], ACT.Copy, scale=g2c[:, c:c + 1]).then_inc(ghi_done, 1)
                    act.wait_ge(sum_done, START + 7 * m + (max(c - SB, 1) if c >= SB else 0))
                    fn(sq[:, c % SB, :], g[:, c % GB, :], ACT.Square).then_inc(sq_done, 1)

                def only_A(n):
                    gelu_y(n)
                    high_x(n)
                    take_v(n, 0)
                    exps(n, 0)
                    take_v(n, 1)
                    exps(n, 1)

                def A_and_B(n, b):
                    take_qT(b)
                    gelu_y(n)
                    take_yT(b)
                    high_x(n)
                    take_v(n, 0)
                    high_x2(b)
                    exps(n, 0)
                    take_v(n, 1)
                    exps(n, 1)

                def all_three(m):
                    n, b = m + LAG, m + 1
                    gelu_g(m, 0)
                    take_qT(b)
                    gelu_g(m, 1)
                    gelu_y(n)
                    gelu_g(m, 2)
                    gelu_g(m, 3)
                    gelu_g(m, 4)
                    take_yT(b)
                    gelu_g(m, 5)
                    high_x(n)
                    gelu_g(m, 6)
                    take_v(n, 0)
                    gelu_g(m, 7)
                    exps(n, 0)
                    take_v(n, 1)
                    high_x2(b)
                    exps(n, 1)

                def B_and_F(m):
                    b = m + 1
                    gelu_g(m, 0)
                    take_qT(b)
                    for c in (1, 2, 3):
                        gelu_g(m, c)
                    take_yT(b)
                    for c in (4, 5, 6, 7):
                        gelu_g(m, c)
                    high_x2(b)

                def only_F(m):
                    for c in range(NC):
                        gelu_g(m, c)

                image_loops(act, only_A, A_and_B, all_three, lambda k: None, B_and_F, only_F)

            @block.gpsimd
            def _(pool):
                tt = nc.gpsimd.tensor_tensor

                def weigh(n):
                    pool.wait_ge(xn_done, START + n)
                    for j in range(2):
                        pool.wait_ge(gelu_done, START + 2 * n + j + 1)
                        tt(z[:, 2 * j:2 * j + 2, :], y[:, 2 * j:2 * j + 2, :], norm_bc[:].unsqueeze(1).to_broadcast([P, 2, D]),
                           ALU.mult).then_inc(z_done, 1)

                def powers_A(n):
                    pool.wait_ge(ms_done, START + n + 1)
                    tt(smA[:, 1, :], smA[:, 0, :], mhalf[:], ALU.pow).then_inc(rms_done, 1)
                    pool.wait_ge(varA_done, START + n + 1)
                    tt(smA[:, 4, :], smA[:, 3, :], mhalf[:], ALU.pow).then_inc(rstdA_done, 1)

                def normalise(n, j):
                    pool.wait_ge(rs_done, START + 2 * n + j + 1)
                    e = qk[:, 2 * j:2 * j + 2, :].rearrange("p t (n d) -> p t n d", d=HD)
                    r = per_head(rs, j)
                    tt(e[:, :, NH:, :], e[:, :, NH:, :], r[:, :, NH:, :],
                       ALU.mult).then_inc(k_done, 1)
                    q = slot(q_ring, n)[:, 2 * j:2 * j + 2, :].rearrange("p t (n d) -> p t n d", d=HD)
                    tt(q, e[:, :, 0:NH, :], r[:, :, 0:NH, :], ALU.mult).then_inc(q_done, 1)

                def add_q(m):
                    pool.wait_ge(q_in, 16 * m + 16)
                    for j in range(2):
                        pool.wait_ge(num_done, START + 4 * m + 2 * j + 2)
                        part = y1[:, 2 * j:2 * j + 2, :]
                        tt(part, part, q_now[:, 2 * j:2 * j + 2, :], ALU.add).then_inc(y_done, 1)

                def powers_B(m):
                    for i in range(2):
                        pool.wait_ge(varB_done, START + 2 * m + i + 1)
                        tt(smB[:, 2 * i + 1, :], smB[:, 2 * i, :], mhalf[:], ALU.pow).then_inc(rstdB_done, 1)

                def residual(m):
                    pool.wait_ge(h2_done, START + 2 * m + 2)
                    if not (isinstance(m, int) and m == 0):
                        pool.wait_ge(stored, 32 * m)
                    tt(res[:], h2, b2_bc[:].unsqueeze(1).to_broadcast([P, T, D]), ALU.add).then_inc(res_done, 1)

                def sums(m, c):
                    if c == 0:
                        return
                    pool.wait_ge(sq_done, START + NC * m + c + 1)
                    if c == 1:
                        pool.wait_ge(st_done, START + 2 * m)
                        tt(s12[:, 0, :], g[:, 0, :], g[:, 1, :], ALU.add).then_inc(s1_done, 1)
                        tt(s12[:, 1, :], sq[:, 0, :], sq[:, 1, :], ALU.add).then_inc(sum_done, 1)
                    else:
                        pool.wait_ge(s1_done, START + 7 * m + c - 1)
                        tt(s12[:, 0, :], s12[:, 0, :], g[:, c % GB, :], ALU.add).then_inc(s1_done, 1)
                        pool.wait_ge(sum_done, START + 7 * m + c - 1)
                        tt(s12[:, 1, :], s12[:, 1, :], sq[:, c % SB, :], ALU.add).then_inc(sum_done, 1)

                def power_F(m):
                    pool.wait_ge(varF_done, START + m + 1)
                    tt(smF[:, 5, :], smF[:, 4, :], mhalf[:], ALU.pow).then_inc(rstdF_done, 1)

                def only_A(n):
                    weigh(n)
                    powers_A(n)
                    normalise(n, 0)
                    normalise(n, 1)

                def A_and_B(n, b):
                    weigh(n)
                    add_q(b)
                    powers_A(n)
                    powers_B(b)
                    residual(b)
                    normalise(n, 0)
                    normalise(n, 1)

                def all_three(m):
                    n, b = m + LAG, m + 1
                    sums(m, 1)
                    weigh(n)
                    powers_A(n)
                    sums(m, 2)
                    add_q(b)
                    sums(m, 3)
                    sums(m, 4)
                    sums(m, 5)
                    powers_B(b)
                    sums(m, 6)
                    normalise(n, 0)
                    sums(m, 7)
                    normalise(n, 1)
                    power_F(m)
                    residual(b)

                def B_and_F(m):
                    b = m + 1
                    sums(m, 1)
                    add_q(b)
                    for c in (2, 3, 4):
                        sums(m, c)
                    powers_B(b)
                    for c in (5, 6, 7):
                        sums(m, c)
                    power_F(m)
                    residual(b)

                def only_F(m):
                    for c in range(NC):
                        sums(m, c)
                    power_F(m)

                image_loops(pool, only_A, A_and_B, all_three, lambda k: None, B_and_F, only_F)

            @block.vector
            def _(dve):
                tt, ts, stt = nc.vector.tensor_tensor, nc.vector.tensor_scalar, nc.vector.scalar_tensor_tensor

                def convolve(n, taps):
                    for k in taps:
                        dy, dx = divmod(k, 3)
                        first = (n // GI) * XP + (n % GI) * (GR * PW) + dy * PW
                        win = xpad[:, bass.ds(first, GR * PW)].rearrange("p (r w) -> p r w", w=PW)[:, :, dx:dx + W]
                        acc = conv[:].rearrange("p (r w) -> p r w", w=W)
                        if k == 0:
                            dve.wait_ge(proj_done, START + 2 * n)
                            ts(acc, win, conv_k[:, 0:1], conv_c[:], ALU.mult, ALU.add).then_inc(conv_step, 1)
                        else:
                            dve.wait_ge(conv_step, START + 9 * n + k)
                            stt(acc, win, conv_k[:, k:k + 1], acc, ALU.mult, ALU.add).then_inc(conv_step, 1)

                def norm_h(n):
                    for t in range(T):
                        if t % 2 == 0:
                            dve.wait_ge(z_done, START + 2 * n + t // 2 + 1)
                        ins = nc.vector.bn_stats(stA[:, t, :], z[:, t, :])
                    ins.then_inc(normA_step, 1)
                    dve.wait_ge(ssq_done, START + n + 1)
                    dve.wait_ge(normA_step, START + 5 * n + 1)
                    ts(smA[:, 0, :], ssq[:], 1.0 / D, TOK_EPS, ALU.mult, ALU.add).then_inc(ms_done, 1)
                    for t in range(T):
                        ins = nc.vector.bn_aggr(mvA[:, t, :], stA[:, t, :])
                    ins.then_inc(normA_step, 1)
                    dve.wait_ge(normA_step, START + 5 * n + 2)
                    dve.wait_ge(rms_done, START + n + 1)
                    tt(smA[:, 2, :], smA[:, 1, :], smA[:, 1, :], ALU.mult).then_inc(normA_step, 1)
                    dve.wait_ge(normA_step, START + 5 * n + 3)
                    tt(smA[:, 3, :], smA[:, 2, :], mvA[:, :, 1], ALU.mult).then_inc(normA_step, 1)
                    dve.wait_ge(normA_step, START + 5 * n + 4)
                    ts(smA[:, 3, :], smA[:, 3, :], LN_EPS, None, ALU.add).then_inc(varA_done, 1)
                    hs = slot(h_ring, n)
                    for t in range(T):
                        stt(hs[:, t, :], z[:, t, :], smA[:, 1, t:t + 1], bo_bc[:], ALU.mult, ALU.add)
                    dve.wait_ge(rstdA_done, START + n + 1)
                    stt(smA[:, 5, :], smA[:, 1, :], XS, smA[:, 4, :], ALU.mult, ALU.mult).then_inc(normA_step, 1)
                    dve.wait_ge(normA_step, START + 5 * n + 5)
                    for t in range(T):
                        ins = ts(y[:, t, :], z[:, t, :], mvA[:, t, 0:1], smA[:, 5, t:t + 1], ALU.subtract, ALU.mult)
                    ins.then_inc(xn_done, 1)

                def low_x(n):
                    for h in range(KH):
                        dve.wait_ge(xhi_done, START + 2 * n + h + 1)
                        tt(xT_lo[:, h, :], psA[h][:], xT_hi[:, h, :], ALU.subtract).then_inc(xlo_done, 1)

                def shift(n, t):
                    bank = psA[(0, 1, 1, 0)[t]][:].rearrange("p (n d) -> p n d", d=HD)
                    dve.wait_ge(qkp_done, START + 4 * n + t + 1)
                    nc.vector.tensor_reduce(mx[:, t, :], bank, AX.X, ALU.max).then_inc(max_done, 1)
                    if t == 0:
                        dve.wait_ge(q_done, START + 2 * n)
                        dve.wait_ge(ctx_done, START + n)
                    dve.wait_ge(max_done, START + 4 * n + t + 1)
                    tt(qk[:, t, :].rearrange("p (n d) -> p n d", d=HD), bank,
                       mx[:, t, :].unsqueeze(2).to_broadcast([P, 2 * NH, HD]), ALU.subtract).then_inc(shift_done, 1)

                def head_sums(n, j):
                    dve.wait_ge(exp_done, START + 2 * n + j + 1)
                    nc.vector.tensor_reduce(sm[:, 2 * j:2 * j + 2, :], qk[:, 2 * j:2 * j + 2, :].rearrange("p t (n d) -> p t n d", d=HD),
                                            AX.X, ALU.add).then_inc(hsum_done, 1)
                    dve.wait_ge(hsum_done, START + 2 * n + j + 1)
                    nc.vector.reciprocal(rs[:, 2 * j:2 * j + 2, :], sm[:, 2 * j:2 * j + 2, :]).then_inc(rs_done, 1)

                def gather_kv(n):
                    dve.wait_ge(ctx_done, START + n + 1)
                    dve.wait_ge(acc_done, START + n)
                    acc = kv_acc[:].rearrange("p h c -> p (h c)")
                    tt(acc, acc, psA[0][:, 0:KH * VC], ALU.add).then_inc(acc_done, 1)

                def close_image(k):
                    dve.wait_ge(acc_done, START + GI * k + GI)
                    dve.wait_ge(qc_done, START + 4 * GI * k)
                    for h in range(KH):
                        tt(kv[:, h, 0:P], kv_acc[:, h, 0:P], mask[:], ALU.mult)
                        ins = ts(kv[:, h, P:CC], mask[:].rearrange("p (n d) -> p n d", d=HD)[:, :, 0], kv_acc[:, h, P:VC], None,
                                 ALU.mult)
                    ins.then_inc(kv_ready, 1)
                    dve.wait_ge(kv_ready, START + k + 1)
                    nc.vector.memset(kv_acc[:], 0.0)

                def divide(m, t):
                    ps = psB[t % 2][:, 0:KH * CC].rearrange("p (h c) -> p h c", h=KH)
                    dve.wait_ge(qc_done, START + 4 * m + t + 1)
                    nc.vector.reciprocal(rden[:, t, :, :], ps[:, :, P:CC]).then_inc(rden_done, 1)
                    if t == 0:
                        dve.wait_ge(x2T_done, START + 2 * m)
                    dve.wait_ge(rden_done, START + 4 * m + t + 1)
                    tt(y1[:, t, :].rearrange("p (h n d) -> p h n d", h=KH, d=HD), ps[:, :, 0:P].rearrange("p h (n d) -> p h n d", d=HD),
                       rden[:, t, :, :].unsqueeze(3).to_broadcast([P, KH, HH, HD]), ALU.mult).then_inc(num_done, 1)

                def add_h(m):
                    dve.wait_ge(res_done, START + m)
                    for j in range(2):
                        dve.wait_ge(wo_done, START + 2 * m + j + 1)
                        tt(h2[:, 2 * j:2 * j + 2, :], psB[j][:].rearrange("p (t d) -> p t d", t=2),
                           slot(h_ring, m)[:, 2 * j:2 * j + 2, :], ALU.add).then_inc(h2_done, 1)

                def norm_h2(m):
                    for t in range(T):
                        if t % 2 == 0:
                            dve.wait_ge(h2_done, START + 2 * m + t // 2 + 1)
                        ins = nc.vector.bn_stats(stB[:, t, :], h2[:, t, :])
                    ins.then_inc(normB_step, 1)
                    dve.wait_ge(normB_step, START + 5 * m + 1)
                    nc.vector.memset(carrier[:], 0.0)
                    for t in range(T):
                        ins = nc.vector.bn_aggr(mvB[:, t, :], stB[:, t, :])
                    ins.then_inc(normB_step, 1)
                    dve.wait_ge(normB_step, START + 5 * m + 2)
                    ts(smB[:, 0, :], mvB[:, :, 1], LN_EPS, None, ALU.add).then_inc(varB_done, 1)
                    dve.wait_ge(rstdB_done, START + 2 * m + 1)
                    tt(smB[:, 4, :], smB[:, 1, :], smB[:, 1, :], ALU.mult).then_inc(normB_step, 1)
                    dve.wait_ge(normB_step, START + 5 * m + 3)
                    tt(smB[:, 2, :], smB[:, 4, :], mvB[:, :, 1], ALU.mult).then_inc(normB_step, 1)
                    dve.wait_ge(normB_step, START + 5 * m + 4)
                    ts(smB[:, 2, :], smB[:, 2, :], LN_EPS, None, ALU.add).then_inc(varB_done, 1)
                    dve.wait_ge(rstdB_done, START + 2 * m + 2)
                    stt(smB[:, 5, :], smB[:, 1, :], XS, smB[:, 3, :], ALU.mult, ALU.mult).then_inc(normB_step, 1)
                    dve.wait_ge(normB_step, START + 5 * m + 5)
                    dve.wait_ge(yT_done, START + 2 * m + 2)
                    for t in range(T):
                        ins = ts(x2[:, t, :], h2[:, t, :], mvB[:, t, 0:1], smB[:, 5, t:t + 1], ALU.subtract, ALU.mult)
                    ins.then_inc(x2_done, 1)

                def low_x2(m):
                    for h in range(KH):
                        dve.wait_ge(x2hi_done, START + 2 * m + h + 1)
                        stt(x2T_lo[:, h, :], psB[h][:], g1c[:, h:h + 1], x2T_hi[:, h, :], ALU.mult, ALU.subtract).then_inc(x2lo_done, 1)

                def low_g(m, c):
                    dve.wait_ge(ghi_done, START + NC * m + c + 1)
                    stt(g_lo[:, c % HB, :], g[:, c % GB, :], g2c[:, c:c + 1], g_hi[:, c % HB, :], ALU.mult,
                        ALU.subtract).then_inc(glo_done, 1)

                def finish(m):
                    for i in range(2):
                        dve.wait_ge(st_done, START + 2 * m + i + 1)
                        nc.vector.tensor_reduce(smF[:, i, :], psF[i][:].rearrange("p (t n) -> p t n", t=T), AX.X,
                                                ALU.add).then_inc(ssum_done, 1)
                    dve.wait_ge(ssum_done, START + 2 * m + 2)
                    ts(smF[:, 2, :], smF[:, 0, :], -1.0 / HID, None, ALU.mult)
                    ts(smF[:, 3, :], smF[:, 1, :], 1.0 / HID, LN_EPS, ALU.mult, ALU.add).then_inc(normF_step, 1)
                    dve.wait_ge(normF_step, START + 2 * m + 1)
                    tt(smF[:, 4, :], smF[:, 2, :], smF[:, 2, :], ALU.mult).then_inc(normF_step, 1)
                    dve.wait_ge(normF_step, START + 2 * m + 2)
                    tt(smF[:, 4, :], smF[:, 3, :], smF[:, 4, :], ALU.subtract).then_inc(varF_done, 1)
                    dve.wait_ge(rstdF_done, START + m + 1)
                    ts(smF[:, 6, :], smF[:, 5, :], a2c[:], None, ALU.mult)
                    tt(smF[:, 7, :], smF[:, 5, :], smF[:, 2, :], ALU.mult).then_inc(coef_done, 1)
                    dve.wait_ge(coef_done, START + m + 1)
                    dve.wait_ge(f2_done, START + NC * m + NC)
                    dve.wait_ge(res_done, START + m + 1)
                    for t in range(T):
                        stt(res[:, t, :], psO[t // 2][:, (t % 2) * D:(t % 2 + 1) * D], smF[:, 6, t:t + 1], res[:, t, :],
                            ALU.mult, ALU.add).then_inc(u_done, 1)
                    for t in range(T):
                        dve.wait_ge(u_done, START + T * m + t + 1)
                        stt(res[:, t, :], g2w_bc[:], smF[:, 7, t:t + 1], res[:, t, :], ALU.mult, ALU.add).then_inc(fin_done, 1)

                def only_A(n):
                    convolve(n, range(9))
                    norm_h(n)
                    low_x(n)
                    for j in range(2):
                        shift(n, 2 * j)
                        shift(n, 2 * j + 1)
                        head_sums(n, j)
                    gather_kv(n)

                def A_and_B(n, b):
                    convolve(n, range(9))
                    for t in range(T):
                        divide(b, t)
                    norm_h(n)
                    low_x(n)
                    add_h(b)
                    norm_h2(b)
                    shift(n, 0)
                    shift(n, 1)
                    low_x2(b)
                    head_sums(n, 0)
                    shift(n, 2)
                    shift(n, 3)
                    head_sums(n, 1)
                    gather_kv(n)

                def all_three(m):
                    n, b = m + LAG, m + 1
                    convolve(n, range(0, 5))
                    low_g(m, 0)
                    convolve(n, range(5, 9))
                    low_g(m, 1)
                    for t in range(T):
                        divide(b, t)
                    low_g(m, 2)
                    norm_h(n)
                    low_g(m, 3)
                    low_g(m, 4)
                    low_g(m, 5)
                    add_h(b)
                    low_x(n)
                    norm_h2(b)
                    low_g(m, 6)
                    shift(n, 0)
                    shift(n, 1)
                    low_g(m, 7)
                    head_sums(n, 0)
                    shift(n, 2)
                    shift(n, 3)
                    low_x2(b)
                    head_sums(n, 1)
                    finish(m)
                    gather_kv(n)

                def B_and_F(m):
                    b = m + 1
                    low_g(m, 0)
                    for t in range(T):
                        divide(b, t)
                    for c in (1, 2, 3, 4):
                        low_g(m, c)
                    add_h(b)
                    low_g(m, 5)
                    norm_h2(b)
                    low_g(m, 6)
                    low_g(m, 7)
                    low_x2(b)
                    finish(m)

                def only_F(m):
                    for c in range(NC):
                        low_g(m, c)
                    finish(m)

                image_loops(dve, only_A, A_and_B, all_three, close_image, B_and_F, only_F)


_INS = ["x", "L0_tok_conv_w", "L0_tok_conv_b", "L0_tok_proj_w", "L0_tok_proj_b", "L0_tok_norm_w",
        "L0_attn_Wq", "L0_attn_bq", "L0_attn_Wk", "L0_attn_bk", "L0_attn_Wv", "L0_attn_bv", "L0_attn_Wo", "L0_attn_bo",
        "L0_ffn_ln1_g", "L0_ffn_ln1_b", "L0_ffn_w1", "L0_ffn_b1", "L0_ffn_ln2_g", "L0_ffn_ln2_b", "L0_ffn_w2", "L0_ffn_b2"]


def kernel(**inputs):
    import numpy as np
    import concourse.bacc as bacc
    from concourse.bass_utils import run_bass_kernel_spmd

    nc = bacc.Bacc("TRN2", target_bir_lowering=False, num_devices=1)
    arrays, args = {}, []
    for name in _INS:
        a = np.ascontiguousarray(inputs[name])
        arrays[f"in_{name}"] = a
        args.append(nc.dram_tensor(f"in_{name}", a.shape, mybir.dt.from_np(a.dtype), kind="ExternalInput").ap())
    B, H, W, _ = inputs["x"].shape
    D = inputs["L0_attn_Wq"].shape[0]
    out = nc.dram_tensor("out", (B, H * W, D), F32, kind="ExternalOutput").ap()
    vit_block(nc, *args, out)
    return run_bass_kernel_spmd(nc, [arrays], core_ids=[0]).results[0]["out"]
```

```python
from contextlib import ExitStack

import concourse.bass as bass
from concourse import mybir

F32 = mybir.dt.float32
F16 = mybir.dt.float16
ALU = mybir.AluOpType
ACT = mybir.ActivationFunctionType
AX = mybir.AxisListType

P = 128
XS = 16.0
WS = 64.0
QS = XS * WS
BROW = 32.0
START = 8
RING = 9
TOK_EPS, LN_EPS = 1e-4, 1e-5


def vit_block(nc, x, conv_w, conv_b, proj_w, proj_b, norm_w, Wq, bq, Wk, bk, Wv, bv, Wo, bo,
              ln1_g, ln1_b, w1, b1, ln2_g, ln2_b, w2, b2, out):
    NB, H, W, C = x.shape
    D = Wq.shape[0]
    HID = w1.shape[0]
    NH, HD = 16, D // 16
    KH = D // P
    NC = HID // P
    T = 4
    TOK = T * P
    GI = H * W // TOK
    NG = NB * GI
    HR = H // 2
    GR = HR // GI
    PR, PW = HR + 2, W + 2
    XP = PR * PW
    HH = NH // KH
    VC = P + 1
    CC = P + HH
    JT = H * W // 2 // P
    assert C == 64 and D == 256 and HD == 16 and GI == 8 and GR * W == 2 * P and P % HD == 0

    ctx = ExitStack()
    with ctx:
        def sb(name, shape, dt=F32):
            return ctx.enter_context(nc.sbuf_tensor(name, shape, dt))

        def sem(name):
            return ctx.enter_context(nc.semaphore(name))

        h_ring = sb("h_ring", [P, RING * T * D])
        q_ring = sb("q_ring", [P, RING * T * D])
        xpad = sb("xpad", [P, NB * XP])
        w1T = [sb(f"w1T{h}", [P, HID], F16) for h in range(KH)]
        w2T = sb("w2T", [P, NC, D], F16)
        wqkv_hi = sb("wqkv_hi", [P, KH, 3 * D], F16)
        wqkv_lo = sb("wqkv_lo", [P, KH, 3 * D], F16)
        wo = sb("wo", [P, KH, D])
        proj = sb("proj", [P, 2, D])
        ones_rows = sb("ones_rows", [P, P], F16)
        qk_bias = sb("qk_bias", [P, 2 * D], F16)
        proj_bias = sb("proj_bias", [P, D], F16)
        norm_bc = sb("norm_bc", [P, D])
        bo_bc = sb("bo_bc", [P, D])
        b2_bc = sb("b2_bc", [P, D])
        g2w_bc = sb("g2w_bc", [P, D])
        ident = sb("ident", [P, P])
        mask = sb("mask", [P, P])
        ones = sb("ones", [P, P])
        cols = sb("cols", [P, 32])
        conv_k = sb("conv_k", [P, 9])
        conv_c = sb("conv_c", [P, 1])
        tern = sb("tern", [P, 2, 4])
        absum = sb("absum", [P, 2])
        gelu_scale = sb("gelu_scale", [P, 1])
        b1c = sb("b1c", [P, NC])
        carrier = sb("carrier", [P, 1])
        g1c = sb("g1c", [P, KH])
        g2c = sb("g2c", [P, NC])
        a2c = sb("a2c", [P, 1])
        mhalf = sb("mhalf", [P, 2, T])
        kv_acc = sb("kv_acc", [P, KH, VC])
        kv = sb("kv", [P, KH, CC])
        conv = sb("conv", [P, 2 * P])
        y = sb("y", [P, T, D])
        z = sb("z", [P, T, D])
        ssq = sb("ssq", [P, T])
        stA = sb("stA", [P, T, 6])
        mvA = sb("mvA", [P, T, 2])
        smA = sb("smA", [P, 4, T])
        xT_hi = sb("xT_hi", [P, KH, TOK], F16)
        xT_lo = sb("xT_lo", [P, KH, TOK], F16)
        qk = sb("qk", [P, T, 2 * D])
        mx = sb("mx", [P, T, 2 * NH])
        sm = sb("sm", [P, T, 2 * NH])
        rs = sb("rs", [P, T, 2 * NH])
        v = sb("v", [P, T, KH, VC])
        bwork = sb("bwork", [P, 3 * T * D])
        qT, y1, h2 = (bwork[:, j * T * D:(j + 1) * T * D] for j in range(3))
        qT = qT.rearrange("p (h t) -> p h t", h=KH)
        y1 = y1.rearrange("p (t d) -> p t d", t=T)
        h2 = h2.rearrange("p (t d) -> p t d", t=T)
        yT, x2 = qT, y1
        q_now = sb("q_now", [P, T, D])
        rden = sb("rden", [P, T, KH, HH])
        stB = sb("stB", [P, T, 6])
        mvB = sb("mvB", [P, T, 2])
        smB = sb("smB", [P, 2, T])
        x2T_hi = sb("x2T_hi", [P, KH, TOK], F16)
        x2T_lo = sb("x2T_lo", [P, KH, TOK], F16)
        GB, SB, HB = 3, 2, 3
        g = sb("g", [P, GB, TOK])
        sq = sb("sq", [P, SB, TOK])
        g_hi = sb("g_hi", [P, HB, TOK], F16)
        g_lo = sb("g_lo", [P, HB, TOK], F16)
        s12 = sb("s12", [P, 2, TOK])
        res = sb("res", [P, T, D])
        smF = sb("smF", [P, 8, T])

        psA = [ctx.enter_context(nc.psum_tensor(f"psA{i}", [P, 512], F32)) for i in range(2)]
        psB = [ctx.enter_context(nc.psum_tensor(f"psB{i}", [P, 512], F32)) for i in range(2)]
        psF = [ctx.enter_context(nc.psum_tensor(f"psF{i}", [P, 512], F32)) for i in range(2)]
        psO = [ctx.enter_context(nc.psum_tensor(f"psO{i}", [P, 512], F32)) for i in range(2)]

        stage_sems = []

        def stage_sem(name):
            stage_sems.append(sem(name))
            return stage_sems[-1]

        conv_step, proj_done, gelu_done, ssq_done = stage_sem("conv_step"), stage_sem("proj_done"), stage_sem("gelu_done"), stage_sem("ssq_done")
        z_done, normA_step, h_done = stage_sem("z_done"), stage_sem("normA_step"), stage_sem("h_done")
        varA_done, rstdA_done, xn_done, xT_done = stage_sem("varA_done"), stage_sem("rstdA_done"), stage_sem("xn_done"), stage_sem("xT_done")
        xhi_done, xlo_done, qkp_done, vp_done = stage_sem("xhi_done"), stage_sem("xlo_done"), stage_sem("qkp_done"), stage_sem("vp_done")
        max_done, shift_done, exp_done, v_out = stage_sem("max_done"), stage_sem("shift_done"), stage_sem("exp_done"), stage_sem("v_out")
        hsum_done, rs_done, q_done, k_done = stage_sem("hsum_done"), stage_sem("rs_done"), stage_sem("q_done"), stage_sem("k_done")
        ctx_done, acc_done, kv_ready = stage_sem("ctx_done"), stage_sem("acc_done"), stage_sem("kv_ready")
        qT_done, qT_out, qc_done, rden_done = stage_sem("qT_done"), stage_sem("qT_out"), stage_sem("qc_done"), stage_sem("rden_done")
        num_done, y_done, yT_done, yT_out = stage_sem("num_done"), stage_sem("y_done"), stage_sem("yT_done"), stage_sem("yT_out")
        wo_done, h2_done, normB_step = stage_sem("wo_done"), stage_sem("h2_done"), stage_sem("normB_step")
        varB_done, rstdB_done, x2_done = stage_sem("varB_done"), stage_sem("rstdB_done"), stage_sem("x2_done")
        x2T_done, x2hi_done, x2lo_done, res_done = stage_sem("x2T_done"), stage_sem("x2hi_done"), stage_sem("x2lo_done"), stage_sem("res_done")
        f1_done, g_done, ghi_done, glo_done = stage_sem("f1_done"), stage_sem("g_done"), stage_sem("ghi_done"), stage_sem("glo_done")
        sq_done, s1_done, sum_done, f2_done = stage_sem("sq_done"), stage_sem("s1_done"), stage_sem("sum_done"), stage_sem("f2_done")
        st_done, ssum_done, normF_step, varF_done = stage_sem("st_done"), stage_sem("ssum_done"), stage_sem("normF_step"), stage_sem("varF_done")
        rstdF_done, coef_done, u_done, fin_done = stage_sem("rstdF_done"), stage_sem("coef_done"), stage_sem("u_done"), stage_sem("fin_done")

        XB = JT * 2 * C
        xin = h_ring[:, 0:NB * XB].rearrange("p (b j h c) -> p b j h c", b=NB, j=JT, h=2)
        WN = NC * D
        w1n, w2n, t1T, tmp = (q_ring[:, j * WN:(j + 1) * WN] for j in range(4))
        t1T = t1T.rearrange("p (h n) -> p h n", h=KH)
        t2T = qk[:].rearrange("p t n -> p (t n)").rearrange("p (c n) -> p c n", c=NC)
        wn = bwork[:, 0:KH * 3 * D].rearrange("p (h n) -> p h n", h=KH)
        bc = q_ring[:, 3 * WN:3 * WN + (2 * NC + KH) * P].rearrange("p (r n) -> p r n", n=P)
        pn = y[:].rearrange("p t n -> p (t n)")[:, 0:2 * P].rearrange("p (b n) -> p b n", b=2)
        pack = z[:].rearrange("p t n -> p (t n)")[:, 0:P]
        brow = z[:].rearrange("p t n -> p (t n)")[:, P:P + 3 * D]

        x_in = [sem(f"x_in{b}") for b in range(NB)]
        w12_in, wqkv_in, small_in, rows_in = sem("w12_in"), sem("wqkv_in"), sem("small_in"), sem("rows_in")
        cleared, const_step, consts, pad_clear = sem("cleared"), sem("const_step"), sem("consts"), sem("pad_clear")
        abs_done, tot_done, ternary, prep_step = sem("abs_done"), sem("tot_done"), sem("ternary"), sem("prep_step")
        tr_done, tr_out, x_tr, x_out, halo = sem("tr_done"), sem("tr_out"), sem("x_tr"), sem("x_out"), sem("halo")
        col_done, col_out, pj_done, pj_out = sem("col_done"), sem("col_out"), sem("pj_done"), sem("pj_out")
        bc_ready, sums_done, hi_done = sem("bc_ready"), sem("sums_done"), sem("hi_done")

        GCOL, BCOL, B1COL, G2COL, B2COL, BVCOL = 0, KH, 2 * KH, 2 * KH + NC, 2 * KH + 2 * NC, 2 * KH + 3 * NC
        with nc.Block() as block:

            @block.sync
            def _(sp):
                for s in stage_sems:
                    sp.sem_inc(s, START)
                sp.dma_start(w1n.rearrange("p (c d) -> p c d", c=NC), w1.rearrange("(c p) d -> p c d", p=P)).then_inc(w12_in, 16)
                sp.dma_start(w2n.rearrange("p (c d) -> p c d", c=KH), w2.rearrange("(c p) d -> p c d", p=P)).then_inc(w12_in, 16)
                for b in range(NB):
                    for half in range(2):
                        rows = x[b, half * HR:(half + 1) * HR, :, :].rearrange("r w c -> (r w) c")
                        sp.dma_start(xin[:, b, :, half, :], rows.rearrange("(p j) c -> p j c", j=JT)).then_inc(x_in[b], 16)

            @block.scalar
            def _(act):
                act.wait_ge(cleared, 1)
                for row, src in ((GCOL, ln1_g), (BCOL, ln1_b), (B1COL, b1), (G2COL, ln2_g), (B2COL, ln2_b), (BVCOL, bv)):
                    n = src.shape[0] // P
                    act.dma_start(pack[row:row + n, :], src.rearrange("(r n) -> r n", n=P)).then_inc(rows_in, 16)
                for part in (0, 32):
                    for col, src in ((0, bq), (D, bk), (2 * D, proj_b)):
                        act.dma_start(brow[part:part + 1, col:col + D], src.rearrange("(a n) -> a n", a=1)).then_inc(rows_in, 16)
                for i, src in enumerate((Wq, Wk, Wv)):
                    act.dma_start(wn[:, :, i * D:(i + 1) * D], src.rearrange("(h p) n -> p h n", p=P)).then_inc(wqkv_in, 16)
                act.dma_start(wo[:], Wo.rearrange("(h p) n -> p h n", p=P)).then_inc(wqkv_in, 16)
                for rep in range(2):
                    act.dma_start(pn[:, :, rep * C:(rep + 1) * C], proj_w.rearrange("(b p) c -> p b c", p=P)).then_inc(small_in, 16)
                    act.dma_start(conv_k[rep * C:(rep + 1) * C, :], conv_w.rearrange("c o a b -> c (o a b)")).then_inc(small_in, 16)
                    act.dma_start(conv_c[rep * C:(rep + 1) * C, :], conv_b.rearrange("(c o) -> c o", o=1)).then_inc(small_in, 16)
                for dst, src in ((norm_bc, norm_w), (bo_bc, bo), (b2_bc, b2)):
                    act.dma_start(dst[:], 
                                  src.rearrange("(a n) -> a n", a=1).to_broadcast([P, D])).then_inc(small_in, 16)
                act.wait_ge(pad_clear, 1)
                for b in range(NB):
                    for u in range(JT // 4):
                        n = b * (JT // 4) + u
                        act.wait_ge(x_tr, n + 1)
                        dst = xpad[:, b * XP:(b + 1) * XP].rearrange("p (r w) -> p r w", w=PW)[:, 1:HR + 1, 1:PW - 1]
                        dst = dst.rearrange("p r (q j) -> p r q j", j=JT)
                        src = psB[n % 2][:].rearrange("p (j r q) -> p j r q", j=4, q=P // HR)
                        for j in range(4):
                            ins = nc.scalar.activation(dst[:, :, :, 4 * u + j], src[:, j, :, :], ACT.Copy)
                        ins.then_inc(x_out, 1)

            @block.gpsimd
            def _(pool):
                nc.gpsimd.memset(z[:], 0.0).then_inc(cleared, 1)
                nc.gpsimd.memset(xpad[:], 0.0).then_inc(pad_clear, 1)
                nc.gpsimd.memset(ones[:], 1.0).then_inc(const_step, 1)
                nc.gpsimd.memset(ident[:], 0.0).then_inc(const_step, 1)
                nc.gpsimd.memset(mask[:], 1.0).then_inc(const_step, 1)
                nc.gpsimd.memset(mhalf[:], -0.5).then_inc(const_step, 1)
                nc.gpsimd.memset(kv_acc[:], 0.0).then_inc(const_step, 1)
                nc.gpsimd.memset(v[:], 1.0).then_inc(const_step, 1)
                nc.gpsimd.memset(ones_rows[:], 0.0).then_inc(const_step, 1)
                nc.gpsimd.memset(qk_bias[:], 0.0).then_inc(const_step, 1)
                nc.gpsimd.memset(proj_bias[:], 0.0).then_inc(const_step, 1)
                nc.gpsimd.memset(proj[:], 0.0).then_inc(const_step, 1)
                pool.wait_ge(const_step, 10)
                nc.gpsimd.affine_select(out=ident[:], in_=ident[:], compare_op=ALU.not_equal, fill=1.0, base=0,
                                        pattern=[[-1, P]], channel_multiplier=1).then_inc(const_step, 1)
                m = mask[:].rearrange("p (b i) -> p b i", i=16)
                nc.gpsimd.affine_select(out=m, in_=m, compare_op=ALU.is_ge, fill=0.0, base=0,
                                        pattern=[[-16, 8], [0, 16]], channel_multiplier=1).then_inc(const_step, 1)
                pool.wait_ge(const_step, 12)
                nc.gpsimd.affine_select(out=m, in_=m, compare_op=ALU.is_ge, fill=0.0, base=15,
                                        pattern=[[16, 8], [0, 16]], channel_multiplier=-1).then_inc(const_step, 1)
                pool.wait_ge(const_step, 13)
                nc.gpsimd.memset(smA[:], 0.0).then_inc(consts, 1)

            @block.vector
            def _(dve):
                steps = [0]

                def step(ins):
                    steps[0] += 1
                    ins.then_inc(prep_step, 1)
                    dve.wait_ge(prep_step, steps[0])

                dve.wait_ge(w12_in, 32)
                nc.vector.tensor_reduce(absum[:, 0:1], w1n, AX.X, ALU.add, apply_absolute_value=True)
                nc.vector.tensor_reduce(absum[:, 1:2], w2n, AX.X, ALU.add, apply_absolute_value=True).then_inc(abs_done, 1)
                dve.wait_ge(tot_done, 1)
                step(nc.vector.tensor_scalar(tern[:, :, 0], psA[0][:, 0:2], 1.0 / (D * HID), 1e-5, ALU.mult, ALU.max))
                step(nc.vector.reciprocal(tern[:, :, 1], tern[:, :, 0]))
                step(nc.vector.reciprocal(tern[:, :, 2], tern[:, :, 1]))
                step(nc.vector.tensor_scalar(gelu_scale[:], tern[:, 0, 2:3], 1.0 / XS, None, ALU.mult))
                step(nc.vector.tensor_scalar(a2c[:], tern[:, 1, 2:3], 1.0 / XS, None, ALU.mult))
                for i, w in enumerate((w1n, w2n)):
                    step(nc.vector.tensor_scalar(tmp, w, tern[:, i, 1:2], 0.5, ALU.mult, ALU.is_gt))
                    step(nc.vector.tensor_scalar(w, w, tern[:, i, 1:2], -0.5, ALU.mult, ALU.is_lt))
                    step(nc.vector.tensor_tensor(w, tmp, w, ALU.subtract))
                    nc.vector.memset(absum[:, i:i + 1], 0.0).then_inc(ternary, 1)
                dve.wait_ge(col_done, 1)
                step(nc.vector.tensor_copy(cols[:, 0:32], psA[1][:, 0:32]))
                nc.vector.tensor_scalar(g1c[:], cols[:, GCOL:GCOL + KH], XS, None, ALU.mult)
                step(nc.vector.tensor_scalar(g2c[:], cols[:, G2COL:G2COL + NC], XS, None, ALU.mult))
                dve.wait_ge(consts, 1)
                for part in (0, 32):
                    nc.vector.memset(ones_rows[part:part + 1, :], BROW)
                for r in range(2 * NC + KH):
                    ins = nc.vector.tensor_scalar(bc[:, r, :], ones[:], cols[:, G2COL + r:G2COL + r + 1], None, ALU.mult)
                ins.then_inc(bc_ready, 1)
                for n in range(2 * NC * KH // 4):
                    dve.wait_ge(tr_done, n + 1)
                    if n < NC * KH // 4:
                        h, q = n // 2, n % 2
                        dst, dst32 = w1T[h][:, q * 512:(q + 1) * 512], t1T[:, h, q * 512:(q + 1) * 512]
                    else:
                        h, q = divmod(n - NC * KH // 4, 2)
                        dst, dst32 = w2T[:, 4 * q:4 * q + 4, h * P:(h + 1) * P], t2T[:, 4 * q:4 * q + 4, h * P:(h + 1) * P]
                    src = psF[n % 2][:] if n < NC * KH // 4 else psF[n % 2][:].rearrange("p (c n) -> p c n", c=4)
                    nc.vector.tensor_copy(dst, src)
                    nc.vector.tensor_copy(dst32, src).then_inc(tr_out, 1)
                dve.wait_ge(wqkv_in, 64)
                nc.vector.tensor_scalar(wqkv_hi[:], wn, WS, None, ALU.mult).then_inc(hi_done, 1)
                dve.wait_ge(hi_done, 1)
                nc.vector.scalar_tensor_tensor(wqkv_lo[:], wn, WS, wqkv_hi[:], ALU.mult, ALU.subtract)
                dve.wait_ge(rows_in, 16 * 12)
                for dst, src in ((qk_bias, brow[:, 0:2 * D]), (proj_bias, brow[:, 2 * D:3 * D])):
                    nc.vector.tensor_scalar(dst[0:1, :], src[0:1, :], BROW, None, ALU.mult)
                    step(nc.vector.tensor_scalar(dst[32:33, :], src[32:33, :], BROW, None, ALU.mult))
                    step(nc.vector.scalar_tensor_tensor(dst[32:33, :], src[32:33, :], BROW, dst[32:33, :], ALU.mult, ALU.subtract))
                dve.wait_ge(small_in, 16 * 9)
                dve.wait_ge(pj_done, 1)
                for half in range(2):
                    rows = slice(half * C, (half + 1) * C)
                    nc.vector.tensor_scalar(proj[rows, half, :], psO[0][rows, 0:D], QS, None, ALU.mult)
                dve.wait_ge(sums_done, 1)
                nc.vector.tensor_scalar(g2w_bc[:], psA[0][:, 0:D], tern[:, 1, 2:3], None, ALU.mult)
                nc.vector.scalar_tensor_tensor(b2_bc[:], psA[1][:, 0:D], tern[:, 1, 2:3], b2_bc[:], ALU.mult, ALU.add)
                nc.vector.scalar_tensor_tensor(b1c[:], psF[0][:, 0:NC], tern[:, 0, 2:3], cols[:, B1COL:B1COL + NC],
                                               ALU.mult, ALU.add)
                nc.vector.tensor_tensor(bo_bc[:], psO[1][:, 0:D], bo_bc[:], ALU.add)
                dve.wait_ge(x_out, NB * JT // 4)
                for b in range(NB):
                    img = xpad[:, b * XP:(b + 1) * XP].rearrange("p (r w) -> p r w", w=PW)
                    nc.vector.tensor_copy(img[0:C, HR + 1, :], img[C:2 * C, 1, :])
                    nc.vector.tensor_copy(img[C:2 * C, 0, :], img[0:C, HR, :])

            @block.tensor
            def _(pe):
                pe.wait_ge(consts, 1)
                pe.wait_ge(abs_done, 1)
                nc.tensor.matmul(psA[0][:, 0:2], ones[:], absum[:], start=True, stop=True).then_inc(tot_done, 1)
                pe.wait_ge(rows_in, 16 * 12)
                nc.tensor.transpose(psA[1][:, 0:P], pack, ident[:]).then_inc(col_done, 1)
                for b in range(NB):
                    pe.wait_ge(x_in[b], 32)
                    for u in range(JT // 4):
                        n = b * (JT // 4) + u
                        if n >= 2:
                            pe.wait_ge(x_out, n - 1)
                        for j in range(4):
                            ins = nc.tensor.transpose(psB[n % 2][:, j * P:(j + 1) * P], xin[:, b, 4 * u + j, :, :], ident[:])
                        ins.then_inc(x_tr, 1)
                for n in range(2 * NC * KH // 4):
                    if n >= 2:
                        pe.wait_ge(tr_out, n - 1)
                    if n < NC * KH // 4:
                        pe.wait_ge(ternary, 1)
                        h, q = n // 2, n % 2
                        blocks = [w1n[:, (4 * q + c) * D + h * P:(4 * q + c) * D + (h + 1) * P] for c in range(4)]
                    else:
                        pe.wait_ge(ternary, 2)
                        h, q = divmod(n - NC * KH // 4, 2)
                        blocks = [w2n[:, h * HID + (4 * q + c) * P:h * HID + (4 * q + c + 1) * P] for c in range(4)]
                    for c, block_ in enumerate(blocks):
                        ins = nc.tensor.transpose(psF[n % 2][:, c * P:(c + 1) * P], block_, ident[:])
                    ins.then_inc(tr_done, 1)
                pe.wait_ge(small_in, 16 * 9)
                for b in range(2):
                    ins = nc.tensor.transpose(psO[0][:, b * P:(b + 1) * P], pn[:, b, :], ident[:])
                ins.then_inc(pj_done, 1)
                pe.wait_ge(bc_ready, 1)
                pe.wait_ge(tr_out, 2 * NC * KH // 4)
                for i in range(2):
                    for c in range(NC):
                        nc.tensor.matmul(psA[i][:, 0:D], bc[:, i * NC + c, :], t2T[:, c, :], start=(c == 0), stop=(c == NC - 1))
                pe.wait_ge(wqkv_in, 64)
                for h in range(KH):
                    nc.tensor.matmul(psO[1][:, 0:D], bc[:, 2 * NC + h, :], wo[:, h, :], start=(h == 0), stop=(h == KH - 1))
                for c in range(NC):
                    for h in range(KH):
                        ins = nc.tensor.matmul(psF[0][:, c:c + 1], t1T[:, h, c * P:(c + 1) * P], cols[:, BCOL + h:BCOL + h + 1],
                                               start=(h == 0), stop=(h == KH - 1))
                ins.then_inc(sums_done, 1)

        q_in, stored = sem("q_in"), sem("stored")

        LAG = GI + 1

        BANKS = {
            "transpose_x 0": (psA[0], acc_done, 1, 0),
            "transpose_x 1": (psA[1], ssq_done, 1, 1),
            "project_qk 0": (psA[0], xlo_done, 2, 1),
            "project_qk 1": (psA[1], xlo_done, 2, 2),
            "project_v 0": (psA[0], shift_done, 4, 1),
            "project_qk 2": (psA[1], shift_done, 4, 2),
            "project_v 1": (psA[0], v_out, 2, 1),
            "project_qk 3": (psA[1], shift_done, 4, 3),
            "project 0": (psA[0], v_out, 2, 0),
            "project 1": (psA[1], shift_done, 4, 0),
            "keys_values": (psA[0], ssq_done, 1, 2),
            "transpose_q 0": (psB[0], x2lo_done, 2, -1),
            "transpose_q 1": (psB[1], x2lo_done, 2, 0),
            "attend 0": (psB[0], qT_out, 2, 1),
            "attend 1": (psB[1], qT_out, 2, 2),
            "attend 2": (psB[0], num_done, 4, 1),
            "attend 3": (psB[1], num_done, 4, 2),
            "transpose_y 0": (psB[0], num_done, 4, 3),
            "transpose_y 1": (psB[1], num_done, 4, 4),
            "output_product 0": (psB[0], yT_out, 2, 1),
            "output_product 1": (psB[1], yT_out, 2, 2),
            "transpose_x2 0": (psB[0], h2_done, 2, 1),
            "transpose_x2 1": (psB[1], h2_done, 2, 2),
            "up 0": (psF[0], ssum_done, 2, -1),
            "up 1": (psF[1], ssum_done, 2, 0),
            "up 2": (psF[0], g_done, 8, 1),
            "up 3": (psF[1], g_done, 8, 2),
            "up 4": (psF[0], g_done, 8, 3),
            "up 5": (psF[1], g_done, 8, 4),
            "up 6": (psF[0], g_done, 8, 5),
            "up 7": (psF[1], g_done, 8, 6),
            "transpose_sums 0": (psF[0], g_done, 8, 7),
            "transpose_sums 1": (psF[1], g_done, 8, 8),
        }
        bank_of = {use: entry[0] for use, entry in BANKS.items()}

        def slot(ring, n):
            return ring[:, bass.ds((n % RING) * (T * D), T * D)].rearrange("p (t d) -> p t d", t=T)

        def per_head(ap, j):
            return ap[:, 2 * j:2 * j + 2, :].unsqueeze(3).to_broadcast([P, 2, ap.shape[2], HD])

        def before(ring, c):
            return c - ring if c >= ring else max(k for k in range(NC) if k % ring == c % ring) - NC

        def group_loops(eng, first_A, only_A, close_image, A_and_B, all_stages, B_and_F, only_F):
            first_A(0)
            with eng.Fori(0, GI) as n:
                only_A(n)
            close_image(0)
            A_and_B(-1)
            with eng.Fori(0, NB - 1) as k:
                with eng.Fori((k * (2 * GI - 1)) // 2, k * GI + GI - 1) as m:
                    all_stages(m)
                close_image(k + 1)
            with eng.Fori(NG - LAG, NG - 1) as m:
                B_and_F(m)
            only_F(NG - 1)

        with nc.Block() as block:

            @block.sync
            def _(sp):
                rows = out.rearrange("b n d -> (b n) d")

                def stage_q(m):
                    if isinstance(m, int):
                        sp.wait_ge(q_done, START + 2)
                    else:
                        sp.wait_ge(qT_done, START + 2 * m)
                        sp.wait_ge(y_done, START + 2 * m)
                    sp.dma_start(q_now[:], slot(q_ring, m)).then_inc(q_in, 16)

                def store(m):
                    firsts = [(m // GI) * (H * W) + (m % GI) * (2 * P) + half * (H * W // 2) for half in range(2)]
                    sp.wait_ge(fin_done, START + T * m + T)
                    for half, first in enumerate(firsts):
                        dst = rows[bass.ds(first, 2 * P), :].rearrange("(t p) d -> p t d", p=P)
                        sp.dma_start(dst, res[:, 2 * half:2 * half + 2, :]).then_inc(stored, 16)

                stage_q(0)
                with sp.Fori(0, NG - 1) as m:
                    stage_q(m + 1)
                    store(m)
                store(NG - 1)
                sp.wait_ge(stored, 32 * NG)

            @block.tensor
            def _(pe):
                mm, tr = nc.tensor.matmul, nc.tensor.transpose

                def bank(use, n):
                    ps, released, per_group, count = BANKS[use]
                    pe.wait_ge(released, START + per_group * n + count)
                    return ps

                def project(n, j):
                    if j == 0:
                        pe.wait_ge(conv_step, START + 9 * n + 9)
                    ps = bank(f"project {j}", n)
                    for u in range(2):
                        dst = ps[:, u * D:(u + 1) * D]
                        mm(dst, conv[:, u * P:(u + 1) * P], proj[:, j, :], start=(u == 0), stop=False, skip_group_check=True)
                        ins = mm(dst, ones_rows[:], proj_bias[:], start=False, stop=True, skip_group_check=True)
                    ins.then_inc(proj_done, 1)

                def transpose_x(n, h):
                    if h == 0:
                        pe.wait_ge(xn_done, START + n + 1)
                    ps = bank(f"transpose_x {h}", n)
                    for t in range(T):
                        ins = tr(ps[:, t * P:(t + 1) * P], y[:, t, h * P:(h + 1) * P], ident[:])
                    ins.then_inc(xT_done, 1)

                def split_product(dst, t, cols_, first, last):
                    tok = slice(t * P, (t + 1) * P)
                    parts = [(h, xa, wa) for h in range(KH)
                             for xa, wa in ((xT_hi, wqkv_hi), (xT_hi, wqkv_lo), (xT_lo, wqkv_hi))]
                    for k, (h, xa, wa) in enumerate(parts):
                        ins = mm(dst, xa[:, h, tok], wa[:, h, cols_], start=(first and k == 0),
                                 stop=(last and k == len(parts) - 1), skip_group_check=True)
                    return ins

                def project_qk(n, t):
                    if t == 0:
                        pe.wait_ge(xlo_done, START + 2 * n + 2)
                    ps = bank(f"project_qk {t}", n)
                    split_product(ps[:], t, slice(0, 2 * D), True, False)
                    mm(ps[:], ones_rows[:], qk_bias[:], start=False, stop=True, skip_group_check=True).then_inc(qkp_done, 1)

                def project_v(n, j):
                    ps = bank(f"project_v {j}", n)
                    for u in range(2):
                        ins = split_product(ps[:, u * D:(u + 1) * D], 2 * j + u, slice(2 * D, 3 * D), u == 0, True)
                    ins.then_inc(vp_done, 1)

                def keys_values(n):
                    pe.wait_ge(k_done, START + 2 * n + 2)
                    pe.wait_ge(v_out, START + 2 * n + 2)
                    ps = bank("keys_values", n)
                    for t in range(T):
                        for h in range(KH):
                            ins = mm(ps[:, h * VC:(h + 1) * VC], qk[:, t, D + h * P:D + (h + 1) * P], v[:, t, h, :],
                                     start=(t == 0 and h == 0), stop=(t == T - 1), skip_group_check=True)
                    ins.then_inc(ctx_done, 1)

                def transpose_q(m, h):
                    if h == 0:
                        pe.wait_ge(q_in, 16 * m + 16)
                    ps = bank(f"transpose_q {h}", m)
                    for t in range(T):
                        ins = tr(ps[:, t * P:(t + 1) * P], q_now[:, t, h * P:(h + 1) * P], ident[:])
                    ins.then_inc(qT_done, 1)

                def attend(m, t):
                    if t == 0:
                        pe.wait_ge(qT_out, START + 2 * m + 2)
                        pe.wait_ge(kv_ready, START + m // GI + 1)
                    ps = bank(f"attend {t}", m)
                    for h in range(KH):
                        ins = mm(ps[:, h * CC:(h + 1) * CC], qT[:, h, t * P:(t + 1) * P], kv[:, h, :],
                                 start=(h == 0), stop=True, skip_group_check=True)
                    ins.then_inc(qc_done, 1)

                def transpose_y(m, h):
                    if h == 0:
                        pe.wait_ge(y_done, START + 2 * m + 2)
                    ps = bank(f"transpose_y {h}", m)
                    for t in range(T):
                        ins = tr(ps[:, t * P:(t + 1) * P], y1[:, t, h * P:(h + 1) * P], ident[:])
                    ins.then_inc(yT_done, 1)

                def output_product(m, j):
                    if j == 0:
                        pe.wait_ge(yT_out, START + 2 * m + 2)
                    ps = bank(f"output_product {j}", m)
                    for u in range(2):
                        t = 2 * j + u
                        for h in range(KH):
                            ins = mm(ps[:, u * D:(u + 1) * D], yT[:, h, t * P:(t + 1) * P], wo[:, h, :],
                                     start=(u == 0 and h == 0), stop=(h == KH - 1), skip_group_check=True)
                    ins.then_inc(wo_done, 1)

                def transpose_x2(m, h):
                    if h == 0:
                        pe.wait_ge(x2_done, START + m + 1)
                    ps = bank(f"transpose_x2 {h}", m)
                    for t in range(T):
                        ins = tr(ps[:, t * P:(t + 1) * P], x2[:, t, h * P:(h + 1) * P], ident[:])
                    ins.then_inc(x2T_done, 1)

                def up(m, c):
                    if c == 0:
                        pe.wait_ge(x2lo_done, START + 2 * m + 2)
                    ps = bank(f"up {c}", m)
                    parts = [(h, xa) for h in range(KH) for xa in (x2T_hi, x2T_lo)]
                    for k, (h, xa) in enumerate(parts):
                        ins = mm(ps[:], w1T[h][:, c * P:(c + 1) * P], xa[:, h, :], start=(k == 0), stop=(k == len(parts) - 1))
                    ins.then_inc(f1_done, 1)

                def down(m, c):
                    if c == 0:
                        pe.wait_ge(u_done, START + T * m)
                    pe.wait_ge(glo_done, START + NC * m + c + 1)
                    for t in range(T):
                        for ga in (g_hi, g_lo):
                            ins = mm(psO[t // 2][:, (t % 2) * D:(t % 2 + 1) * D], ga[:, c % HB, t * P:(t + 1) * P], w2T[:, c, :],
                                     start=(c == 0 and t % 2 == 0 and ga is g_hi), stop=(c == NC - 1 and ga is g_lo),
                                     skip_group_check=True)
                    ins.then_inc(f2_done, 1)

                def transpose_sums(m, i):
                    if i == 0:
                        pe.wait_ge(sum_done, START + 7 * m + 7)
                    ps = bank(f"transpose_sums {i}", m)
                    for t in range(T):
                        ins = tr(ps[:, t * P:(t + 1) * P], s12[:, i, t * P:(t + 1) * P], ident[:])
                    ins.then_inc(st_done, 1)

                def first_A(a):
                    project(a, 0)
                    project(a, 1)

                def only_A(n):
                    a = n + 1
                    transpose_x(n, 0)
                    transpose_x(n, 1)
                    project_qk(n, 0)
                    project_qk(n, 1)
                    project_v(n, 0)
                    project_qk(n, 2)
                    project_v(n, 1)
                    project_qk(n, 3)
                    project(a, 0)
                    project(a, 1)
                    keys_values(n)

                def A_and_B(m):
                    n, a, b = m + LAG, m + LAG + 1, m + 1
                    transpose_x(n, 0)
                    transpose_x(n, 1)
                    project_qk(n, 0)
                    project_qk(n, 1)
                    transpose_q(b, 0)
                    transpose_q(b, 1)
                    project_v(n, 0)
                    for i in range(0, 4):
                        attend(b, i)
                    project_qk(n, 2)
                    project_v(n, 1)
                    transpose_y(b, 0)
                    transpose_y(b, 1)
                    project_qk(n, 3)
                    output_product(b, 0)
                    output_product(b, 1)
                    project(a, 0)
                    project(a, 1)
                    transpose_x2(b, 0)
                    transpose_x2(b, 1)
                    keys_values(n)

                def all_stages(m):
                    n, a, b = m + LAG, m + LAG + 1, m + 1
                    for i in range(0, 5):
                        up(m, i)
                    transpose_x(n, 0)
                    transpose_x(n, 1)
                    down(m, 0)
                    down(m, 1)
                    project_qk(n, 0)
                    project_qk(n, 1)
                    transpose_q(b, 0)
                    transpose_q(b, 1)
                    project_v(n, 0)
                    up(m, 5)
                    attend(b, 0)
                    attend(b, 1)
                    up(m, 6)
                    attend(b, 2)
                    attend(b, 3)
                    project_qk(n, 2)
                    project_v(n, 1)
                    transpose_y(b, 0)
                    transpose_y(b, 1)
                    project_qk(n, 3)
                    output_product(b, 0)
                    output_product(b, 1)
                    up(m, 7)
                    down(m, 2)
                    down(m, 3)
                    project(a, 0)
                    project(a, 1)
                    down(m, 4)
                    transpose_x2(b, 0)
                    transpose_x2(b, 1)
                    transpose_sums(m, 0)
                    transpose_sums(m, 1)
                    for i in range(5, 8):
                        down(m, i)
                    keys_values(n)

                def B_and_F(m):
                    b = m + 1
                    for i in range(0, 4):
                        up(m, i)
                    down(m, 0)
                    up(m, 4)
                    transpose_q(b, 0)
                    transpose_q(b, 1)
                    down(m, 1)
                    up(m, 5)
                    attend(b, 0)
                    attend(b, 1)
                    up(m, 6)
                    attend(b, 2)
                    attend(b, 3)
                    down(m, 2)
                    transpose_y(b, 0)
                    transpose_y(b, 1)
                    down(m, 3)
                    output_product(b, 0)
                    output_product(b, 1)
                    down(m, 4)
                    up(m, 7)
                    down(m, 5)
                    down(m, 6)
                    transpose_x2(b, 0)
                    transpose_x2(b, 1)
                    transpose_sums(m, 0)
                    transpose_sums(m, 1)
                    down(m, 7)

                def only_F(m):
                    for i in range(0, 5):
                        up(m, i)
                    down(m, 0)
                    down(m, 1)
                    for i in range(5, 8):
                        up(m, i)
                    for i in range(2, 5):
                        down(m, i)
                    transpose_sums(m, 0)
                    transpose_sums(m, 1)
                    for i in range(5, 8):
                        down(m, i)

                group_loops(pe, first_A, only_A, lambda k: None, A_and_B, all_stages, B_and_F, only_F)

            @block.scalar
            def _(act):
                fn = nc.scalar.activation

                def gelu_y(n, j):
                    if j == 0:
                        act.wait_ge(xT_done, START + 2 * n)
                    act.wait_ge(proj_done, START + 2 * n + j + 1)
                    fn(y[:, 2 * j:2 * j + 2, :], bank_of["project %d" % j][:].rearrange("p (t d) -> p t d", t=2), ACT.Gelu,
                       scale=1.0 / QS).then_inc(gelu_done, 1)

                def square_y(n):
                    act.wait_ge(gelu_done, START + 2 * n + 2)
                    act.wait_ge(xn_done, START + n)
                    for t in range(T):
                        ins = fn(bank_of["project %d" % (t // 2)][:, (t % 2) * D:(t % 2 + 1) * D], y[:, t, :], ACT.Square,
                                 accum_out=ssq[:, t:t + 1])
                    ins.then_inc(ssq_done, 1)

                def high_x(n, h):
                    if h == 0:
                        act.wait_ge(vp_done, START + 2 * n)
                        act.wait_ge(qkp_done, START + 4 * n)
                    act.wait_ge(xT_done, START + 2 * n + h + 1)
                    fn(xT_hi[:, h, :], bank_of["transpose_x %d" % h][:], ACT.Copy, scale=XS).then_inc(xhi_done, 1)

                def take_v(n, j):
                    if j == 0:
                        act.wait_ge(ctx_done, START + n)
                    act.wait_ge(vp_done, START + 2 * n + j + 1)
                    fn(v[:, 2 * j:2 * j + 2, :, 0:P], bank_of["project_v %d" % j][:].rearrange("p (t h d) -> p t h d", t=2, h=KH),
                       ACT.Copy, scale=1.0 / QS).then_inc(v_out, 1)

                def exps(n, j):
                    act.wait_ge(shift_done, START + 4 * n + 2 * j + 2)
                    fn(qk[:, 2 * j:2 * j + 2, :], qk[:, 2 * j:2 * j + 2, :], ACT.Exp, scale=1.0 / QS).then_inc(exp_done, 1)

                def take_qT(m, h):
                    if h == 0:
                        act.wait_ge(wo_done, START + 2 * m)
                    act.wait_ge(qT_done, START + 2 * m + h + 1)
                    fn(qT[:, h, :], bank_of["transpose_q %d" % h][:], ACT.Copy).then_inc(qT_out, 1)

                def take_yT(m, h):
                    if h == 0:
                        act.wait_ge(qc_done, START + 4 * m + 4)
                    act.wait_ge(yT_done, START + 2 * m + h + 1)
                    fn(yT[:, h, :], bank_of["transpose_y %d" % h][:], ACT.Copy).then_inc(yT_out, 1)

                def high_x2(m, h):
                    if h == 0:
                        act.wait_ge(f1_done, START + NC * m)
                    act.wait_ge(x2T_done, START + 2 * m + h + 1)
                    fn(x2T_hi[:, h, :], bank_of["transpose_x2 %d" % h][:], ACT.Copy, scale=g1c[:, h:h + 1]).then_inc(x2hi_done, 1)

                def gelu_g(m, c):
                    act.wait_ge(f1_done, START + NC * m + c + 1)
                    last = before(GB, c)
                    act.wait_ge(glo_done, START + NC * m + last + 1)
                    act.wait_ge(sum_done, START + 7 * m + (max(last, 1) if last >= 0 else last + 1))
                    fn(g[:, c % GB, :], bank_of["up %d" % c][:], ACT.Gelu, scale=gelu_scale[:], bias=b1c[:, c:c + 1]).then_inc(g_done, 1)

                def high_g(m, c):
                    act.wait_ge(f2_done, START + NC * m + before(HB, c) + 1)
                    act.wait_ge(g_done, START + NC * m + c + 1)
                    fn(g_hi[:, c % HB, :], g[:, c % GB, :], ACT.Copy, scale=g2c[:, c:c + 1]).then_inc(ghi_done, 1)

                def square_g(m, c):
                    last = before(SB, c)
                    act.wait_ge(sum_done, START + 7 * m + (max(last, 1) if last >= 0 else last + 1))
                    act.wait_ge(g_done, START + NC * m + c + 1)
                    fn(sq[:, c % SB, :], g[:, c % GB, :], ACT.Square).then_inc(sq_done, 1)

                def first_A(a):
                    gelu_y(a, 0)
                    gelu_y(a, 1)
                    square_y(a)

                def only_A(n):
                    a = n + 1
                    high_x(n, 0)
                    high_x(n, 1)
                    take_v(n, 0)
                    exps(n, 0)
                    take_v(n, 1)
                    exps(n, 1)
                    gelu_y(a, 0)
                    gelu_y(a, 1)
                    square_y(a)

                def A_and_B(m):
                    n, a, b = m + LAG, m + LAG + 1, m + 1
                    high_x(n, 0)
                    high_x(n, 1)
                    take_qT(b, 0)
                    take_qT(b, 1)
                    take_v(n, 0)
                    exps(n, 0)
                    take_yT(b, 0)
                    take_yT(b, 1)
                    take_v(n, 1)
                    exps(n, 1)
                    gelu_y(a, 0)
                    gelu_y(a, 1)
                    square_y(a)
                    high_x2(b, 0)
                    high_x2(b, 1)

                def all_stages(m):
                    n, a, b = m + LAG, m + LAG + 1, m + 1
                    gelu_g(m, 0)
                    high_g(m, 0)
                    gelu_g(m, 1)
                    gelu_g(m, 2)
                    high_g(m, 1)
                    high_g(m, 2)
                    square_g(m, 0)
                    square_g(m, 1)
                    high_x(n, 0)
                    high_x(n, 1)
                    square_g(m, 2)
                    gelu_g(m, 3)
                    square_g(m, 3)
                    take_qT(b, 0)
                    take_qT(b, 1)
                    gelu_g(m, 4)
                    gelu_g(m, 5)
                    square_g(m, 4)
                    high_g(m, 3)
                    take_v(n, 0)
                    high_g(m, 4)
                    exps(n, 0)
                    square_g(m, 5)
                    take_yT(b, 0)
                    take_yT(b, 1)
                    take_v(n, 1)
                    gelu_g(m, 6)
                    square_g(m, 6)
                    exps(n, 1)
                    gelu_g(m, 7)
                    square_g(m, 7)
                    gelu_y(a, 0)
                    high_g(m, 5)
                    high_g(m, 6)
                    gelu_y(a, 1)
                    high_g(m, 7)
                    square_y(a)
                    high_x2(b, 0)
                    high_x2(b, 1)

                def B_and_F(m):
                    b = m + 1
                    gelu_g(m, 0)
                    square_g(m, 0)
                    gelu_g(m, 1)
                    high_g(m, 0)
                    gelu_g(m, 2)
                    high_g(m, 1)
                    square_g(m, 1)
                    high_g(m, 2)
                    take_qT(b, 0)
                    gelu_g(m, 3)
                    take_qT(b, 1)
                    square_g(m, 2)
                    gelu_g(m, 4)
                    high_g(m, 3)
                    high_g(m, 4)
                    square_g(m, 3)
                    gelu_g(m, 5)
                    square_g(m, 4)
                    take_yT(b, 0)
                    take_yT(b, 1)
                    high_g(m, 5)
                    square_g(m, 5)
                    gelu_g(m, 6)
                    square_g(m, 6)
                    high_g(m, 6)
                    gelu_g(m, 7)
                    high_g(m, 7)
                    square_g(m, 7)
                    high_x2(b, 0)
                    high_x2(b, 1)

                def only_F(m):
                    gelu_g(m, 0)
                    high_g(m, 0)
                    gelu_g(m, 1)
                    gelu_g(m, 2)
                    high_g(m, 1)
                    high_g(m, 2)
                    for i in range(0, 3):
                        square_g(m, i)
                    gelu_g(m, 3)
                    square_g(m, 3)
                    gelu_g(m, 4)
                    gelu_g(m, 5)
                    square_g(m, 4)
                    high_g(m, 3)
                    high_g(m, 4)
                    square_g(m, 5)
                    gelu_g(m, 6)
                    square_g(m, 6)
                    gelu_g(m, 7)
                    square_g(m, 7)
                    for i in range(5, 8):
                        high_g(m, i)

                group_loops(act, first_A, only_A, lambda k: None, A_and_B, all_stages, B_and_F, only_F)

            @block.gpsimd
            def _(pool):
                tt = nc.gpsimd.tensor_tensor

                def weigh(n, j):
                    if j == 0:
                        pool.wait_ge(xn_done, START + n)
                        pool.wait_ge(h_done, START + n)
                    pool.wait_ge(gelu_done, START + 2 * n + j + 1)
                    tt(z[:, 2 * j:2 * j + 2, :], y[:, 2 * j:2 * j + 2, :], norm_bc[:].unsqueeze(1).to_broadcast([P, 2, D]),
                       ALU.mult).then_inc(z_done, 1)

                def powers_z(n):
                    pool.wait_ge(varA_done, START + n + 1)
                    tt(smA[:, 2:4, :], smA[:, 0:2, :], mhalf[:], ALU.pow).then_inc(rstdA_done, 1)

                def normalise_k(n, j):
                    pool.wait_ge(rs_done, START + 2 * n + j + 1)
                    e = qk[:, 2 * j:2 * j + 2, D:].rearrange("p t (n d) -> p t n d", d=HD)
                    tt(e, e, per_head(rs, j)[:, :, NH:, :], ALU.mult).then_inc(k_done, 1)

                def normalise_q(n, j):
                    pool.wait_ge(rs_done, START + 2 * n + j + 1)
                    e = qk[:, 2 * j:2 * j + 2, 0:D].rearrange("p t (n d) -> p t n d", d=HD)
                    q = slot(q_ring, n)[:, 2 * j:2 * j + 2, :].rearrange("p t (n d) -> p t n d", d=HD)
                    tt(q, e, per_head(rs, j)[:, :, 0:NH, :], ALU.mult).then_inc(q_done, 1)

                def add_q(m, j):
                    if j == 0:
                        pool.wait_ge(q_in, 16 * m + 16)
                    pool.wait_ge(num_done, START + 4 * m + 2 * j + 2)
                    part = y1[:, 2 * j:2 * j + 2, :]
                    tt(part, part, q_now[:, 2 * j:2 * j + 2, :], ALU.add).then_inc(y_done, 1)

                def power_h2(m):
                    pool.wait_ge(varB_done, START + m + 1)
                    tt(smB[:, 1, :], smB[:, 0, :], mhalf[:, 0, :], ALU.pow).then_inc(rstdB_done, 1)

                def residual(m):
                    pool.wait_ge(h2_done, START + 2 * m + 2)
                    if not (isinstance(m, int) and m == 0):
                        pool.wait_ge(stored, 32 * m)
                    tt(res[:], h2, b2_bc[:].unsqueeze(1).to_broadcast([P, T, D]), ALU.add).then_inc(res_done, 1)

                def sums(m, c):
                    pool.wait_ge(sq_done, START + NC * m + c + 1)
                    if c == 1:
                        pool.wait_ge(st_done, START + 2 * m)
                        tt(s12[:, 0, :], g[:, 0, :], g[:, 1, :], ALU.add).then_inc(s1_done, 1)
                        tt(s12[:, 1, :], sq[:, 0, :], sq[:, 1, :], ALU.add).then_inc(sum_done, 1)
                    else:
                        pool.wait_ge(s1_done, START + 7 * m + c - 1)
                        tt(s12[:, 0, :], s12[:, 0, :], g[:, c % GB, :], ALU.add).then_inc(s1_done, 1)
                        pool.wait_ge(sum_done, START + 7 * m + c - 1)
                        tt(s12[:, 1, :], s12[:, 1, :], sq[:, c % SB, :], ALU.add).then_inc(sum_done, 1)

                def power_g(m):
                    pool.wait_ge(varF_done, START + m + 1)
                    tt(smF[:, 5, :], smF[:, 4, :], mhalf[:, 0, :], ALU.pow).then_inc(rstdF_done, 1)

                def first_A(a):
                    weigh(a, 0)
                    weigh(a, 1)
                    powers_z(a)

                def only_A(n):
                    a = n + 1
                    normalise_q(n, 0)
                    normalise_k(n, 0)
                    normalise_k(n, 1)
                    weigh(a, 0)
                    weigh(a, 1)
                    powers_z(a)
                    normalise_q(n, 1)

                def A_and_B(m):
                    n, a, b = m + LAG, m + LAG + 1, m + 1
                    add_q(b, 0)
                    add_q(b, 1)
                    power_h2(b)
                    normalise_q(n, 0)
                    normalise_k(n, 0)
                    normalise_k(n, 1)
                    weigh(a, 0)
                    weigh(a, 1)
                    normalise_q(n, 1)
                    powers_z(a)
                    residual(b)

                def all_stages(m):
                    n, a, b = m + LAG, m + LAG + 1, m + 1
                    for i in range(1, 4):
                        sums(m, i)
                    add_q(b, 0)
                    add_q(b, 1)
                    for i in range(4, 7):
                        sums(m, i)
                    power_h2(b)
                    sums(m, 7)
                    normalise_q(n, 0)
                    normalise_k(n, 0)
                    normalise_k(n, 1)
                    power_g(m)
                    weigh(a, 0)
                    weigh(a, 1)
                    normalise_q(n, 1)
                    powers_z(a)
                    residual(b)

                def B_and_F(m):
                    b = m + 1
                    sums(m, 1)
                    sums(m, 2)
                    add_q(b, 0)
                    add_q(b, 1)
                    for i in range(3, 7):
                        sums(m, i)
                    power_h2(b)
                    sums(m, 7)
                    power_g(m)
                    residual(b)

                def only_F(m):
                    for i in range(1, 8):
                        sums(m, i)
                    power_g(m)

                group_loops(pool, first_A, only_A, lambda k: None, A_and_B, all_stages, B_and_F, only_F)

            @block.vector
            def _(dve):
                tt, ts, stt = nc.vector.tensor_tensor, nc.vector.tensor_scalar, nc.vector.scalar_tensor_tensor

                def convolve(n, part):
                    i = n % NG
                    for k in (range(0, 5), range(5, 9))[part]:
                        dy, dx = divmod(k, 3)
                        first = (i // GI) * XP + (i % GI) * (GR * PW) + dy * PW
                        win = xpad[:, bass.ds(first, GR * PW)].rearrange("p (r w) -> p r w", w=PW)[:, :, dx:dx + W]
                        acc = conv[:].rearrange("p (r w) -> p r w", w=W)
                        if k == 0:
                            dve.wait_ge(proj_done, START + 2 * n)
                            ts(acc, win, conv_k[:, 0:1], conv_c[:], ALU.mult, ALU.add).then_inc(conv_step, 1)
                        else:
                            dve.wait_ge(conv_step, START + 9 * n + k)
                            stt(acc, win, conv_k[:, k:k + 1], acc, ALU.mult, ALU.add).then_inc(conv_step, 1)

                def stats_z(n):
                    for t in range(T):
                        if t % 2 == 0:
                            dve.wait_ge(z_done, START + 2 * n + t // 2 + 1)
                        ins = nc.vector.bn_stats(stA[:, t, :], z[:, t, :])
                    ins.then_inc(normA_step, 1)
                    dve.wait_ge(ssq_done, START + n + 1)
                    dve.wait_ge(normA_step, START + 2 * n + 1)
                    ts(smA[:, 0, :], ssq[:], 1.0 / D, TOK_EPS, ALU.mult, ALU.add)
                    for t in range(T):
                        ins = nc.vector.bn_aggr(mvA[:, t, :], stA[:, t, :])
                    ins.then_inc(normA_step, 1)
                    dve.wait_ge(normA_step, START + 2 * n + 2)
                    stt(smA[:, 1, :], smA[:, 0, :], LN_EPS, mvA[:, :, 1], ALU.mult, ALU.add).then_inc(varA_done, 1)

                def norm_z(n):
                    dve.wait_ge(rstdA_done, START + n + 1)
                    for t in range(T):
                        ins = ts(y[:, t, :], z[:, t, :], mvA[:, t, 0:1], smA[:, 3, t:t + 1], ALU.subtract, ALU.mult)
                    ins.then_inc(xn_done, 1)

                def scale_h(n):
                    hs = slot(h_ring, n)
                    for t in range(T):
                        ins = stt(hs[:, t, :], z[:, t, :], smA[:, 2, t:t + 1], bo_bc[:], ALU.mult, ALU.add)
                    ins.then_inc(h_done, 1)

                def low_x(n, h):
                    dve.wait_ge(xhi_done, START + 2 * n + h + 1)
                    stt(xT_lo[:, h, :], bank_of["transpose_x %d" % h][:], XS, xT_hi[:, h, :], ALU.mult,
                        ALU.subtract).then_inc(xlo_done, 1)

                def shift(n, t):
                    ps = bank_of["project_qk %d" % t][:].rearrange("p (n d) -> p n d", d=HD)
                    dve.wait_ge(qkp_done, START + 4 * n + t + 1)
                    nc.vector.tensor_reduce(mx[:, t, :], ps, AX.X, ALU.max).then_inc(max_done, 1)
                    if t == 0:
                        dve.wait_ge(q_done, START + 2 * n)
                        dve.wait_ge(ctx_done, START + n)
                    dve.wait_ge(max_done, START + 4 * n + t + 1)
                    tt(qk[:, t, :].rearrange("p (n d) -> p n d", d=HD), ps,
                       mx[:, t, :].unsqueeze(2).to_broadcast([P, 2 * NH, HD]), ALU.subtract).then_inc(shift_done, 1)

                def head_sums(n, j):
                    dve.wait_ge(exp_done, START + 2 * n + j + 1)
                    nc.vector.tensor_reduce(sm[:, 2 * j:2 * j + 2, :], qk[:, 2 * j:2 * j + 2, :].rearrange("p t (n d) -> p t n d", d=HD),
                                            AX.X, ALU.add).then_inc(hsum_done, 1)
                    dve.wait_ge(hsum_done, START + 2 * n + j + 1)
                    nc.vector.reciprocal(rs[:, 2 * j:2 * j + 2, :], sm[:, 2 * j:2 * j + 2, :]).then_inc(rs_done, 1)

                def gather_kv(n):
                    dve.wait_ge(ctx_done, START + n + 1)
                    dve.wait_ge(acc_done, START + n)
                    acc = kv_acc[:].rearrange("p h c -> p (h c)")
                    tt(acc, acc, bank_of["keys_values"][:, 0:KH * VC], ALU.add).then_inc(acc_done, 1)

                def close_image(k):
                    dve.wait_ge(acc_done, START + GI * k + GI)
                    dve.wait_ge(qc_done, START + 4 * GI * k)
                    for h in range(KH):
                        tt(kv[:, h, 0:P], kv_acc[:, h, 0:P], mask[:], ALU.mult)
                        ins = ts(kv[:, h, P:CC], mask[:].rearrange("p (n d) -> p n d", d=HD)[:, :, 0], kv_acc[:, h, P:VC], None,
                                 ALU.mult)
                    ins.then_inc(kv_ready, 1)
                    dve.wait_ge(kv_ready, START + k + 1)
                    nc.vector.memset(kv_acc[:], 0.0)

                def divide(m, t):
                    ps = bank_of["attend %d" % t][:, 0:KH * CC].rearrange("p (h c) -> p h c", h=KH)
                    dve.wait_ge(qc_done, START + 4 * m + t + 1)
                    nc.vector.reciprocal(rden[:, t, :, :], ps[:, :, P:CC]).then_inc(rden_done, 1)
                    if t == 0:
                        dve.wait_ge(x2T_done, START + 2 * m)
                    dve.wait_ge(rden_done, START + 4 * m + t + 1)
                    tt(y1[:, t, :].rearrange("p (h n d) -> p h n d", h=KH, d=HD), ps[:, :, 0:P].rearrange("p h (n d) -> p h n d", d=HD),
                       rden[:, t, :, :].unsqueeze(3).to_broadcast([P, KH, HH, HD]), ALU.mult).then_inc(num_done, 1)

                def add_h(m, j):
                    if j == 0:
                        dve.wait_ge(res_done, START + m)
                    dve.wait_ge(wo_done, START + 2 * m + j + 1)
                    tt(h2[:, 2 * j:2 * j + 2, :], bank_of["output_product %d" % j][:].rearrange("p (t d) -> p t d", t=2),
                       slot(h_ring, m)[:, 2 * j:2 * j + 2, :], ALU.add).then_inc(h2_done, 1)

                def stats_h2(m):
                    for t in range(T):
                        if t % 2 == 0:
                            dve.wait_ge(h2_done, START + 2 * m + t // 2 + 1)
                        ins = nc.vector.bn_stats(stB[:, t, :], h2[:, t, :])
                    ins.then_inc(normB_step, 1)
                    dve.wait_ge(normB_step, START + 2 * m + 1)
                    nc.vector.memset(carrier[:], 0.0)
                    for t in range(T):
                        ins = nc.vector.bn_aggr(mvB[:, t, :], stB[:, t, :])
                    ins.then_inc(normB_step, 1)
                    dve.wait_ge(normB_step, START + 2 * m + 2)
                    ts(smB[:, 0, :], mvB[:, :, 1], 1.0 + LN_EPS, LN_EPS * LN_EPS, ALU.mult, ALU.add).then_inc(varB_done, 1)

                def norm_h2(m):
                    dve.wait_ge(yT_done, START + 2 * m + 2)
                    dve.wait_ge(rstdB_done, START + m + 1)
                    for t in range(T):
                        ins = ts(x2[:, t, :], h2[:, t, :], mvB[:, t, 0:1], smB[:, 1, t:t + 1], ALU.subtract, ALU.mult)
                    ins.then_inc(x2_done, 1)

                def low_x2(m, h):
                    dve.wait_ge(x2hi_done, START + 2 * m + h + 1)
                    stt(x2T_lo[:, h, :], bank_of["transpose_x2 %d" % h][:], g1c[:, h:h + 1], x2T_hi[:, h, :], ALU.mult,
                        ALU.subtract).then_inc(x2lo_done, 1)

                def low_g(m, c):
                    dve.wait_ge(ghi_done, START + NC * m + c + 1)
                    stt(g_lo[:, c % HB, :], g[:, c % GB, :], g2c[:, c:c + 1], g_hi[:, c % HB, :], ALU.mult,
                        ALU.subtract).then_inc(glo_done, 1)

                def stats_g(m):
                    for i in range(2):
                        dve.wait_ge(st_done, START + 2 * m + i + 1)
                        nc.vector.tensor_reduce(smF[:, i, :], bank_of["transpose_sums %d" % i][:].rearrange("p (t n) -> p t n", t=T),
                                                AX.X, ALU.add).then_inc(ssum_done, 1)
                    dve.wait_ge(ssum_done, START + 2 * m + 2)
                    ts(smF[:, 2, :], smF[:, 0, :], -1.0 / HID, None, ALU.mult)
                    ts(smF[:, 3, :], smF[:, 1, :], 1.0 / HID, LN_EPS, ALU.mult, ALU.add).then_inc(normF_step, 1)
                    dve.wait_ge(normF_step, START + 2 * m + 1)
                    tt(smF[:, 4, :], smF[:, 2, :], smF[:, 2, :], ALU.mult).then_inc(normF_step, 1)
                    dve.wait_ge(normF_step, START + 2 * m + 2)
                    tt(smF[:, 4, :], smF[:, 3, :], smF[:, 4, :], ALU.subtract).then_inc(varF_done, 1)

                def scale_out(m):
                    dve.wait_ge(rstdF_done, START + m + 1)
                    ts(smF[:, 6, :], smF[:, 5, :], a2c[:], None, ALU.mult)
                    tt(smF[:, 7, :], smF[:, 5, :], smF[:, 2, :], ALU.mult).then_inc(coef_done, 1)
                    dve.wait_ge(coef_done, START + m + 1)
                    dve.wait_ge(f2_done, START + NC * m + NC)
                    dve.wait_ge(res_done, START + m + 1)
                    for t in range(T):
                        stt(res[:, t, :], psO[t // 2][:, (t % 2) * D:(t % 2 + 1) * D], smF[:, 6, t:t + 1], res[:, t, :],
                            ALU.mult, ALU.add).then_inc(u_done, 1)

                def center_out(m):
                    for t in range(T):
                        dve.wait_ge(u_done, START + T * m + t + 1)
                        stt(res[:, t, :], g2w_bc[:], smF[:, 7, t:t + 1], res[:, t, :], ALU.mult, ALU.add).then_inc(fin_done, 1)

                def first_A(a):
                    convolve(a, 0)
                    convolve(a, 1)
                    stats_z(a)
                    norm_z(a)

                def only_A(n):
                    a = n + 1
                    scale_h(n)
                    low_x(n, 0)
                    low_x(n, 1)
                    convolve(a, 0)
                    shift(n, 0)
                    shift(n, 1)
                    convolve(a, 1)
                    shift(n, 2)
                    head_sums(n, 0)
                    shift(n, 3)
                    head_sums(n, 1)
                    stats_z(a)
                    gather_kv(n)
                    norm_z(a)

                def A_and_B(m):
                    n, a, b = m + LAG, m + LAG + 1, m + 1
                    low_x(n, 0)
                    low_x(n, 1)
                    convolve(a, 0)
                    shift(n, 0)
                    convolve(a, 1)
                    shift(n, 1)
                    for i in range(0, 4):
                        divide(b, i)
                    shift(n, 2)
                    head_sums(n, 0)
                    scale_h(n)
                    shift(n, 3)
                    add_h(b, 0)
                    add_h(b, 1)
                    stats_h2(b)
                    head_sums(n, 1)
                    norm_h2(b)
                    low_x2(b, 0)
                    low_x2(b, 1)
                    stats_z(a)
                    gather_kv(n)
                    norm_z(a)

                def all_stages(m):
                    n, a, b = m + LAG, m + LAG + 1, m + 1
                    low_g(m, 0)
                    low_g(m, 1)
                    low_x(n, 0)
                    low_x(n, 1)
                    convolve(a, 0)
                    shift(n, 0)
                    low_g(m, 2)
                    convolve(a, 1)
                    shift(n, 1)
                    for i in range(0, 4):
                        divide(b, i)
                    shift(n, 2)
                    low_g(m, 3)
                    head_sums(n, 0)
                    scale_h(n)
                    shift(n, 3)
                    low_g(m, 4)
                    add_h(b, 0)
                    add_h(b, 1)
                    stats_h2(b)
                    head_sums(n, 1)
                    norm_h2(b)
                    for i in range(5, 8):
                        low_g(m, i)
                    stats_g(m)
                    low_x2(b, 0)
                    low_x2(b, 1)
                    scale_out(m)
                    center_out(m)
                    stats_z(a)
                    gather_kv(n)
                    norm_z(a)

                def B_and_F(m):
                    b = m + 1
                    for i in range(0, 3):
                        low_g(m, i)
                    divide(b, 0)
                    divide(b, 1)
                    low_g(m, 3)
                    divide(b, 2)
                    divide(b, 3)
                    low_g(m, 4)
                    add_h(b, 0)
                    low_g(m, 5)
                    add_h(b, 1)
                    low_g(m, 6)
                    stats_h2(b)
                    norm_h2(b)
                    low_g(m, 7)
                    stats_g(m)
                    scale_out(m)
                    center_out(m)
                    low_x2(b, 0)
                    low_x2(b, 1)

                def only_F(m):
                    for i in range(0, 8):
                        low_g(m, i)
                    stats_g(m)
                    scale_out(m)
                    center_out(m)

                group_loops(dve, first_A, only_A, close_image, A_and_B, all_stages, B_and_F, only_F)


_INS = ["x", "L0_tok_conv_w", "L0_tok_conv_b", "L0_tok_proj_w", "L0_tok_proj_b", "L0_tok_norm_w",
        "L0_attn_Wq", "L0_attn_bq", "L0_attn_Wk", "L0_attn_bk", "L0_attn_Wv", "L0_attn_bv", "L0_attn_Wo", "L0_attn_bo",
        "L0_ffn_ln1_g", "L0_ffn_ln1_b", "L0_ffn_w1", "L0_ffn_b1", "L0_ffn_ln2_g", "L0_ffn_ln2_b", "L0_ffn_w2", "L0_ffn_b2"]


def kernel(**inputs):
    import numpy as np
    import concourse.bacc as bacc
    from concourse.bass_utils import run_bass_kernel_spmd

    nc = bacc.Bacc("TRN2", target_bir_lowering=False, num_devices=1)
    arrays, args = {}, []
    for name in _INS:
        a = np.ascontiguousarray(inputs[name])
        arrays[f"in_{name}"] = a
        args.append(nc.dram_tensor(f"in_{name}", a.shape, mybir.dt.from_np(a.dtype), kind="ExternalInput").ap())
    B, H, W, _ = inputs["x"].shape
    D = inputs["L0_attn_Wq"].shape[0]
    out = nc.dram_tensor("out", (B, H * W, D), F32, kind="ExternalOutput").ap()
    vit_block(nc, *args, out)
    return run_bass_kernel_spmd(nc, [arrays], core_ids=[0]).results[0]["out"]
```

```python
from contextlib import ExitStack

import concourse.bass as bass
from concourse import mybir

F32 = mybir.dt.float32
F16 = mybir.dt.float16
ALU = mybir.AluOpType
ACT = mybir.ActivationFunctionType
AX = mybir.AxisListType

P = 128
XS = 16.0
WS = 64.0
QS = XS * WS
BROW = 32.0
START = 8
RING = 9
TOK_EPS, LN_EPS = 1e-4, 1e-5


def vit_block(nc, x, conv_w, conv_b, proj_w, proj_b, norm_w, Wq, bq, Wk, bk, Wv, bv, Wo, bo,
              ln1_g, ln1_b, w1, b1, ln2_g, ln2_b, w2, b2, out):
    NB, H, W, C = x.shape
    D = Wq.shape[0]
    HID = w1.shape[0]
    NH, HD = 16, D // 16
    KH = D // P
    NC = HID // P
    T = 4
    TOK = T * P
    GI = H * W // TOK
    NG = NB * GI
    HR = H // 2
    GR = HR // GI
    PR, PW = HR + 2, W + 2
    XP = PR * PW
    HH = NH // KH
    VC = P + 1
    CC = P + HH
    JT = H * W // 2 // P
    assert C == 64 and D == 256 and HD == 16 and GI == 8 and GR * W == 2 * P and P % HD == 0

    ctx = ExitStack()
    with ctx:
        def sb(name, shape, dt=F32):
            return ctx.enter_context(nc.sbuf_tensor(name, shape, dt))

        def sem(name):
            return ctx.enter_context(nc.semaphore(name))

        h_ring = sb("h_ring", [P, RING * T * D])
        q_ring = sb("q_ring", [P, RING * T * D])
        xpad = sb("xpad", [P, NB * XP])
        w1T = [sb(f"w1T{h}", [P, HID], F16) for h in range(KH)]
        w2T = sb("w2T", [P, NC, D], F16)
        wqkv_hi = sb("wqkv_hi", [P, KH, 3 * D], F16)
        wqkv_lo = sb("wqkv_lo", [P, KH, 3 * D], F16)
        wo = sb("wo", [P, KH, D])
        proj = sb("proj", [P, 2, D])
        ones_rows = sb("ones_rows", [P, P], F16)
        qk_bias = sb("qk_bias", [P, 2 * D], F16)
        proj_bias = sb("proj_bias", [P, D], F16)
        norm_bc = sb("norm_bc", [P, D])
        bo_bc = sb("bo_bc", [P, D])
        b2_bc = sb("b2_bc", [P, D])
        g2w_bc = sb("g2w_bc", [P, D])
        ident = sb("ident", [P, P])
        mask = sb("mask", [P, P])
        ones = sb("ones", [P, P])
        cols = sb("cols", [P, 32])
        conv_k = sb("conv_k", [P, 9])
        conv_c = sb("conv_c", [P, 1])
        tern = sb("tern", [P, 2, 4])
        absum = sb("absum", [P, 2])
        gelu_scale = sb("gelu_scale", [P, 1])
        b1c = sb("b1c", [P, NC])
        carrier = sb("carrier", [P, 1])
        g1c = sb("g1c", [P, KH])
        g2c = sb("g2c", [P, NC])
        a2c = sb("a2c", [P, 1])
        mhalf = sb("mhalf", [P, 2, T])
        kv_acc = sb("kv_acc", [P, KH, VC])
        kv = sb("kv", [P, KH, CC])
        conv = sb("conv", [P, 2 * P])
        y = sb("y", [P, T, D])
        z = sb("z", [P, T, D])
        ssq = sb("ssq", [P, T])
        stA = sb("stA", [P, T, 6])
        mvA = sb("mvA", [P, T, 2])
        smA = sb("smA", [P, 6, T])
        xT_hi = sb("xT_hi", [P, KH, TOK], F16)
        xT_lo = sb("xT_lo", [P, KH, TOK], F16)
        qk = sb("qk", [P, T, 2 * D])
        mx = sb("mx", [P, T, 2 * NH])
        sm = sb("sm", [P, T, 2 * NH])
        rs = sb("rs", [P, T, 2 * NH])
        v = sb("v", [P, T, KH, VC])
        GB, SB, HB = 3, 2, 3
        late = sb("late", [P, 5 * T * D + (GB + SB + 2) * TOK])
        late_used = [0]

        def take(size):
            late_used[0] += size
            return late[:, late_used[0] - size:late_used[0]]

        qT = take(T * D).rearrange("p (h t) -> p h t", h=KH)
        y1, h2, q_now, res = (take(T * D).rearrange("p (t d) -> p t d", t=T) for _ in range(4))
        g, sq, s12 = (take(k * TOK).rearrange("p (k n) -> p k n", n=TOK) for k in (GB, SB, 2))
        yT, x2 = qT, y1
        rden = sb("rden", [P, T, KH, HH])
        stB = sb("stB", [P, T, 6])
        mvB = sb("mvB", [P, T, 2])
        smB = sb("smB", [P, 4, T])
        x2T_hi = sb("x2T_hi", [P, KH, TOK], F16)
        x2T_lo = sb("x2T_lo", [P, KH, TOK], F16)
        g_hi = sb("g_hi", [P, HB, TOK], F16)
        g_lo = sb("g_lo", [P, HB, TOK], F16)
        smF = sb("smF", [P, 6, T])

        psA = [ctx.enter_context(nc.psum_tensor(f"psA{i}", [P, 512], F32)) for i in range(2)]
        psB = [ctx.enter_context(nc.psum_tensor(f"psB{i}", [P, 512], F32)) for i in range(2)]
        psF = [ctx.enter_context(nc.psum_tensor(f"psF{i}", [P, 512], F32)) for i in range(2)]
        psO = [ctx.enter_context(nc.psum_tensor(f"psO{i}", [P, 512], F32)) for i in range(2)]

        stage_sems = []

        def stage_sem(name):
            stage_sems.append(sem(name))
            return stage_sems[-1]

        conv_step, proj_done, gelu_done, ssq_done = stage_sem("conv_step"), stage_sem("proj_done"), stage_sem("gelu_done"), stage_sem("ssq_done")
        z_done, normA_step, h_done = stage_sem("z_done"), stage_sem("normA_step"), stage_sem("h_done")
        shiftA_done, shiftB_done = stage_sem("shiftA_done"), stage_sem("shiftB_done")
        varA_done, rstdA_done, xn_done, xT_done = stage_sem("varA_done"), stage_sem("rstdA_done"), stage_sem("xn_done"), stage_sem("xT_done")
        xhi_done, xlo_done, qkp_done, vp_done = stage_sem("xhi_done"), stage_sem("xlo_done"), stage_sem("qkp_done"), stage_sem("vp_done")
        max_done, shift_done, exp_done, v_out = stage_sem("max_done"), stage_sem("shift_done"), stage_sem("exp_done"), stage_sem("v_out")
        hsum_done, rs_done, q_done, k_done = stage_sem("hsum_done"), stage_sem("rs_done"), stage_sem("q_done"), stage_sem("k_done")
        ctx_done, acc_done, kv_ready = stage_sem("ctx_done"), stage_sem("acc_done"), stage_sem("kv_ready")
        qT_done, qT_out, qc_done, rden_done = stage_sem("qT_done"), stage_sem("qT_out"), stage_sem("qc_done"), stage_sem("rden_done")
        num_done, y_done, yT_done, yT_out = stage_sem("num_done"), stage_sem("y_done"), stage_sem("yT_done"), stage_sem("yT_out")
        wo_done, h2_done, normB_step = stage_sem("wo_done"), stage_sem("h2_done"), stage_sem("normB_step")
        varB_done, rstdB_done, x2_done = stage_sem("varB_done"), stage_sem("rstdB_done"), stage_sem("x2_done")
        x2T_done, x2hi_done, x2lo_done, res_done = stage_sem("x2T_done"), stage_sem("x2hi_done"), stage_sem("x2lo_done"), stage_sem("res_done")
        f1_done, g_done, ghi_done, glo_done = stage_sem("f1_done"), stage_sem("g_done"), stage_sem("ghi_done"), stage_sem("glo_done")
        sq_done, s1_done, sum_done, f2_done = stage_sem("sq_done"), stage_sem("s1_done"), stage_sem("sum_done"), stage_sem("f2_done")
        st_done, ssum_done, normF_step, varF_done = stage_sem("st_done"), stage_sem("ssum_done"), stage_sem("normF_step"), stage_sem("varF_done")
        stored = stage_sem("stored")
        rstdF_done, coef_done, u_done, fin_done = stage_sem("rstdF_done"), stage_sem("coef_done"), stage_sem("u_done"), stage_sem("fin_done")

        XB = JT * 2 * C
        assert XB == 2 * T * D and 2 * NB <= RING - 1
        xin = [h_ring[:, k * T * D:(k + 2) * T * D].rearrange("p (j h c) -> p j h c", j=JT, h=2)
               for k in [1] + [RING - 2 * b for b in range(1, NB)]]
        wn = qk[:].rearrange("p t n -> p (t n)")[:, 0:KH * 3 * D].rearrange("p (h n) -> p h n", h=KH)
        y_flat, z_flat = y[:].rearrange("p t n -> p (t n)"), z[:].rearrange("p t n -> p (t n)")
        pn = y_flat[:, 0:2 * P].rearrange("p (b n) -> p b n", b=2)
        bv_spread = y_flat[:, 2 * P:(2 + KH) * P].rearrange("p (h n) -> p h n", h=KH)
        pack, brow = z_flat[:, 0:P], z_flat[:, P:P + 3 * D]
        WN = NC * D
        w1n, w2n, t1T, t2T = (late[:, j * WN:(j + 1) * WN] for j in range(4))
        over = (t1T, t2T)
        vec_spread = w1n.rearrange("p (r n) -> p r n", n=P)
        t1T = t1T.rearrange("p (h n) -> p h n", h=KH)
        t2T = t2T.rearrange("p (c n) -> p c n", c=NC)
        assert 4 * WN <= late_used[0]

        x_in = [sem(f"x_in{b}") for b in range(NB)]
        w12_in, wqkv_in, small_in, rows_in = sem("w12_in"), sem("wqkv_in"), sem("small_in"), sem("rows_in")
        cleared, const_step, consts, pad_clear = sem("cleared"), sem("const_step"), sem("consts"), sem("pad_clear")
        abs_done, tot_done, compared, ternary = sem("abs_done"), sem("tot_done"), sem("compared"), sem("ternary")
        setup_step, prep_step, hi_done = sem("setup_step"), sem("prep_step"), sem("hi_done")
        tr_done, tr_out, x_tr, x_out = sem("tr_done"), sem("tr_out"), sem("x_tr"), sem("x_out")
        col_done, pj_done, bv_ready, bo_done = sem("col_done"), sem("pj_done"), sem("bv_ready"), sem("bo_done")
        spread, sums_done, folded = sem("spread"), sem("sums_done"), sem("folded")

        GCOL, BCOL, B1COL, G2COL, B2COL, BVCOL = 0, KH, 2 * KH, 2 * KH + NC, 2 * KH + 2 * NC, 2 * KH + 3 * NC

        def transpose_image(pe, b, ps):
            pe.wait_ge(x_in[b], 32)
            for u in range(JT // 4):
                n = b * (JT // 4) + u
                if n >= 2:
                    pe.wait_ge(x_out, n - 1)
                for j in range(4):
                    ins = nc.tensor.transpose(ps[n % 2][:, j * P:(j + 1) * P], xin[b][:, 4 * u + j, :, :], ident[:])
                ins.then_inc(x_tr, 1)

        def take_image(act, b, ps):
            inside = xpad[:, b * XP:(b + 1) * XP].rearrange("p (r w) -> p r w", w=PW)[:, 1:HR + 1, 1:PW - 1]
            inside = inside.rearrange("p r (q j) -> p j r q", j=JT)
            for u in range(JT // 4):
                n = b * (JT // 4) + u
                act.wait_ge(x_tr, n + 1)
                src = ps[n % 2][:].rearrange("p (j r q) -> p j r q", j=4, q=P // HR)
                for j in range(4):
                    ins = nc.scalar.activation(inside[:, 4 * u + j], src[:, j], ACT.Copy)
                ins.then_inc(x_out, 1)

        def share_rows(dve, b):
            dve.wait_ge(x_out, (b + 1) * (JT // 4))
            img = xpad[:, b * XP:(b + 1) * XP].rearrange("p (r w) -> p r w", w=PW)
            nc.vector.tensor_copy(img[0:C, HR + 1, :], img[C:2 * C, 1, :])
            nc.vector.tensor_copy(img[C:2 * C, 0, :], img[0:C, HR, :])

        with nc.Block() as block:

            @block.sync
            def _(sp):
                for b in range(NB):
                    if b == 1:
                        sp.wait_ge(cleared, 1)
                        for row, src in ((GCOL, ln1_g), (BCOL, ln1_b), (B1COL, b1), (G2COL, ln2_g), (B2COL, ln2_b), (BVCOL, bv)):
                            n = src.shape[0] // P
                            sp.dma_start(pack[row:row + n, :], src.rearrange("(r n) -> r n", n=P)).then_inc(rows_in, 16)
                        for part in (0, 32):
                            for col, src in ((0, bq), (D, bk), (2 * D, proj_b)):
                                sp.dma_start(brow[part:part + 1, col:col + D], src.rearrange("(a n) -> a n", a=1)).then_inc(rows_in, 16)
                        for s in stage_sems:
                            sp.sem_inc(s, START)
                        sp.wait_ge(wqkv_in, 64)
                        sp.wait_ge(small_in, 16 * 9)
                        sp.wait_ge(rows_in, 16 * 12)
                    for half in range(2):
                        rows = x[b, half * HR:(half + 1) * HR, :, :].rearrange("r w c -> (r w) c")
                        sp.dma_start(xin[b][:, :, half, :], rows.rearrange("(p j) c -> p j c", j=JT)).then_inc(x_in[b], 16)

            @block.scalar
            def _(act):
                for i, src in enumerate((Wq, Wk, Wv)):
                    act.dma_start(wn[:, :, i * D:(i + 1) * D], src.rearrange("(h p) n -> p h n", p=P)).then_inc(wqkv_in, 16)
                act.dma_start(wo[:], Wo.rearrange("(h p) n -> p h n", p=P)).then_inc(wqkv_in, 16)
                for rep in range(2):
                    act.dma_start(pn[:, :, rep * C:(rep + 1) * C], proj_w.rearrange("(b p) c -> p b c", p=P)).then_inc(small_in, 16)
                    act.dma_start(conv_k[rep * C:(rep + 1) * C, :], conv_w.rearrange("c o a b -> c (o a b)")).then_inc(small_in, 16)
                    act.dma_start(conv_c[rep * C:(rep + 1) * C, :], conv_b.rearrange("(c o) -> c o", o=1)).then_inc(small_in, 16)
                for dst, src in ((norm_bc, norm_w), (bo_bc, bo), (b2_bc, b2)):
                    act.dma_start(dst[:], src.rearrange("(a n) -> a n", a=1).to_broadcast([P, D])).then_inc(small_in, 16)
                act.wait_ge(pad_clear, 1)
                take_image(act, 0, psB)

            @block.gpsimd
            def _(pool):
                nc.gpsimd.memset(z[:], 0.0).then_inc(cleared, 1)
                nc.gpsimd.memset(ones[:], 1.0).then_inc(const_step, 1)
                nc.gpsimd.memset(ident[:], 0.0).then_inc(const_step, 1)
                nc.gpsimd.memset(mask[:], 1.0).then_inc(const_step, 1)
                pool.wait_ge(const_step, 3)
                nc.gpsimd.affine_select(out=ident[:], in_=ident[:], compare_op=ALU.not_equal, fill=1.0, base=0,
                                        pattern=[[-1, P]], channel_multiplier=1).then_inc(const_step, 1)
                m = mask[:].rearrange("p (b i) -> p b i", i=16)
                nc.gpsimd.affine_select(out=m, in_=m, compare_op=ALU.is_ge, fill=0.0, base=0,
                                        pattern=[[-16, 8], [0, 16]], channel_multiplier=1).then_inc(const_step, 1)
                pool.wait_ge(const_step, 5)
                nc.gpsimd.affine_select(out=m, in_=m, compare_op=ALU.is_ge, fill=0.0, base=15,
                                        pattern=[[16, 8], [0, 16]], channel_multiplier=-1).then_inc(const_step, 1)
                nc.gpsimd.memset(mhalf[:], -0.5).then_inc(const_step, 1)
                nc.gpsimd.memset(kv_acc[:], 0.0).then_inc(const_step, 1)
                nc.gpsimd.memset(v[:], 1.0).then_inc(const_step, 1)
                nc.gpsimd.memset(ones_rows[:], 0.0).then_inc(const_step, 1)
                nc.gpsimd.memset(qk_bias[:], 0.0).then_inc(const_step, 1)
                nc.gpsimd.memset(proj_bias[:], 0.0).then_inc(const_step, 1)
                nc.gpsimd.memset(proj[:], 0.0).then_inc(const_step, 1)
                pool.wait_ge(const_step, 13)
                nc.gpsimd.memset(smA[:], 0.0).then_inc(consts, 1)

            @block.vector
            def _(dve):
                steps = [0]

                def step(ins):
                    steps[0] += 1
                    ins.then_inc(setup_step, 1)
                    dve.wait_ge(setup_step, steps[0])

                nc.vector.memset(xpad[:], 0.0).then_inc(pad_clear, 1)
                dve.wait_ge(col_done, 1)
                step(nc.vector.tensor_copy(cols[:, 0:32], psA[1][:, 0:32]))
                nc.vector.tensor_scalar(g1c[:], cols[:, GCOL:GCOL + KH], XS, None, ALU.mult)
                nc.vector.tensor_scalar(g2c[:], cols[:, G2COL:G2COL + NC], XS, None, ALU.mult)
                dve.wait_ge(consts, 1)
                for part in (0, 32):
                    nc.vector.memset(ones_rows[part:part + 1, :], BROW)
                for h in range(KH):
                    ins = nc.vector.tensor_scalar(bv_spread[:, h, :], ones[:], cols[:, BVCOL + h:BVCOL + h + 1], None, ALU.mult)
                ins.then_inc(bv_ready, 1)
                dve.wait_ge(wqkv_in, 64)
                nc.vector.tensor_scalar(wqkv_hi[:], wn, WS, None, ALU.mult).then_inc(hi_done, 1)
                dve.wait_ge(hi_done, 1)
                nc.vector.scalar_tensor_tensor(wqkv_lo[:], wn, WS, wqkv_hi[:], ALU.mult, ALU.subtract)
                dve.wait_ge(rows_in, 16 * 12)
                for dst, src in ((qk_bias, brow[:, 0:2 * D]), (proj_bias, brow[:, 2 * D:3 * D])):
                    nc.vector.tensor_scalar(dst[0:1, :], src[0:1, :], BROW, None, ALU.mult)
                    step(nc.vector.tensor_scalar(dst[32:33, :], src[32:33, :], BROW, None, ALU.mult))
                    step(nc.vector.scalar_tensor_tensor(dst[32:33, :], src[32:33, :], BROW, dst[32:33, :], ALU.mult, ALU.subtract))
                dve.wait_ge(small_in, 16 * 9)
                dve.wait_ge(pj_done, 1)
                for half in range(2):
                    rows = slice(half * C, (half + 1) * C)
                    nc.vector.tensor_scalar(proj[rows, half, :], psO[0][rows, 0:D], QS, None, ALU.mult)
                dve.wait_ge(bo_done, 1)
                nc.vector.tensor_tensor(bo_bc[:], psO[1][:, 0:D], bo_bc[:], ALU.add)
                share_rows(dve, 0)

            @block.tensor
            def _(pe):
                pe.wait_ge(consts, 1)
                transpose_image(pe, 0, psB)
                pe.wait_ge(rows_in, 16 * 12)
                nc.tensor.transpose(psA[1][:, 0:P], pack, ident[:]).then_inc(col_done, 1)
                pe.wait_ge(small_in, 16 * 9)
                for b in range(2):
                    ins = nc.tensor.transpose(psO[0][:, b * P:(b + 1) * P], pn[:, b, :], ident[:])
                ins.then_inc(pj_done, 1)
                pe.wait_ge(bv_ready, 1)
                pe.wait_ge(wqkv_in, 64)
                for h in range(KH):
                    ins = nc.tensor.matmul(psO[1][:, 0:D], bv_spread[:, h, :], wo[:, h, :], start=(h == 0), stop=(h == KH - 1))
                ins.then_inc(bo_done, 1)

        q_in = sem("q_in")

        LAG = GI + 1

        banks = {
            "transpose_q 0": psB[0],
            "transpose_q 1": psB[1],
            "up 0": psF[0],
            "up 1": psF[1],
            "transpose_x 0": psA[0],
            "attend 0": psB[0],
            "up 2": psF[0],
            "attend 1": psB[1],
            "transpose_x 1": psA[1],
            "up 3": psF[1],
            "attend 2": psB[0],
            "attend 3": psB[1],
            "up 4": psF[0],
            "project_qk 0": psA[0],
            "up 5": psF[1],
            "project_qk 1": psA[1],
            "project_qk 2": psA[0],
            "transpose_y 0": psB[0],
            "up 6": psF[0],
            "transpose_y 1": psB[1],
            "up 7": psF[1],
            "project_qk 3": psA[1],
            "output_product 0": psB[0],
            "output_product 1": psB[1],
            "project_v 0": psA[0],
            "project_v 1": psA[1],
            "project 0": psA[0],
            "project 1": psA[1],
            "token_sums": psF[0],
            "transpose_x2 0": psB[0],
            "transpose_x2 1": psB[1],
            "keys_values": psA[0],
        }
        first_image_banks = dict(banks, **{"project 0": psB[0], "project 1": psB[1]})
        bank_of = {}
        turns = {
            "transpose_q 0": (x2lo_done, 2, -1),
            "transpose_q 1": (x2lo_done, 2, 0),
            "up 0": (ssum_done, 1, 0),
            "up 1": (g_done, 8, 0),
            "transpose_x 0": (acc_done, 1, 0),
            "attend 0": (qT_out, 2, 1),
            "up 2": (g_done, 8, 1),
            "attend 1": (qT_out, 2, 2),
            "transpose_x 1": (ssq_done, 1, 1),
            "up 3": (g_done, 8, 2),
            "attend 2": (num_done, 4, 1),
            "attend 3": (num_done, 4, 2),
            "up 4": (g_done, 8, 3),
            "project_qk 0": (xlo_done, 2, 1),
            "up 5": (g_done, 8, 4),
            "project_qk 1": (xlo_done, 2, 2),
            "project_qk 2": (shift_done, 4, 1),
            "transpose_y 0": (num_done, 4, 3),
            "up 6": (g_done, 8, 5),
            "transpose_y 1": (num_done, 4, 4),
            "up 7": (g_done, 8, 6),
            "project_qk 3": (shift_done, 4, 2),
            "output_product 0": (yT_out, 2, 1),
            "output_product 1": (yT_out, 2, 2),
            "project_v 0": (shift_done, 4, 3),
            "project_v 1": (shift_done, 4, 4),
            "project 0": (v_out, 2, -1),
            "project 1": (v_out, 2, 0),
            "token_sums": (g_done, 8, 7),
            "transpose_x2 0": (h2_done, 2, 1),
            "transpose_x2 1": (h2_done, 2, 2),
            "keys_values": (ssq_done, 1, 2),
        }
        first_image_turns = {
            "transpose_x 0": (v_out, 2, -1),
            "transpose_x 1": (v_out, 2, 0),
            "project_qk 0": (acc_done, 1, 0),
            "project_qk 1": (xlo_done, 2, 2),
            "project_qk 2": (shift_done, 4, 1),
            "project_qk 3": (shift_done, 4, 2),
            "project_v 0": (shift_done, 4, 3),
            "project_v 1": (shift_done, 4, 4),
            "project 0": (ssq_done, 1, 0),
            "project 1": (ssq_done, 1, 0),
            "keys_values": (xlo_done, 2, 3),
        }

        def slot(ring, n):
            return ring[:, bass.ds((n % RING) * (T * D), T * D)].rearrange("p (t d) -> p t d", t=T)

        def per_head(ap, j):
            return ap[:, 2 * j:2 * j + 2, :].unsqueeze(3).to_broadcast([P, 2, ap.shape[2], HD])

        def before(ring, c):
            return c - ring if c >= ring else max(k for k in range(NC) if k % ring == c % ring) - NC

        def nothing(*_):
            pass

        def group_loops(eng, prepare, first_A, second_A, only_A, last_product, close_image, A_and_B, all_stages, B_and_F, only_F):
            bank_of.update(first_image_banks)
            prepare[0]()
            first_A(0)
            prepare[1]()
            second_A(0)
            for n in range(1, GI):
                prepare[n + 1]()
                only_A(n)
            prepare[GI + 1]()
            last_product(GI - 1)
            close_image(0)
            bank_of.update(banks)
            A_and_B(-1)
            with eng.Fori(0, NB - 1) as k:
                with eng.Fori((k * (2 * GI - 1)) // 2, k * GI + GI - 1) as m:
                    all_stages(m)
                close_image(k + 1)
            with eng.Fori(NG - LAG, NG - 1) as m:
                B_and_F(m)
            only_F(NG - 1)

        with nc.Block() as block:

            @block.sync
            def _(sp):
                sp.dma_start(w1n.rearrange("p (c d) -> p c d", c=NC), w1.rearrange("(c p) d -> p c d", p=P)).then_inc(w12_in, 16)
                sp.dma_start(w2n.rearrange("p (c d) -> p c d", c=KH), w2.rearrange("(c p) d -> p c d", p=P)).then_inc(w12_in, 16)
                rows = out.rearrange("b n d -> (b n) d")

                def stage_q(m):
                    if isinstance(m, int):
                        sp.wait_ge(q_done, START + 2 * m + 2)
                    sp.wait_ge(qT_done, START + 2 * m)
                    sp.wait_ge(y_done, START + 2 * m)
                    sp.dma_start(q_now[:], slot(q_ring, m)).then_inc(q_in, 16)

                def store(m):
                    firsts = [(m // GI) * (H * W) + (m % GI) * (2 * P) + half * (H * W // 2) for half in range(2)]
                    sp.wait_ge(fin_done, START + T * m + T)
                    for half, first in enumerate(firsts):
                        dst = rows[bass.ds(first, 2 * P), :].rearrange("(t p) d -> p t d", p=P)
                        sp.dma_start(dst, res[:, 2 * half:2 * half + 2, :]).then_inc(stored, 16)

                sp.wait_ge(folded, 1)
                stage_q(0)
                stage_q(1)
                with sp.Fori(0, NG - 2) as m:
                    stage_q(m + 2)
                    store(m)
                store(NG - 2)
                store(NG - 1)
                sp.wait_ge(stored, START + 32 * NG)

            @block.tensor
            def _(pe):
                mm, tr = nc.tensor.matmul, nc.tensor.transpose
                turn = {}

                def bank(use, n):
                    released, per_group, count = turn[use]
                    pe.wait_ge(released, START + per_group * n + count)
                    return bank_of[use]

                def project(n, j):
                    if j == 0:
                        pe.wait_ge(conv_step, START + 9 * n + 9)
                    ps = bank(f"project {j}", n)
                    for u in range(2):
                        dst = ps[:, u * D:(u + 1) * D]
                        mm(dst, conv[:, u * P:(u + 1) * P], proj[:, j, :], start=(u == 0), stop=False, skip_group_check=True)
                        ins = mm(dst, ones_rows[:], proj_bias[:], start=False, stop=True, skip_group_check=True)
                    ins.then_inc(proj_done, 1)

                def transpose_x(n, h):
                    if h == 0:
                        pe.wait_ge(xn_done, START + n + 1)
                    ps = bank(f"transpose_x {h}", n)
                    for t in range(T):
                        ins = tr(ps[:, t * P:(t + 1) * P], y[:, t, h * P:(h + 1) * P], ident[:])
                    ins.then_inc(xT_done, 1)

                def split_product(dst, t, cols_, first, last):
                    tok = slice(t * P, (t + 1) * P)
                    parts = [(h, xa, wa) for h in range(KH)
                             for xa, wa in ((xT_hi, wqkv_hi), (xT_hi, wqkv_lo), (xT_lo, wqkv_hi))]
                    for k, (h, xa, wa) in enumerate(parts):
                        ins = mm(dst, xa[:, h, tok], wa[:, h, cols_], start=(first and k == 0),
                                 stop=(last and k == len(parts) - 1), skip_group_check=True)
                    return ins

                def project_qk(n, t):
                    if t == 0:
                        pe.wait_ge(xlo_done, START + 2 * n + 2)
                    ps = bank(f"project_qk {t}", n)
                    split_product(ps[:], t, slice(0, 2 * D), True, False)
                    mm(ps[:], ones_rows[:], qk_bias[:], start=False, stop=True, skip_group_check=True).then_inc(qkp_done, 1)

                def project_v(n, j):
                    ps = bank(f"project_v {j}", n)
                    for u in range(2):
                        ins = split_product(ps[:, u * D:(u + 1) * D], 2 * j + u, slice(2 * D, 3 * D), u == 0, True)
                    ins.then_inc(vp_done, 1)

                def keys_values(n):
                    pe.wait_ge(k_done, START + 2 * n + 2)
                    pe.wait_ge(v_out, START + 2 * n + 2)
                    ps = bank("keys_values", n)
                    for t in range(T):
                        for h in range(KH):
                            ins = mm(ps[:, h * VC:(h + 1) * VC], qk[:, t, D + h * P:D + (h + 1) * P], v[:, t, h, :],
                                     start=(t == 0 and h == 0), stop=(t == T - 1), skip_group_check=True)
                    ins.then_inc(ctx_done, 1)

                def transpose_q(m, h):
                    if h == 0:
                        pe.wait_ge(q_in, 16 * m + 16)
                    ps = bank(f"transpose_q {h}", m)
                    for t in range(T):
                        ins = tr(ps[:, t * P:(t + 1) * P], q_now[:, t, h * P:(h + 1) * P], ident[:])
                    ins.then_inc(qT_done, 1)

                def attend(m, t):
                    if t == 0:
                        pe.wait_ge(qT_out, START + 2 * m + 2)
                        pe.wait_ge(kv_ready, START + m // GI + 1)
                    ps = bank(f"attend {t}", m)
                    for h in range(KH):
                        ins = mm(ps[:, h * CC:(h + 1) * CC], qT[:, h, t * P:(t + 1) * P], kv[:, h, :],
                                 start=(h == 0), stop=True, skip_group_check=True)
                    ins.then_inc(qc_done, 1)

                def transpose_y(m, h):
                    if h == 0:
                        pe.wait_ge(y_done, START + 2 * m + 2)
                    ps = bank(f"transpose_y {h}", m)
                    for t in range(T):
                        ins = tr(ps[:, t * P:(t + 1) * P], y1[:, t, h * P:(h + 1) * P], ident[:])
                    ins.then_inc(yT_done, 1)

                def output_product(m, j):
                    if j == 0:
                        pe.wait_ge(yT_out, START + 2 * m + 2)
                    ps = bank(f"output_product {j}", m)
                    for u in range(2):
                        t = 2 * j + u
                        for h in range(KH):
                            ins = mm(ps[:, u * D:(u + 1) * D], yT[:, h, t * P:(t + 1) * P], wo[:, h, :],
                                     start=(u == 0 and h == 0), stop=(h == KH - 1), skip_group_check=True)
                    ins.then_inc(wo_done, 1)

                def transpose_x2(m, h):
                    if h == 0:
                        pe.wait_ge(x2_done, START + m + 1)
                    ps = bank(f"transpose_x2 {h}", m)
                    for t in range(T):
                        ins = tr(ps[:, t * P:(t + 1) * P], x2[:, t, h * P:(h + 1) * P], ident[:])
                    ins.then_inc(x2T_done, 1)

                def up(m, c):
                    if c == 0:
                        pe.wait_ge(x2lo_done, START + 2 * m + 2)
                    ps = bank(f"up {c}", m)
                    parts = [(h, xa) for h in range(KH) for xa in (x2T_hi, x2T_lo)]
                    for k, (h, xa) in enumerate(parts):
                        ins = mm(ps[:], w1T[h][:, c * P:(c + 1) * P], xa[:, h, :], start=(k == 0), stop=(k == len(parts) - 1))
                    ins.then_inc(f1_done, 1)

                def down(m, c):
                    if c == 0:
                        pe.wait_ge(u_done, START + T * m)
                    pe.wait_ge(glo_done, START + NC * m + c + 1)
                    for t in range(T):
                        for ga in (g_hi, g_lo):
                            ins = mm(psO[t // 2][:, (t % 2) * D:(t % 2 + 1) * D], ga[:, c % HB, t * P:(t + 1) * P], w2T[:, c, :],
                                     start=(c == 0 and t % 2 == 0 and ga is g_hi), stop=(c == NC - 1 and ga is g_lo),
                                     skip_group_check=True)
                    ins.then_inc(f2_done, 1)

                def token_sums(m):
                    pe.wait_ge(s1_done, START + 7 * m + 7)
                    pe.wait_ge(sum_done, START + 7 * m + 7)
                    ps = bank("token_sums", m)
                    for i in range(2):
                        for t in range(T):
                            ins = mm(ps[:, i * T + t:i * T + t + 1], s12[:, i, t * P:(t + 1) * P], ones[:, 0:1], start=True, stop=True)
                    ins.then_inc(st_done, 1)

                def add_abs():
                    pe.wait_ge(abs_done, 2)
                    mm(psO[0][:, 0:2], ones[:], absum[:], start=True, stop=True).then_inc(tot_done, 1)

                def transpose_ternary(weight):
                    pe.wait_ge(ternary, weight + 1)
                    for n in range(weight * 2 * KH, (weight + 1) * 2 * KH):
                        h, part = divmod(n % (2 * KH), 2)
                        if n >= 2:
                            pe.wait_ge(tr_out, n - 1)
                        for c in range(4 * part, 4 * part + 4):
                            src = w1n[:, c * D + h * P:c * D + (h + 1) * P] if weight == 0 else w2n[:, h * HID + c * P:h * HID + (c + 1) * P]
                            ins = tr(psF[n % 2][:, c % 4 * P:(c % 4 + 1) * P], src, ident[:])
                        ins.then_inc(tr_done, 1)

                def vector_through(i):
                    pe.wait_ge(spread, 1)
                    pe.wait_ge(tr_out, 4 * KH)
                    for c in range(NC):
                        ins = mm(psO[i][:, 0:D], vec_spread[:, i * NC + c, :], t2T[:, c, :], start=(c == 0), stop=(c == NC - 1))
                    ins.then_inc(sums_done, 1)

                def bias_through():
                    pe.wait_ge(tr_out, 4 * KH)
                    for c in range(NC):
                        for h in range(KH):
                            ins = mm(psF[0][:, c:c + 1], t1T[:, h, c * P:(c + 1) * P], cols[:, BCOL + h:BCOL + h + 1],
                                     start=(h == 0), stop=(h == KH - 1))
                    ins.then_inc(sums_done, 1)

                images = [lambda b=b: transpose_image(pe, b, psF) for b in range(1, NB)]
                ternary_steps = [lambda w=w: transpose_ternary(w) for w in range(2)]
                vectors = [lambda i=i: vector_through(i) for i in range(2)]
                prepare = (*images, add_abs, nothing, *ternary_steps, *vectors, bias_through)

                def first_A(a):
                    turn.update(first_image_turns)
                    project(a, 0)
                    project(a, 1)

                def second_A(n):
                    a = n + 1
                    transpose_x(n, 0)
                    transpose_x(n, 1)
                    project(a, 0)
                    project(a, 1)
                    for i in range(0, 4):
                        project_qk(n, i)
                    project_v(n, 0)
                    project_v(n, 1)

                def only_A(n):
                    a = n + 1
                    transpose_x(n, 0)
                    transpose_x(n, 1)
                    keys_values(n - 1)
                    project(a, 0)
                    project(a, 1)
                    for i in range(0, 4):
                        project_qk(n, i)
                    project_v(n, 0)
                    project_v(n, 1)

                def last_product(n):
                    turn["keys_values"] = v_out, 2, 2
                    keys_values(n)

                def A_and_B(m):
                    pe.wait_ge(acc_done, START + GI)
                    pe.wait_ge(ssq_done, START + GI + 1)
                    turn.update(turns)
                    n, a, b = m + LAG, m + LAG + 1, m + 1
                    transpose_q(b, 0)
                    transpose_q(b, 1)
                    transpose_x(n, 0)
                    attend(b, 0)
                    attend(b, 1)
                    transpose_x(n, 1)
                    attend(b, 2)
                    attend(b, 3)
                    for i in range(0, 3):
                        project_qk(n, i)
                    transpose_y(b, 0)
                    transpose_y(b, 1)
                    project_qk(n, 3)
                    output_product(b, 0)
                    output_product(b, 1)
                    project_v(n, 0)
                    project_v(n, 1)
                    project(a, 0)
                    project(a, 1)
                    transpose_x2(b, 0)
                    transpose_x2(b, 1)
                    keys_values(n)

                def all_stages(m):
                    n, a, b = m + LAG, m + LAG + 1, m + 1
                    transpose_q(b, 0)
                    transpose_q(b, 1)
                    up(m, 0)
                    up(m, 1)
                    transpose_x(n, 0)
                    attend(b, 0)
                    up(m, 2)
                    attend(b, 1)
                    transpose_x(n, 1)
                    up(m, 3)
                    attend(b, 2)
                    attend(b, 3)
                    up(m, 4)
                    project_qk(n, 0)
                    down(m, 0)
                    up(m, 5)
                    project_qk(n, 1)
                    down(m, 1)
                    project_qk(n, 2)
                    transpose_y(b, 0)
                    up(m, 6)
                    transpose_y(b, 1)
                    up(m, 7)
                    project_qk(n, 3)
                    down(m, 2)
                    output_product(b, 0)
                    output_product(b, 1)
                    down(m, 3)
                    project_v(n, 0)
                    project_v(n, 1)
                    project(a, 0)
                    project(a, 1)
                    token_sums(m)
                    for i in range(4, 7):
                        down(m, i)
                    transpose_x2(b, 0)
                    transpose_x2(b, 1)
                    keys_values(n)
                    down(m, 7)

                def B_and_F(m):
                    b = m + 1
                    transpose_q(b, 0)
                    transpose_q(b, 1)
                    up(m, 0)
                    up(m, 1)
                    attend(b, 0)
                    attend(b, 1)
                    up(m, 2)
                    up(m, 3)
                    attend(b, 2)
                    attend(b, 3)
                    up(m, 4)
                    down(m, 0)
                    up(m, 5)
                    down(m, 1)
                    transpose_y(b, 0)
                    transpose_y(b, 1)
                    up(m, 6)
                    output_product(b, 0)
                    output_product(b, 1)
                    up(m, 7)
                    for i in range(2, 6):
                        down(m, i)
                    token_sums(m)
                    transpose_x2(b, 0)
                    transpose_x2(b, 1)
                    down(m, 6)
                    down(m, 7)

                def only_F(m):
                    for i in range(0, 5):
                        up(m, i)
                    down(m, 0)
                    down(m, 1)
                    up(m, 5)
                    down(m, 2)
                    up(m, 6)
                    down(m, 3)
                    up(m, 7)
                    down(m, 4)
                    token_sums(m)
                    for i in range(5, 8):
                        down(m, i)

                group_loops(pe, prepare, first_A, second_A, only_A, last_product, nothing, A_and_B, all_stages, B_and_F, only_F)

            @block.scalar
            def _(act):
                fn = nc.scalar.activation

                def gelu_y(n, j):
                    if j == 0:
                        act.wait_ge(xT_done, START + 2 * n)
                    act.wait_ge(proj_done, START + 2 * n + j + 1)
                    fn(y[:, 2 * j:2 * j + 2, :], bank_of["project %d" % j][:].rearrange("p (t d) -> p t d", t=2), ACT.Gelu,
                       scale=1.0 / QS).then_inc(gelu_done, 1)

                def square_y(n):
                    act.wait_ge(gelu_done, START + 2 * n + 2)
                    act.wait_ge(xn_done, START + n)
                    for t in range(T):
                        ins = fn(bank_of["project %d" % (t // 2)][:, (t % 2) * D:(t % 2 + 1) * D], y[:, t, :], ACT.Square,
                                 accum_out=ssq[:, t:t + 1])
                    ins.then_inc(ssq_done, 1)

                def norm_z(n):
                    act.wait_ge(shiftA_done, START + n + 1)
                    for t in range(T):
                        ins = fn(y[:, t, :], z[:, t, :], ACT.Identity, scale=smA[:, 3, t:t + 1], bias=smA[:, 5, t:t + 1])
                    ins.then_inc(xn_done, 1)

                def high_x(n, h):
                    if h == 0:
                        act.wait_ge(vp_done, START + 2 * n)
                        act.wait_ge(qkp_done, START + 4 * n)
                    act.wait_ge(xT_done, START + 2 * n + h + 1)
                    fn(xT_hi[:, h, :], bank_of["transpose_x %d" % h][:], ACT.Copy, scale=XS).then_inc(xhi_done, 1)

                def take_v(n, j):
                    if j == 0:
                        act.wait_ge(ctx_done, START + n)
                    act.wait_ge(vp_done, START + 2 * n + j + 1)
                    fn(v[:, 2 * j:2 * j + 2, :, 0:P], bank_of["project_v %d" % j][:].rearrange("p (t h d) -> p t h d", t=2, h=KH),
                       ACT.Copy, scale=1.0 / QS).then_inc(v_out, 1)

                def exps(n, j):
                    act.wait_ge(shift_done, START + 4 * n + 2 * j + 2)
                    fn(qk[:, 2 * j:2 * j + 2, :], qk[:, 2 * j:2 * j + 2, :], ACT.Exp, scale=1.0 / QS).then_inc(exp_done, 1)

                def take_qT(m, h):
                    if h == 0:
                        act.wait_ge(wo_done, START + 2 * m)
                    act.wait_ge(qT_done, START + 2 * m + h + 1)
                    fn(qT[:, h, :], bank_of["transpose_q %d" % h][:], ACT.Copy).then_inc(qT_out, 1)

                def take_yT(m, h):
                    if h == 0:
                        act.wait_ge(qc_done, START + 4 * m + 4)
                    act.wait_ge(yT_done, START + 2 * m + h + 1)
                    fn(yT[:, h, :], bank_of["transpose_y %d" % h][:], ACT.Copy).then_inc(yT_out, 1)

                def norm_h2(m):
                    act.wait_ge(yT_done, START + 2 * m + 2)
                    act.wait_ge(shiftB_done, START + m + 1)
                    for t in range(T):
                        ins = fn(x2[:, t, :], h2[:, t, :], ACT.Identity, scale=smB[:, 1, t:t + 1], bias=smB[:, 3, t:t + 1])
                    ins.then_inc(x2_done, 1)

                def high_x2(m, h):
                    if h == 0:
                        act.wait_ge(f1_done, START + NC * m)
                    act.wait_ge(x2T_done, START + 2 * m + h + 1)
                    fn(x2T_hi[:, h, :], bank_of["transpose_x2 %d" % h][:], ACT.Copy, scale=g1c[:, h:h + 1]).then_inc(x2hi_done, 1)

                def gelu_g(m, c):
                    act.wait_ge(f1_done, START + NC * m + c + 1)
                    last = before(GB, c)
                    act.wait_ge(glo_done, START + NC * m + last + 1)
                    act.wait_ge(s1_done, START + 7 * m + (max(last, 1) if last >= 0 else last + 1))
                    fn(g[:, c % GB, :], bank_of["up %d" % c][:], ACT.Gelu, scale=gelu_scale[:], bias=b1c[:, c:c + 1]).then_inc(g_done, 1)

                def high_g(m, c):
                    act.wait_ge(f2_done, START + NC * m + before(HB, c) + 1)
                    act.wait_ge(g_done, START + NC * m + c + 1)
                    fn(g_hi[:, c % HB, :], g[:, c % GB, :], ACT.Copy, scale=g2c[:, c:c + 1]).then_inc(ghi_done, 1)

                def square_g(m, c):
                    last = before(SB, c)
                    act.wait_ge(sum_done, START + 7 * m + (max(last, 1) if last >= 0 else last + 1))
                    act.wait_ge(g_done, START + NC * m + c + 1)
                    fn(sq[:, c % SB, :], g[:, c % GB, :], ACT.Square).then_inc(sq_done, 1)

                def add_magnitudes():
                    act.wait_ge(w12_in, 32)
                    for i, w in enumerate((w1n, w2n)):
                        fn(over[i], w, ACT.Abs, accum_out=absum[:, i:i + 1]).then_inc(abs_done, 1)

                def take_ternary(weight):
                    for n in range(weight * 2 * KH, (weight + 1) * 2 * KH):
                        act.wait_ge(tr_done, n + 1)
                        h, part = divmod(n % (2 * KH), 2)
                        src = psF[n % 2][:]
                        if n < 2 * KH:
                            dst, dst32 = (w[:, part * 512:(part + 1) * 512] for w in (w1T[h], t1T[:, h, :]))
                        else:
                            src = src.rearrange("p (c n) -> p c n", c=4)
                            dst, dst32 = (w[:, 4 * part:4 * part + 4, h * P:(h + 1) * P] for w in (w2T, t2T))
                        fn(dst, src, ACT.Copy)
                        fn(dst32, src, ACT.Copy).then_inc(tr_out, 1)

                images = [lambda b=b: take_image(act, b, psF) for b in range(1, NB)]
                ternary_steps = [lambda w=w: take_ternary(w) for w in range(2)]
                prepare = (*images, add_magnitudes, nothing, *ternary_steps, nothing, nothing, nothing)

                def first_A(a):
                    gelu_y(a, 0)
                    gelu_y(a, 1)
                    square_y(a)
                    norm_z(a)

                def second_A(n):
                    a = n + 1
                    high_x(n, 0)
                    high_x(n, 1)
                    gelu_y(a, 0)
                    gelu_y(a, 1)
                    square_y(a)
                    exps(n, 0)
                    exps(n, 1)
                    norm_z(a)
                    take_v(n, 0)
                    take_v(n, 1)

                def only_A(n):
                    a = n + 1
                    high_x(n, 0)
                    high_x(n, 1)
                    gelu_y(a, 0)
                    gelu_y(a, 1)
                    square_y(a)
                    exps(n, 0)
                    exps(n, 1)
                    norm_z(a)
                    take_v(n, 0)
                    take_v(n, 1)

                def last_product(n):
                    pass

                def A_and_B(m):
                    n, a, b = m + LAG, m + LAG + 1, m + 1
                    take_qT(b, 0)
                    take_qT(b, 1)
                    high_x(n, 0)
                    high_x(n, 1)
                    take_yT(b, 0)
                    take_yT(b, 1)
                    exps(n, 0)
                    exps(n, 1)
                    take_v(n, 0)
                    take_v(n, 1)
                    gelu_y(a, 0)
                    gelu_y(a, 1)
                    square_y(a)
                    norm_h2(b)
                    high_x2(b, 0)
                    high_x2(b, 1)
                    norm_z(a)

                def all_stages(m):
                    n, a, b = m + LAG, m + LAG + 1, m + 1
                    take_qT(b, 0)
                    take_qT(b, 1)
                    gelu_g(m, 0)
                    square_g(m, 0)
                    gelu_g(m, 1)
                    square_g(m, 1)
                    gelu_g(m, 2)
                    high_x(n, 0)
                    high_x(n, 1)
                    high_g(m, 0)
                    square_g(m, 2)
                    gelu_g(m, 3)
                    square_g(m, 3)
                    for i in range(1, 4):
                        high_g(m, i)
                    gelu_g(m, 4)
                    high_g(m, 4)
                    square_g(m, 4)
                    gelu_g(m, 5)
                    take_yT(b, 0)
                    square_g(m, 5)
                    gelu_g(m, 6)
                    take_yT(b, 1)
                    exps(n, 0)
                    high_g(m, 5)
                    square_g(m, 6)
                    exps(n, 1)
                    gelu_g(m, 7)
                    square_g(m, 7)
                    high_g(m, 6)
                    take_v(n, 0)
                    take_v(n, 1)
                    gelu_y(a, 0)
                    gelu_y(a, 1)
                    square_y(a)
                    norm_h2(b)
                    high_g(m, 7)
                    high_x2(b, 0)
                    high_x2(b, 1)
                    norm_z(a)

                def B_and_F(m):
                    b = m + 1
                    take_qT(b, 0)
                    take_qT(b, 1)
                    gelu_g(m, 0)
                    square_g(m, 0)
                    gelu_g(m, 1)
                    square_g(m, 1)
                    high_g(m, 0)
                    gelu_g(m, 2)
                    high_g(m, 1)
                    gelu_g(m, 3)
                    square_g(m, 2)
                    high_g(m, 2)
                    square_g(m, 3)
                    high_g(m, 3)
                    gelu_g(m, 4)
                    take_yT(b, 0)
                    take_yT(b, 1)
                    high_g(m, 4)
                    gelu_g(m, 5)
                    square_g(m, 4)
                    square_g(m, 5)
                    gelu_g(m, 6)
                    square_g(m, 6)
                    gelu_g(m, 7)
                    square_g(m, 7)
                    high_g(m, 5)
                    high_g(m, 6)
                    norm_h2(b)
                    high_g(m, 7)
                    high_x2(b, 0)
                    high_x2(b, 1)

                def only_F(m):
                    gelu_g(m, 0)
                    high_g(m, 0)
                    square_g(m, 0)
                    gelu_g(m, 1)
                    square_g(m, 1)
                    gelu_g(m, 2)
                    high_g(m, 1)
                    high_g(m, 2)
                    square_g(m, 2)
                    gelu_g(m, 3)
                    gelu_g(m, 4)
                    square_g(m, 3)
                    high_g(m, 3)
                    square_g(m, 4)
                    gelu_g(m, 5)
                    square_g(m, 5)
                    high_g(m, 4)
                    gelu_g(m, 6)
                    square_g(m, 6)
                    gelu_g(m, 7)
                    square_g(m, 7)
                    for i in range(5, 8):
                        high_g(m, i)

                group_loops(act, prepare, first_A, second_A, only_A, last_product, nothing, A_and_B, all_stages, B_and_F, only_F)

            @block.gpsimd
            def _(pool):
                tt = nc.gpsimd.tensor_tensor

                def weigh(n, j):
                    if j == 0:
                        pool.wait_ge(xn_done, START + n)
                        pool.wait_ge(h_done, START + n)
                    pool.wait_ge(gelu_done, START + 2 * n + j + 1)
                    tt(z[:, 2 * j:2 * j + 2, :], y[:, 2 * j:2 * j + 2, :], norm_bc[:].unsqueeze(1).to_broadcast([P, 2, D]),
                       ALU.mult).then_inc(z_done, 1)

                def powers_z(n):
                    pool.wait_ge(varA_done, START + n + 1)
                    tt(smA[:, 2:4, :], smA[:, 0:2, :], mhalf[:], ALU.pow).then_inc(rstdA_done, 1)
                    pool.wait_ge(rstdA_done, START + n + 1)
                    tt(smA[:, 5, :], smA[:, 4, :], smA[:, 3, :], ALU.mult).then_inc(shiftA_done, 1)

                def normalise_k(n, j):
                    pool.wait_ge(rs_done, START + 2 * n + j + 1)
                    e = qk[:, 2 * j:2 * j + 2, D:].rearrange("p t (n d) -> p t n d", d=HD)
                    tt(e, e, per_head(rs, j)[:, :, NH:, :], ALU.mult).then_inc(k_done, 1)

                def normalise_q(n, j):
                    pool.wait_ge(rs_done, START + 2 * n + j + 1)
                    e = qk[:, 2 * j:2 * j + 2, 0:D].rearrange("p t (n d) -> p t n d", d=HD)
                    q = slot(q_ring, n)[:, 2 * j:2 * j + 2, :].rearrange("p t (n d) -> p t n d", d=HD)
                    tt(q, e, per_head(rs, j)[:, :, 0:NH, :], ALU.mult).then_inc(q_done, 1)

                def add_q(m, j):
                    if j == 0:
                        pool.wait_ge(q_in, 16 * m + 16)
                    pool.wait_ge(num_done, START + 4 * m + 2 * j + 2)
                    part = y1[:, 2 * j:2 * j + 2, :]
                    tt(part, part, q_now[:, 2 * j:2 * j + 2, :], ALU.add).then_inc(y_done, 1)

                def power_h2(m):
                    pool.wait_ge(varB_done, START + m + 1)
                    tt(smB[:, 1, :], smB[:, 0, :], mhalf[:, 0, :], ALU.pow).then_inc(rstdB_done, 1)
                    pool.wait_ge(rstdB_done, START + m + 1)
                    tt(smB[:, 3, :], smB[:, 2, :], smB[:, 1, :], ALU.mult).then_inc(shiftB_done, 1)

                def residual(m):
                    pool.wait_ge(h2_done, START + 2 * m + 2)
                    pool.wait_ge(stored, START + 32 * m)
                    tt(res[:], h2, b2_bc[:].unsqueeze(1).to_broadcast([P, T, D]), ALU.add).then_inc(res_done, 1)

                def add_gelu(m, c):
                    pool.wait_ge(g_done, START + NC * m + c + 1)
                    if c == 1:
                        pool.wait_ge(st_done, START + m)
                        tt(s12[:, 0, :], g[:, 0, :], g[:, 1, :], ALU.add).then_inc(s1_done, 1)
                    else:
                        pool.wait_ge(s1_done, START + 7 * m + c - 1)
                        tt(s12[:, 0, :], s12[:, 0, :], g[:, c % GB, :], ALU.add).then_inc(s1_done, 1)

                def add_square(m, c):
                    pool.wait_ge(sq_done, START + NC * m + c + 1)
                    if c == 1:
                        pool.wait_ge(st_done, START + m)
                        tt(s12[:, 1, :], sq[:, 0, :], sq[:, 1, :], ALU.add).then_inc(sum_done, 1)
                    else:
                        pool.wait_ge(sum_done, START + 7 * m + c - 1)
                        tt(s12[:, 1, :], s12[:, 1, :], sq[:, c % SB, :], ALU.add).then_inc(sum_done, 1)

                def sums(m, c):
                    add_gelu(m, c)
                    add_square(m, c)

                def power_g(m):
                    pool.wait_ge(varF_done, START + m + 1)
                    tt(smF[:, 3, :], smF[:, 2, :], mhalf[:, 0, :], ALU.pow).then_inc(rstdF_done, 1)

                def make_ternary():
                    for i, w in enumerate((w1n, w2n)):
                        pool.wait_ge(compared, i + 1)
                        tt(w, over[i], w, ALU.subtract).then_inc(ternary, 1)

                prepare = (*[nothing] * NB, make_ternary, nothing, nothing, nothing, nothing, nothing)

                def first_A(a):
                    weigh(a, 0)
                    weigh(a, 1)
                    powers_z(a)

                def second_A(n):
                    a = n + 1
                    weigh(a, 0)
                    weigh(a, 1)
                    powers_z(a)
                    normalise_k(n, 0)
                    normalise_k(n, 1)
                    normalise_q(n, 0)
                    normalise_q(n, 1)

                def only_A(n):
                    a = n + 1
                    weigh(a, 0)
                    weigh(a, 1)
                    powers_z(a)
                    normalise_k(n, 0)
                    normalise_k(n, 1)
                    normalise_q(n, 0)
                    normalise_q(n, 1)

                def last_product(n):
                    pass

                def A_and_B(m):
                    n, a, b = m + LAG, m + LAG + 1, m + 1
                    add_q(b, 0)
                    add_q(b, 1)
                    power_h2(b)
                    weigh(a, 0)
                    weigh(a, 1)
                    normalise_k(n, 0)
                    normalise_k(n, 1)
                    powers_z(a)
                    normalise_q(n, 0)
                    normalise_q(n, 1)

                def all_stages(m):
                    n, a, b = m + LAG, m + LAG + 1, m + 1
                    sums(m, 1)
                    add_q(b, 0)
                    sums(m, 2)
                    add_q(b, 1)
                    sums(m, 3)
                    residual(m)
                    for i in range(4, 8):
                        sums(m, i)
                    power_h2(b)
                    weigh(a, 0)
                    weigh(a, 1)
                    normalise_k(n, 0)
                    normalise_k(n, 1)
                    powers_z(a)
                    power_g(m)
                    normalise_q(n, 0)
                    normalise_q(n, 1)

                def B_and_F(m):
                    b = m + 1
                    add_square(m, 1)
                    add_q(b, 0)
                    add_q(b, 1)
                    add_square(m, 2)
                    add_square(m, 3)
                    residual(m)
                    for i in range(4, 8):
                        add_square(m, i)
                    power_h2(b)
                    power_g(m)

                def only_F(m):
                    residual(m)
                    for i in range(1, 8):
                        add_square(m, i)
                    power_g(m)

                group_loops(pool, prepare, first_A, second_A, only_A, last_product, nothing, A_and_B, all_stages, B_and_F, only_F)

            @block.vector
            def _(dve):
                tt, ts, stt = nc.vector.tensor_tensor, nc.vector.tensor_scalar, nc.vector.scalar_tensor_tensor

                def convolve(n, k):
                    i = n % NG
                    dy, dx = divmod(k, 3)
                    first = (i // GI) * XP + (i % GI) * (GR * PW) + dy * PW
                    win = xpad[:, bass.ds(first, GR * PW)].rearrange("p (r w) -> p r w", w=PW)[:, :, dx:dx + W]
                    acc = conv[:].rearrange("p (r w) -> p r w", w=W)
                    if k == 0:
                        dve.wait_ge(proj_done, START + 2 * n)
                        ts(acc, win, conv_k[:, 0:1], conv_c[:], ALU.mult, ALU.add).then_inc(conv_step, 1)
                    else:
                        dve.wait_ge(conv_step, START + 9 * n + k)
                        stt(acc, win, conv_k[:, k:k + 1], acc, ALU.mult, ALU.add).then_inc(conv_step, 1)

                def stats_z(n):
                    for t in range(T):
                        if t % 2 == 0:
                            dve.wait_ge(z_done, START + 2 * n + t // 2 + 1)
                        ins = nc.vector.bn_stats(stA[:, t, :], z[:, t, :])
                    ins.then_inc(normA_step, 1)
                    dve.wait_ge(ssq_done, START + n + 1)
                    dve.wait_ge(normA_step, START + 2 * n + 1)
                    ts(smA[:, 0, :], ssq[:], 1.0 / D, TOK_EPS, ALU.mult, ALU.add)
                    for t in range(T):
                        ins = nc.vector.bn_aggr(mvA[:, t, :], stA[:, t, :])
                    ins.then_inc(normA_step, 1)
                    dve.wait_ge(normA_step, START + 2 * n + 2)
                    ts(smA[:, 4, :], mvA[:, :, 0], -1.0, None, ALU.mult)
                    stt(smA[:, 1, :], smA[:, 0, :], LN_EPS, mvA[:, :, 1], ALU.mult, ALU.add).then_inc(varA_done, 1)

                def scale_h(n):
                    hs = slot(h_ring, n)
                    for t in range(T):
                        ins = stt(hs[:, t, :], z[:, t, :], smA[:, 2, t:t + 1], bo_bc[:], ALU.mult, ALU.add)
                    ins.then_inc(h_done, 1)

                def low_x(n, h):
                    dve.wait_ge(xhi_done, START + 2 * n + h + 1)
                    stt(xT_lo[:, h, :], bank_of["transpose_x %d" % h][:], XS, xT_hi[:, h, :], ALU.mult,
                        ALU.subtract).then_inc(xlo_done, 1)

                def shift(n, t):
                    ps = bank_of["project_qk %d" % t][:].rearrange("p (n d) -> p n d", d=HD)
                    dve.wait_ge(qkp_done, START + 4 * n + t + 1)
                    nc.vector.tensor_reduce(mx[:, t, :], ps, AX.X, ALU.max).then_inc(max_done, 1)
                    if t == 0:
                        dve.wait_ge(q_done, START + 2 * n)
                        dve.wait_ge(ctx_done, START + n)
                    dve.wait_ge(max_done, START + 4 * n + t + 1)
                    tt(qk[:, t, :].rearrange("p (n d) -> p n d", d=HD), ps,
                       mx[:, t, :].unsqueeze(2).to_broadcast([P, 2 * NH, HD]), ALU.subtract).then_inc(shift_done, 1)

                def head_sums(n, j):
                    dve.wait_ge(exp_done, START + 2 * n + j + 1)
                    nc.vector.tensor_reduce(sm[:, 2 * j:2 * j + 2, :], qk[:, 2 * j:2 * j + 2, :].rearrange("p t (n d) -> p t n d", d=HD),
                                            AX.X, ALU.add).then_inc(hsum_done, 1)
                    dve.wait_ge(hsum_done, START + 2 * n + j + 1)
                    nc.vector.reciprocal(rs[:, 2 * j:2 * j + 2, :], sm[:, 2 * j:2 * j + 2, :]).then_inc(rs_done, 1)

                def gather_kv(n):
                    dve.wait_ge(ctx_done, START + n + 1)
                    dve.wait_ge(acc_done, START + n)
                    acc = kv_acc[:].rearrange("p h c -> p (h c)")
                    tt(acc, acc, bank_of["keys_values"][:, 0:KH * VC], ALU.add).then_inc(acc_done, 1)

                def close_image(k):
                    dve.wait_ge(acc_done, START + GI * k + GI)
                    dve.wait_ge(qc_done, START + 4 * GI * k)
                    for h in range(KH):
                        tt(kv[:, h, 0:P], kv_acc[:, h, 0:P], mask[:], ALU.mult)
                        ins = ts(kv[:, h, P:CC], mask[:].rearrange("p (n d) -> p n d", d=HD)[:, :, 0], kv_acc[:, h, P:VC], None,
                                 ALU.mult)
                    ins.then_inc(kv_ready, 1)
                    dve.wait_ge(kv_ready, START + k + 1)
                    nc.vector.memset(kv_acc[:], 0.0)

                def divide(m, t):
                    ps = bank_of["attend %d" % t][:, 0:KH * CC].rearrange("p (h c) -> p h c", h=KH)
                    dve.wait_ge(qc_done, START + 4 * m + t + 1)
                    nc.vector.reciprocal(rden[:, t, :, :], ps[:, :, P:CC]).then_inc(rden_done, 1)
                    if t == 0:
                        dve.wait_ge(x2T_done, START + 2 * m)
                    dve.wait_ge(rden_done, START + 4 * m + t + 1)
                    tt(y1[:, t, :].rearrange("p (h n d) -> p h n d", h=KH, d=HD), ps[:, :, 0:P].rearrange("p h (n d) -> p h n d", d=HD),
                       rden[:, t, :, :].unsqueeze(3).to_broadcast([P, KH, HH, HD]), ALU.mult).then_inc(num_done, 1)

                def add_h(m, j):
                    if j == 0:
                        dve.wait_ge(res_done, START + m)
                    dve.wait_ge(wo_done, START + 2 * m + j + 1)
                    tt(h2[:, 2 * j:2 * j + 2, :], bank_of["output_product %d" % j][:].rearrange("p (t d) -> p t d", t=2),
                       slot(h_ring, m)[:, 2 * j:2 * j + 2, :], ALU.add).then_inc(h2_done, 1)

                def stats_h2(m):
                    for t in range(T):
                        if t % 2 == 0:
                            dve.wait_ge(h2_done, START + 2 * m + t // 2 + 1)
                        ins = nc.vector.bn_stats(stB[:, t, :], h2[:, t, :])
                    ins.then_inc(normB_step, 1)
                    dve.wait_ge(normB_step, START + 2 * m + 1)
                    nc.vector.memset(carrier[:], 0.0)
                    for t in range(T):
                        ins = nc.vector.bn_aggr(mvB[:, t, :], stB[:, t, :])
                    ins.then_inc(normB_step, 1)
                    dve.wait_ge(normB_step, START + 2 * m + 2)
                    ts(smB[:, 2, :], mvB[:, :, 0], -1.0, None, ALU.mult)
                    ts(smB[:, 0, :], mvB[:, :, 1], 1.0 + LN_EPS, LN_EPS * LN_EPS, ALU.mult, ALU.add).then_inc(varB_done, 1)

                def low_x2(m, h):
                    dve.wait_ge(x2hi_done, START + 2 * m + h + 1)
                    stt(x2T_lo[:, h, :], bank_of["transpose_x2 %d" % h][:], g1c[:, h:h + 1], x2T_hi[:, h, :], ALU.mult,
                        ALU.subtract).then_inc(x2lo_done, 1)

                def low_g(m, c):
                    dve.wait_ge(ghi_done, START + NC * m + c + 1)
                    stt(g_lo[:, c % HB, :], g[:, c % GB, :], g2c[:, c:c + 1], g_hi[:, c % HB, :], ALU.mult,
                        ALU.subtract).then_inc(glo_done, 1)

                def add_gelu(m, c):
                    dve.wait_ge(g_done, START + NC * m + c + 1)
                    if c == 1:
                        dve.wait_ge(st_done, START + m)
                        tt(s12[:, 0, :], g[:, 0, :], g[:, 1, :], ALU.add).then_inc(s1_done, 1)
                    else:
                        dve.wait_ge(s1_done, START + 7 * m + c - 1)
                        tt(s12[:, 0, :], s12[:, 0, :], g[:, c % GB, :], ALU.add).then_inc(s1_done, 1)

                def stats_g(m):
                    ps = bank_of["token_sums"]
                    dve.wait_ge(st_done, START + m + 1)
                    ts(smF[:, 0, :], ps[:, 0:T], -1.0 / HID, None, ALU.mult)
                    ts(smF[:, 1, :], ps[:, T:2 * T], 1.0 / HID, LN_EPS, ALU.mult, ALU.add).then_inc(ssum_done, 1)
                    dve.wait_ge(ssum_done, START + m + 1)
                    tt(smF[:, 2, :], smF[:, 0, :], smF[:, 0, :], ALU.mult).then_inc(normF_step, 1)
                    dve.wait_ge(normF_step, START + m + 1)
                    tt(smF[:, 2, :], smF[:, 1, :], smF[:, 2, :], ALU.subtract).then_inc(varF_done, 1)

                def scale_out(m):
                    dve.wait_ge(rstdF_done, START + m + 1)
                    ts(smF[:, 4, :], smF[:, 3, :], a2c[:], None, ALU.mult)
                    tt(smF[:, 5, :], smF[:, 3, :], smF[:, 0, :], ALU.mult).then_inc(coef_done, 1)
                    dve.wait_ge(coef_done, START + m + 1)
                    dve.wait_ge(f2_done, START + NC * m + NC)
                    dve.wait_ge(res_done, START + m + 1)
                    for t in range(T):
                        stt(res[:, t, :], psO[t // 2][:, (t % 2) * D:(t % 2 + 1) * D], smF[:, 4, t:t + 1], res[:, t, :],
                            ALU.mult, ALU.add).then_inc(u_done, 1)

                def center_out(m):
                    for t in range(T):
                        dve.wait_ge(u_done, START + T * m + t + 1)
                        stt(res[:, t, :], g2w_bc[:], smF[:, 5, t:t + 1], res[:, t, :], ALU.mult, ALU.add).then_inc(fin_done, 1)

                steps = [0]

                def step(ins):
                    steps[0] += 1
                    ins.then_inc(prep_step, 1)
                    dve.wait_ge(prep_step, steps[0])

                def compare():
                    dve.wait_ge(tot_done, 1)
                    step(ts(tern[:, :, 0], psO[0][:, 0:2], 1.0 / (D * HID), 1e-5, ALU.mult, ALU.max))
                    step(nc.vector.reciprocal(tern[:, :, 1], tern[:, :, 0]))
                    step(nc.vector.reciprocal(tern[:, :, 2], tern[:, :, 1]))
                    ts(gelu_scale[:], tern[:, 0, 2:3], 1.0 / XS, None, ALU.mult)
                    ts(a2c[:], tern[:, 1, 2:3], 1.0 / XS, None, ALU.mult)
                    for i, w in enumerate((w1n, w2n)):
                        ts(over[i], w, tern[:, i, 1:2], 0.5, ALU.mult, ALU.is_gt)
                        ts(w, w, tern[:, i, 1:2], -0.5, ALU.mult, ALU.is_lt).then_inc(compared, 1)

                def spread_vectors():
                    dve.wait_ge(tr_done, 2 * KH)
                    for i in range(2 * NC):
                        ins = ts(vec_spread[:, i, :], ones[:], cols[:, G2COL + i:G2COL + i + 1], None, ALU.mult)
                    ins.then_inc(spread, 1)

                def fold_vectors():
                    dve.wait_ge(sums_done, 3)
                    ts(g2w_bc[:], psO[0][:, 0:D], tern[:, 1, 2:3], None, ALU.mult)
                    stt(b2_bc[:], psO[1][:, 0:D], tern[:, 1, 2:3], b2_bc[:], ALU.mult, ALU.add)
                    stt(b1c[:], psF[0][:, 0:NC], tern[:, 0, 2:3], cols[:, B1COL:B1COL + NC], ALU.mult, ALU.add).then_inc(folded, 1)

                def share_all_rows():
                    for b in range(1, NB):
                        share_rows(dve, b)

                prepare = (*[nothing] * (NB - 1), share_all_rows, compare, nothing, spread_vectors, nothing, nothing, fold_vectors)

                def first_A(a):
                    for i in range(0, 9):
                        convolve(a, i)
                    stats_z(a)

                def second_A(n):
                    a = n + 1
                    for i in range(0, 4):
                        convolve(a, i)
                    low_x(n, 0)
                    for i in range(4, 9):
                        convolve(a, i)
                    low_x(n, 1)
                    scale_h(n)
                    shift(n, 0)
                    shift(n, 1)
                    stats_z(a)
                    shift(n, 2)
                    shift(n, 3)
                    head_sums(n, 0)
                    head_sums(n, 1)

                def only_A(n):
                    a = n + 1
                    for i in range(0, 4):
                        convolve(a, i)
                    low_x(n, 0)
                    for i in range(4, 9):
                        convolve(a, i)
                    gather_kv(n - 1)
                    low_x(n, 1)
                    scale_h(n)
                    shift(n, 0)
                    shift(n, 1)
                    stats_z(a)
                    shift(n, 2)
                    shift(n, 3)
                    head_sums(n, 0)
                    head_sums(n, 1)

                def last_product(n):
                    gather_kv(n)

                def A_and_B(m):
                    n, a, b = m + LAG, m + LAG + 1, m + 1
                    divide(b, 0)
                    convolve(a, 0)
                    divide(b, 1)
                    convolve(a, 1)
                    low_x(n, 0)
                    low_x(n, 1)
                    divide(b, 2)
                    convolve(a, 2)
                    divide(b, 3)
                    shift(n, 0)
                    convolve(a, 3)
                    convolve(a, 4)
                    shift(n, 1)
                    convolve(a, 5)
                    convolve(a, 6)
                    shift(n, 2)
                    convolve(a, 7)
                    shift(n, 3)
                    convolve(a, 8)
                    scale_h(n)
                    add_h(b, 0)
                    add_h(b, 1)
                    stats_h2(b)
                    head_sums(n, 0)
                    head_sums(n, 1)
                    stats_z(a)
                    low_x2(b, 0)
                    low_x2(b, 1)
                    gather_kv(n)

                def all_stages(m):
                    n, a, b = m + LAG, m + LAG + 1, m + 1
                    divide(b, 0)
                    convolve(a, 0)
                    divide(b, 1)
                    convolve(a, 1)
                    low_x(n, 0)
                    low_x(n, 1)
                    divide(b, 2)
                    low_g(m, 0)
                    convolve(a, 2)
                    divide(b, 3)
                    shift(n, 0)
                    convolve(a, 3)
                    low_g(m, 1)
                    convolve(a, 4)
                    low_g(m, 2)
                    low_g(m, 3)
                    shift(n, 1)
                    convolve(a, 5)
                    convolve(a, 6)
                    low_g(m, 4)
                    shift(n, 2)
                    convolve(a, 7)
                    shift(n, 3)
                    convolve(a, 8)
                    low_g(m, 5)
                    scale_h(n)
                    add_h(b, 0)
                    add_h(b, 1)
                    stats_h2(b)
                    head_sums(n, 0)
                    head_sums(n, 1)
                    low_g(m, 6)
                    stats_z(a)
                    stats_g(m)
                    low_g(m, 7)
                    low_x2(b, 0)
                    low_x2(b, 1)
                    gather_kv(n)
                    scale_out(m)
                    center_out(m)

                def B_and_F(m):
                    b = m + 1
                    divide(b, 0)
                    divide(b, 1)
                    add_gelu(m, 1)
                    low_g(m, 0)
                    divide(b, 2)
                    divide(b, 3)
                    low_g(m, 1)
                    low_g(m, 2)
                    for i in range(2, 5):
                        add_gelu(m, i)
                    low_g(m, 3)
                    low_g(m, 4)
                    add_gelu(m, 5)
                    add_h(b, 0)
                    add_gelu(m, 6)
                    add_h(b, 1)
                    stats_h2(b)
                    low_g(m, 5)
                    add_gelu(m, 7)
                    low_g(m, 6)
                    low_g(m, 7)
                    stats_g(m)
                    low_x2(b, 0)
                    low_x2(b, 1)
                    scale_out(m)
                    center_out(m)

                def only_F(m):
                    add_gelu(m, 1)
                    low_g(m, 0)
                    add_gelu(m, 2)
                    low_g(m, 1)
                    low_g(m, 2)
                    add_gelu(m, 3)
                    low_g(m, 3)
                    add_gelu(m, 4)
                    add_gelu(m, 5)
                    low_g(m, 4)
                    add_gelu(m, 6)
                    add_gelu(m, 7)
                    for i in range(5, 8):
                        low_g(m, i)
                    stats_g(m)
                    scale_out(m)
                    center_out(m)

                group_loops(dve, prepare, first_A, second_A, only_A, last_product, close_image, A_and_B, all_stages, B_and_F, only_F)


_INS = ["x", "L0_tok_conv_w", "L0_tok_conv_b", "L0_tok_proj_w", "L0_tok_proj_b", "L0_tok_norm_w",
        "L0_attn_Wq", "L0_attn_bq", "L0_attn_Wk", "L0_attn_bk", "L0_attn_Wv", "L0_attn_bv", "L0_attn_Wo", "L0_attn_bo",
        "L0_ffn_ln1_g", "L0_ffn_ln1_b", "L0_ffn_w1", "L0_ffn_b1", "L0_ffn_ln2_g", "L0_ffn_ln2_b", "L0_ffn_w2", "L0_ffn_b2"]


def kernel(**inputs):
    import numpy as np
    import concourse.bacc as bacc
    from concourse.bass_utils import run_bass_kernel_spmd

    nc = bacc.Bacc("TRN2", target_bir_lowering=False, num_devices=1)
    arrays, args = {}, []
    for name in _INS:
        a = np.ascontiguousarray(inputs[name])
        arrays[f"in_{name}"] = a
        args.append(nc.dram_tensor(f"in_{name}", a.shape, mybir.dt.from_np(a.dtype), kind="ExternalInput").ap())
    B, H, W, _ = inputs["x"].shape
    D = inputs["L0_attn_Wq"].shape[0]
    out = nc.dram_tensor("out", (B, H * W, D), F32, kind="ExternalOutput").ap()
    vit_block(nc, *args, out)
    return run_bass_kernel_spmd(nc, [arrays], core_ids=[0]).results[0]["out"]
```
